# Optimizing a Trainium2 kernel written in Bass

```python
import numpy as np
import jax
import jax.numpy as jnp

def _softmax(x, axis=-1):
    return jax.nn.softmax(x, axis=axis)

def _gelu(x):
    return jax.nn.gelu(x, approximate=True)

def _silu(x):
    return jax.nn.silu(x)

def _sigmoid(x):
    return jax.nn.sigmoid(x)

def _layernorm(x, axis=-1, eps=1e-05):
    m = jnp.mean(x, axis=axis, keepdims=True)
    v = jnp.var(x, axis=axis, keepdims=True)
    return (x - m) / jnp.sqrt(v + eps)

def _scatter_add(tgt, idx, src, axis=0):
    return tgt.at[idx].add(src)

def _segment_sum(src, seg, n):
    return jax.ops.segment_sum(src, seg, n)
kernel_name = 'mk_adj_resnorm_d4_adj_r2_8b3a6e'

def setup_inputs(seed: int=0):
    np.random.seed(seed)
    _w = jnp.asarray

    def _rec_inputs():
        import jax
        import jax.numpy as jnp
        _gk = jax.random.key(seed)
        x = -0.0002928 + 1 * jax.random.normal(jax.random.fold_in(_gk, 1), (128, 128, 128), jnp.float32)
        _a = jax.random.bernoulli(jax.random.fold_in(_gk, 2), 0.03125, (128, 128, 128))
        _a = jnp.logical_or(_a, jnp.swapaxes(_a, -1, -2))
        _a = jnp.logical_or(_a, jnp.eye(128, dtype=bool))
        _af = _a.astype(jnp.float32)
        _af = _af * jax.random.uniform(jax.random.fold_in(_gk, 3), (128, 128, 128), jnp.float32, 0.05, 1)
        adj = _af
        return (x, adj)
    x, adj = _rec_inputs()

    def _L0_gnn_setup():
        import jax, jax.numpy as jnp
        import numpy as np
        B, N, D, H = (8, 1024, 128, 512)
        RMS_EPS = 1e-06

        def _rmsnorm(h, w, eps=RMS_EPS):
            var = jnp.mean(jnp.square(h), axis=-1, keepdims=True)
            return h * jax.lax.rsqrt(var + eps) * w
        key = jax.random.key(seed)
        ks = jax.random.split(key, 5)
        x = jax.random.normal(ks[0], (B, N, D), dtype=jnp.float32)
        adjacency = jax.random.uniform(ks[1], (B, N, N), dtype=jnp.float32)
        epsilon = jnp.zeros((), dtype=jnp.float32)
        W1 = jax.random.normal(ks[2], (D, H), dtype=jnp.float32) * (1.0 / np.sqrt(D))
        b1 = jnp.zeros((H,), dtype=jnp.float32)
        rms_weight = jnp.ones((H,), dtype=jnp.float32)
        W2 = jax.random.normal(ks[3], (H, D), dtype=jnp.float32) * (1.0 / np.sqrt(H))
        b2 = jnp.zeros((D,), dtype=jnp.float32)
        return {'x': x, 'adjacency': adjacency, 'epsilon': epsilon, 'W1': W1, 'b1': b1, 'rms_weight': rms_weight, 'W2': W2, 'b2': b2}
    _L0_gnn_all = _L0_gnn_setup()
    _L0_gnn_in = {k: v for k, v in _L0_gnn_all.items() if k in ('epsilon', 'W1', 'b1', 'rms_weight', 'W2', 'b2')}
    del _L0_gnn_all

    def _L1_gnn_setup():
        import jax, jax.numpy as jnp
        import numpy as np
        from jax import lax
        DIM = 128
        EPS = 1e-05

        def _bn(h, g, b, m, v):
            scale = g / jnp.sqrt(v + EPS)
            return h * scale[None, :, None] + (b - m * scale)[None, :, None]

        def _conv1d(h, w, pad):
            return lax.conv_general_dilated(h, w, window_strides=(1,), padding=[(pad, pad)], dimension_numbers=('NCH', 'OIH', 'NCH'))
        key = jax.random.key(seed)
        ks = jax.random.split(key, 16)
        bs, n, d = (16, 1024, DIM)
        s = 0.05
        return {'x': jax.random.normal(ks[0], (bs, n, d), jnp.float32), 'mask': jnp.ones((bs, n, n), jnp.float32), 'w_se': jax.random.normal(ks[1], (3, d), jnp.float32) * s, 'b_se': jnp.zeros((3,), jnp.float32), 'conv1_w': jax.random.normal(ks[2], (d, d, 1), jnp.float32) * s, 'bn1_g': jnp.ones((d,), jnp.float32), 'bn1_b': jnp.zeros((d,), jnp.float32), 'bn1_m': jnp.zeros((d,), jnp.float32), 'bn1_v': jnp.ones((d,), jnp.float32), 'conv2_w': jax.random.normal(ks[3], (d, d, 17), jnp.float32) * s, 'bn2_g': jnp.ones((d,), jnp.float32), 'bn2_b': jnp.zeros((d,), jnp.float32), 'bn2_m': jnp.zeros((d,), jnp.float32), 'bn2_v': jnp.ones((d,), jnp.float32), 'w_msg': jax.random.normal(ks[4], (d, d), jnp.float32) * s, 'b_msg': jnp.zeros((d,), jnp.float32), 'w_ih': jax.random.normal(ks[5], (3 * d, 2 * d), jnp.float32) * s, 'b_ih': jnp.zeros((3 * d,), jnp.float32), 'w_hh': jax.random.normal(ks[6], (3 * d, d), jnp.float32) * s, 'b_hh': jnp.zeros((3 * d,), jnp.float32)}
    _L1_gnn_all = _L1_gnn_setup()
    _L1_gnn_in = {k: v for k, v in _L1_gnn_all.items() if k in ('w_se', 'b_se', 'conv1_w', 'bn1_g', 'bn1_b', 'bn1_m', 'bn1_v', 'conv2_w', 'bn2_g', 'bn2_b', 'bn2_m', 'bn2_v', 'w_msg', 'b_msg', 'w_ih', 'b_ih', 'w_hh', 'b_hh')}
    del _L1_gnn_all

    def _L2_gnn_setup():
        import jax, jax.numpy as jnp
        import numpy as np
        K = 4
        EPS = 1e-09
        LEAKY_SLOPE = 0.2
        key = jax.random.key(seed)
        k1, k2, k3, k4, k5 = jax.random.split(key, 5)
        B, N, IN, OUT = (8, 1024, 128, 128)
        h = jax.random.normal(k1, (B, N, IN), dtype=jnp.float32)
        adj = jax.random.uniform(k2, (B, N, N), dtype=jnp.float32)
        W = jax.random.normal(k3, (OUT, IN), dtype=jnp.float32) * 0.05
        conv_w = jax.random.normal(k4, (K,), dtype=jnp.float32)
        conv_b = jax.random.normal(k5, (1,), dtype=jnp.float32)
        return {'h': h, 'adj': adj, 'W': W, 'conv_w': conv_w, 'conv_b': conv_b}
    _L2_gnn_all = _L2_gnn_setup()
    _L2_gnn_in = {k: v for k, v in _L2_gnn_all.items() if k in ('W', 'conv_w', 'conv_b')}
    del _L2_gnn_all

    def _L3_gnn_setup():
        import jax, jax.numpy as jnp
        import numpy as np
        D_IN = 128
        D_HID = 256
        key = jax.random.key(seed)
        k1, k2, k3, k4, k5, k6 = jax.random.split(key, 6)
        x = jax.random.normal(k1, (8, 2048, D_IN), dtype=jnp.float32)
        adj = jax.random.uniform(k2, (8, 2048, 2048), dtype=jnp.float32)
        s1 = 1.0 / np.sqrt(D_IN)
        s2 = 1.0 / np.sqrt(D_HID)
        W1 = jax.random.uniform(k3, (D_IN, D_HID), dtype=jnp.float32, minval=-s1, maxval=s1)
        b1 = jax.random.uniform(k4, (D_HID,), dtype=jnp.float32, minval=-s1, maxval=s1)
        W2 = jax.random.uniform(k5, (D_HID, D_IN), dtype=jnp.float32, minval=-s2, maxval=s2)
        b2 = jax.random.uniform(k6, (D_IN,), dtype=jnp.float32, minval=-s2, maxval=s2)
        eps = jnp.zeros((1,), dtype=jnp.float32)
        return {'x': x, 'adj': adj, 'eps': eps, 'W1': W1, 'b1': b1, 'W2': W2, 'b2': b2}
    _L3_gnn_all = _L3_gnn_setup()
    _L3_gnn_in = {k: v for k, v in _L3_gnn_all.items() if k in ('eps', 'W1', 'b1', 'W2', 'b2')}
    del _L3_gnn_all
    return {'x': x, 'adj': adj, 'L0_gnn_epsilon': _L0_gnn_in['epsilon'], 'L0_gnn_W1': _L0_gnn_in['W1'], 'L0_gnn_b1': _L0_gnn_in['b1'], 'L0_gnn_rms_weight': _L0_gnn_in['rms_weight'], 'L0_gnn_W2': _L0_gnn_in['W2'], 'L0_gnn_b2': _L0_gnn_in['b2'], 'L1_gnn_w_se': _L1_gnn_in['w_se'], 'L1_gnn_b_se': _L1_gnn_in['b_se'], 'L1_gnn_conv1_w': _L1_gnn_in['conv1_w'], 'L1_gnn_bn1_g': _L1_gnn_in['bn1_g'], 'L1_gnn_bn1_b': _L1_gnn_in['bn1_b'], 'L1_gnn_bn1_m': _L1_gnn_in['bn1_m'], 'L1_gnn_bn1_v': _L1_gnn_in['bn1_v'], 'L1_gnn_conv2_w': _L1_gnn_in['conv2_w'], 'L1_gnn_bn2_g': _L1_gnn_in['bn2_g'], 'L1_gnn_bn2_b': _L1_gnn_in['bn2_b'], 'L1_gnn_bn2_m': _L1_gnn_in['bn2_m'], 'L1_gnn_bn2_v': _L1_gnn_in['bn2_v'], 'L1_gnn_w_msg': _L1_gnn_in['w_msg'], 'L1_gnn_b_msg': _L1_gnn_in['b_msg'], 'L1_gnn_w_ih': _L1_gnn_in['w_ih'], 'L1_gnn_b_ih': _L1_gnn_in['b_ih'], 'L1_gnn_w_hh': _L1_gnn_in['w_hh'], 'L1_gnn_b_hh': _L1_gnn_in['b_hh'], 'L2_gnn_W': _L2_gnn_in['W'], 'L2_gnn_conv_w': _L2_gnn_in['conv_w'], 'L2_gnn_conv_b': _L2_gnn_in['conv_b'], 'L3_gnn_eps': _L3_gnn_in['eps'], 'L3_gnn_W1': _L3_gnn_in['W1'], 'L3_gnn_b1': _L3_gnn_in['b1'], 'L3_gnn_W2': _L3_gnn_in['W2'], 'L3_gnn_b2': _L3_gnn_in['b2']}

def reference(x, adj, L0_gnn_epsilon, L0_gnn_W1, L0_gnn_b1, L0_gnn_rms_weight, L0_gnn_W2, L0_gnn_b2, L1_gnn_w_se, L1_gnn_b_se, L1_gnn_conv1_w, L1_gnn_bn1_g, L1_gnn_bn1_b, L1_gnn_bn1_m, L1_gnn_bn1_v, L1_gnn_conv2_w, L1_gnn_bn2_g, L1_gnn_bn2_b, L1_gnn_bn2_m, L1_gnn_bn2_v, L1_gnn_w_msg, L1_gnn_b_msg, L1_gnn_w_ih, L1_gnn_b_ih, L1_gnn_w_hh, L1_gnn_b_hh, L2_gnn_W, L2_gnn_conv_w, L2_gnn_conv_b, L3_gnn_eps, L3_gnn_W1, L3_gnn_b1, L3_gnn_W2, L3_gnn_b2):
    import jax
    import jax.numpy as jnp

    def _L0_gnn_ref(x, adjacency, epsilon, W1, b1, rms_weight, W2, b2):
        import jax, jax.numpy as jnp
        import numpy as np
        B, N, D, H = (8, 1024, 128, 512)
        RMS_EPS = 1e-06

        def _rmsnorm(h, w, eps=RMS_EPS):
            var = jnp.mean(jnp.square(h), axis=-1, keepdims=True)
            return h * jax.lax.rsqrt(var + eps) * w
        neighbor_sum = jnp.einsum('bnm,bmd->bnd', adjacency, x)
        agg = epsilon * x + neighbor_sum
        h = jnp.einsum('bnd,dh->bnh', agg, W1) + b1
        h = jax.nn.silu(_rmsnorm(h, rms_weight))
        out = jnp.einsum('bnh,hd->bnd', h, W2) + b2
        return out

    def _L1_gnn_ref(x, mask, w_se, b_se, conv1_w, bn1_g, bn1_b, bn1_m, bn1_v, conv2_w, bn2_g, bn2_b, bn2_m, bn2_v, w_msg, b_msg, w_ih, b_ih, w_hh, b_hh):
        import jax, jax.numpy as jnp
        import numpy as np
        from jax import lax
        DIM = 128
        EPS = 1e-05

        def _bn(h, g, b, m, v):
            scale = g / jnp.sqrt(v + EPS)
            return h * scale[None, :, None] + (b - m * scale)[None, :, None]

        def _conv1d(h, w, pad):
            return lax.conv_general_dilated(h, w, window_strides=(1,), padding=[(pad, pad)], dimension_numbers=('NCH', 'OIH', 'NCH'))
        d = x.shape[-1]
        xc = jnp.transpose(x, (0, 2, 1))
        h = _bn(_conv1d(xc, conv1_w, 0), bn1_g, bn1_b, bn1_m, bn1_v)
        h = jax.nn.relu(h)
        h = _bn(_conv1d(h, conv2_w, 8), bn2_g, bn2_b, bn2_m, bn2_v)
        x_conv = jnp.transpose(jax.nn.relu(h + xc), (0, 2, 1))
        s = x @ w_se.T + b_se
        sq = jnp.sum(s * s, axis=-1)
        dist = sq[:, :, None] + sq[:, None, :] - 2.0 * jnp.einsum('bnd,bmd->bnm', s, s)
        A = jnp.exp(-dist) * mask
        msg = jax.nn.relu(x @ w_msg.T + b_msg)
        x_nmp = jnp.einsum('bnm,bmd->bnd', A, msg)
        x_in = jnp.concatenate([x_conv, x_nmp], axis=-1)
        gi = x_in @ w_ih.T + b_ih
        gh = x @ w_hh.T + b_hh
        gi_r, gi_z, gi_n = (gi[..., :d], gi[..., d:2 * d], gi[..., 2 * d:])
        gh_r, gh_z, gh_n = (gh[..., :d], gh[..., d:2 * d], gh[..., 2 * d:])
        r = jax.nn.sigmoid(gi_r + gh_r)
        z = jax.nn.sigmoid(gi_z + gh_z)
        nn_ = jnp.tanh(gi_n + r * gh_n)
        return (1.0 - z) * nn_ + z * x

    def _L2_gnn_ref(h, adj, W, conv_w, conv_b):
        import jax, jax.numpy as jnp
        import numpy as np
        K = 4
        EPS = 1e-09
        LEAKY_SLOPE = 0.2
        h_trans = jnp.einsum('bni,oi->bno', h, W)
        row_sum = adj.sum(axis=2, keepdims=True) + EPS
        adj_norm = adj / row_sum
        curr = h_trans
        out = conv_w[0] * curr
        for k in range(1, K):
            curr = jnp.einsum('bnm,bmo->bno', adj_norm, curr)
            out = out + conv_w[k] * curr
        out = out + conv_b[0]
        return jnp.where(out >= 0, out, LEAKY_SLOPE * out)

    def _L3_gnn_ref(x, adj, eps, W1, b1, W2, b2):
        import jax, jax.numpy as jnp
        import numpy as np
        D_IN = 128
        D_HID = 256
        aggregated = jnp.einsum('bnm,bmd->bnd', adj, x)
        h = (1.0 + eps) * x + aggregated
        h = jax.nn.relu(h @ W1 + b1)
        return h @ W2 + b2
    x = _layernorm(x + _L0_gnn_ref(x, adj, L0_gnn_epsilon, L0_gnn_W1, L0_gnn_b1, L0_gnn_rms_weight, L0_gnn_W2, L0_gnn_b2), axis=-1)
    x = _layernorm(x + _L1_gnn_ref(x, adj, L1_gnn_w_se, L1_gnn_b_se, L1_gnn_conv1_w, L1_gnn_bn1_g, L1_gnn_bn1_b, L1_gnn_bn1_m, L1_gnn_bn1_v, L1_gnn_conv2_w, L1_gnn_bn2_g, L1_gnn_bn2_b, L1_gnn_bn2_m, L1_gnn_bn2_v, L1_gnn_w_msg, L1_gnn_b_msg, L1_gnn_w_ih, L1_gnn_b_ih, L1_gnn_w_hh, L1_gnn_b_hh), axis=-1)
    x = _layernorm(x + _L2_gnn_ref(x, adj, L2_gnn_W, L2_gnn_conv_w, L2_gnn_conv_b), axis=-1)
    x = _layernorm(x + _L3_gnn_ref(x, adj, L3_gnn_eps, L3_gnn_W1, L3_gnn_b1, L3_gnn_W2, L3_gnn_b2), axis=-1)
    return x

_drawn_inputs = setup_inputs


def setup_inputs(seed=0):
    import zlib

    import numpy as np

    out = dict(_drawn_inputs(seed))
    spreads = {'L0_gnn_b1': (0.0, 0.1),
     'L0_gnn_rms_weight': (1.0, 0.2),
     'L0_gnn_b2': (0.0, 0.1),
     'L1_gnn_b_se': (0.0, 0.8),
     'L1_gnn_bn1_g': (1.0, 0.6),
     'L1_gnn_bn1_b': (0.0, 0.392),
     'L1_gnn_bn1_m': (0.0, 0.377),
     'L1_gnn_bn1_v': (1.0, 0.6),
     'L1_gnn_bn2_g': (1.0, 0.2),
     'L1_gnn_bn2_b': (0.0, 0.659),
     'L1_gnn_bn2_m': (0.0, 0.519),
     'L1_gnn_bn2_v': (1.0, 0.6),
     'L1_gnn_b_msg': (0.0, 0.347),
     'L1_gnn_b_ih': (0.0, 0.1),
     'L1_gnn_b_hh': (0.0, 0.379)}
    factors = {'L3_gnn_b1': 3.328}
    for name, (base, spread) in spreads.items():
        noise = np.random.default_rng([zlib.crc32(name.encode()), seed]).standard_normal(out[name].shape)
        drawn = base * np.exp(spread * noise) if base else spread * noise
        out[name] = jnp.asarray(drawn.astype(out[name].dtype))
    for name, factor in factors.items():
        out[name] = (out[name] * factor).astype(out[name].dtype)
    return out
```

```python
from contextlib import ExitStack

import concourse.bass as bass
from concourse import mybir

F32 = mybir.dt.float32
F32R = mybir.dt.float32r
ALU = mybir.AluOpType
ACT = mybir.ActivationFunctionType
AX_X = mybir.AxisListType.X

P = 128
LN_EPS = 1e-5
RMS_EPS = 1e-6
BN_EPS = 1e-5
ROW_SUM_EPS = 1e-9
LEAKY_SLOPE = 0.2

STEPS = """
adj_t_ps at_eps at row_inv nb_ps agg_hi agg_lo h_ps0 h_ps1 h_ps2 h_ps3 h0 h1 h2 h3 sq0 sq1 sq2 sq3
sq01 sq23 sq_sum sq_ps ms r_rms r_ps hn0 hn1 hn2 hn3 th0 th1 th2 th3 s0 s1 s2 s3 row_sum
xb y0_ps y0 bn0 mv0 ve0 r0 x1_rows
x1_ps x1 x1_hi x1_lo msg_ps msg_pre msg pts_ps pts_r0 pts_l1 pts_r2 pts_l0 c1_ps hc_hi hc hc_lo
ghn_ps ghn dist_ps edge edge_adj nmp_ps xn_hi xn_lo c2_ps c2_res xc_hi xc xc_lo
r_gate_ps z_gate_ps n_gate_ps tr tz u v nn x_minus_n x_plus_n zq y1 y1_ps bn1 mv1 ve1 r1 x2_rows
x2_ps x2 ht_ps w3h w2h w1h w0h hop1_ps t2 hop2_ps t1 hop3_ps prop leaky y2 bn2 mv2 ve2 r2 x3_rows
x3b at3 agg3_ps agg3_hi agg3_lo z_ps0 z_ps1 z0 z1 y3_ps y3 bn3 mv3 ve3 r3 out_rows
""".split()


def after(engine, semaphore, count):
    if isinstance(count, int) and count <= 0:
        return
    engine.wait_ge(semaphore, count)


class Turn:

    def __init__(self, t, parity, stages, engine=None):
        at = [t + k for k in range(4)]
        if engine is not None:
            at = [engine.snap(a) for a in at]
        self.t, self.stages = t, stages
        self.now1, self.was1, self.old1 = at[3], at[2], at[1]
        self.now2, self.was2, self.old2 = at[2], at[1], at[0]
        self.now3, self.was3 = at[1], at[0]
        self.slot1, self.slot2, self.slot3 = parity, 1 - parity, parity


def run_turns(engine, turn, groups):
    turn(Turn(-2, 0, (1,)))
    turn(Turn(-1, 1, (1, 2)))
    turn(Turn(0, 0, (1, 2, 3)))
    turn(Turn(1, 1, (1, 2, 3)))
    with engine.Fori(2, groups - 2, 2) as t:
        turn(Turn(t, 0, (1, 2, 3), engine))
        turn(Turn(t + 1, 1, (1, 2, 3), engine))
    turn(Turn(groups - 2, 0, (2, 3)))
    turn(Turn(groups - 1, 1, (3,)))


def graph_layers(nc, x, adj, out, w):
    B, N, D = x.shape
    G = 4
    GROUPS = B // G
    W = G * N
    assert N == P and D == P and GROUPS % 2 == 0
    H0 = w["L0_gnn_W1"].shape[1] // P
    H3 = w["L3_gnn_W1"].shape[1] // P
    TAPS = w["L1_gnn_conv2_w"].shape[2]
    PAD = TAPS // 2
    NP = N + 2 * PAD
    CODES = w["L1_gnn_w_se"].shape[0]

    CONV2, CONV1, SE = 0, TAPS, TAPS + 1
    IH = TAPS + 2
    HH = IH + 6
    MSG = HH + 3
    PROP = MSG + 1
    NT = PROP + 1
    assert NT < 8 * G

    with ExitStack() as ctx:
        def sb(name, shape, dt=F32):
            return ctx.enter_context(nc.sbuf_tensor(name, shape, dt))

        def rows(name, dt=F32):
            return sb(name, [P, G, P], dt)

        bank = [ctx.enter_context(nc.psum_tensor(f"bank{i}", [P, G, P], F32)) for i in range(8)]
        sem = {n: ctx.enter_context(nc.semaphore(n)) for n in STEPS}
        x_in = [ctx.enter_context(nc.semaphore(f"x_in{i}")) for i in range(2)]
        adj_in = [ctx.enter_context(nc.semaphore(f"adj_in{i}")) for i in range(2)]
        stored = [ctx.enter_context(nc.semaphore(f"stored{i}")) for i in range(2)]
        vectors_in = ctx.enter_context(nc.semaphore("vectors_in"))
        weights_in = ctx.enter_context(nc.semaphore("weights_in"))
        codes_in = ctx.enter_context(nc.semaphore("codes_in"))
        cleared = ctx.enter_context(nc.semaphore("cleared"))
        set_pool = ctx.enter_context(nc.semaphore("set_pool"))
        set_dve = ctx.enter_context(nc.semaphore("set_dve"))
        set_pe = ctx.enter_context(nc.semaphore("set_pe"))
        set_act = ctx.enter_context(nc.semaphore("set_act"))

        ident = sb("ident", [P, P])
        ones = sb("ones", [P, P])
        minus_half = sb("minus_half", [P, G])
        w1f = sb("w1f", [P, H0 * P])
        w1_hi = sb("w1_hi", [P, H0 * P], F32R)
        w1_lo = sb("w1_lo", [P, H0 * P], F32R)
        w2 = sb("w2", [P, H0, D])
        w31f = sb("w31f", [P, H3 * P])
        w31_hi = sb("w31_hi", [P, H3 * P], F32R)
        w31_lo = sb("w31_lo", [P, H3 * P], F32R)
        w32 = sb("w32", [P, H3, D])
        arena = sb("arena", [P, 5, G, P])
        assert P * TAPS <= 5 * G * P
        conv2_w = arena[:].rearrange("p a g n -> p (a g n)")[:, 0:P * TAPS].rearrange(
            "p (i k) -> p i k", k=TAPS)
        conv1_w = sb("conv1_w", [P, P])
        codes_w = sb("codes_w", [P, P])
        msg_w = sb("msg_w", [P, P])
        ih_w = sb("ih_w", [P, 3, 2, P])
        hh_w = sb("hh_w", [P, 3, P])
        prop_w = sb("prop_w", [P, P])
        wt_hi = sb("wt_hi", [P, NT, P], F32R)
        wt_lo = sb("wt_lo", [P, NT, P], F32R)
        wt_full = sb("wt_full", [P, 2, P])
        vectors = [("b1", w["L0_gnn_b1"], H0), ("rms", w["L0_gnn_rms_weight"], H0), ("g1", w["L1_gnn_bn1_g"], 1),
                   ("g2", w["L1_gnn_bn2_g"], 1), ("b1n", w["L1_gnn_bn1_b"], 1), ("b2n", w["L1_gnn_bn2_b"], 1),
                   ("m1", w["L1_gnn_bn1_m"], 1), ("m2", w["L1_gnn_bn2_m"], 1), ("v1", w["L1_gnn_bn1_v"], 1),
                   ("v2", w["L1_gnn_bn2_v"], 1), ("bi", w["L1_gnn_b_ih"], 3), ("bh", w["L1_gnn_b_hh"], 3),
                   ("b31", w["L3_gnn_b1"], H3)]
        first_row, VR = {}, 0
        for name, _, count in vectors:
            first_row[name] = VR
            VR += count
        vector_rows = sb("vector_rows", [VR, P])
        vector_cols = sb("vector_cols", [P, VR])

        def columns(name, count):
            return vector_cols[:, first_row[name]:first_row[name] + count]

        b1_col = columns("b1", H0)
        rms_col = columns("rms", H0)
        half_rms = sb("half_rms", [P, H0])
        b31_col = columns("b31", H3)
        codes_b = sb("codes_b", [P, 1])
        bn_g, bn_b, bn_m, bn_v = (columns(n, 2) for n in ("g1", "b1n", "m1", "v1"))
        bn_ve = sb("bn_ve", [P, 2])
        bn_r = sb("bn_r", [P, 2])
        bn_scale = sb("bn_scale", [P, 2])
        bn_ms = sb("bn_ms", [P, 2])
        bn_shift = sb("bn_shift", [P, 2])
        gate_bi = columns("bi", 3)
        gate_bh = columns("bh", 3)
        gate_b = sb("gate_b", [P, 2])
        half_gate_b = sb("half_gate_b", [P, 2])
        half_bhn = sb("half_bhn", [P, 1])
        b2_row = sb("b2_row", [P, D])
        msg_row = sb("msg_row", [P, D])
        b32_row = sb("b32_row", [P, D])
        eps0 = sb("eps0", [P, 1])
        eps3 = sb("eps3", [P, 1])
        one_eps3 = sb("one_eps3", [P, 1])
        prop_k = sb("prop_k", [P, 4])
        prop_b = sb("prop_b", [P, 1])

        x_rows = [rows(f"x_rows{i}") for i in range(2)]
        adj_rows = [rows(f"adj_rows{i}") for i in range(2)]
        at = [rows(f"at{i}") for i in range(2)]
        row_inv = [sb(f"row_inv{i}", [P, G]) for i in range(2)]
        row_sum = sb("row_sum", [P, G])
        row_sum_eps = sb("row_sum_eps", [P, G])
        at_eps = rows("at_eps")
        agg_hi, agg_lo = rows("agg_hi", F32R), rows("agg_lo", F32R)
        h = [rows(f"h{c}") for c in range(H0)]
        sq = [rows(f"sq{c}") for c in range(H0)]
        hn = [rows(f"hn{c}") for c in range(H0)]
        th = [rows(f"th{c}") for c in range(H0)]
        s = h
        sq01, sq23, sq_sum = sq[0], sq[2], sq[1]
        ms = sb("ms", [P, G])
        r_rms = sb("r_rms", [P, G])
        xb = rows("xb")
        y0 = rows("y0")
        x1_rows = rows("x1_rows")
        x1 = rows("x1")
        x1_hi, x1_lo = rows("x1_hi", F32R), rows("x1_lo", F32R)
        msg_pre, msg = rows("msg_pre"), rows("msg")
        pts_l, pts_r = rows("pts_l"), rows("pts_r")
        hc = rows("hc")
        hc_hi, hc_lo = sb("hc_hi", [P, G, NP], F32R), sb("hc_lo", [P, G, NP], F32R)
        ghn = rows("ghn")
        edge, edge_adj = rows("edge"), rows("edge_adj")
        xn_hi, xn_lo = rows("xn_hi", F32R), rows("xn_lo", F32R)
        c2_res, xc = rows("c2_res"), rows("xc")
        xc_hi, xc_lo = rows("xc_hi", F32R), rows("xc_lo", F32R)
        tr, tz, u, nn = rows("tr"), rows("tz"), rows("u"), rows("nn")
        v = u
        x_minus_n, x_plus_n, zq = rows("x_minus_n"), rows("x_plus_n"), rows("zq")
        y1 = zq
        x2_rows, x2 = rows("x2_rows"), rows("x2")
        wh = [rows(f"w{k}h") for k in range(4)]
        t2, t1, prop = rows("t2"), rows("t1"), rows("prop")
        leaky = prop
        y2, x3_rows, x3b, at3, y3 = (arena[:, i] for i in range(5))
        agg3_hi, agg3_lo = rows("agg3_hi", F32R), rows("agg3_lo", F32R)
        z3 = [rows(f"z3_{c}") for c in range(H3)]
        out_rows = [rows(f"out_rows{i}") for i in range(2)]
        stats = [sb(f"stats{i}", [P, G, 6]) for i in range(4)]
        mv = [sb(f"mv{i}", [P, G, 2]) for i in range(4)]
        ve = [sb(f"ve{i}", [P, G]) for i in range(4)]
        rstd = [sb(f"rstd{i}", [P, G]) for i in range(4)]

        def cols(tile):
            return tile[:].rearrange("p g n -> p (g n)")

        def over_graphs(tile):
            return tile[:].unsqueeze(1).to_broadcast([P, G, P])

        x_dram = x.rearrange("(k g) n d -> k n g d", g=G)
        adj_dram = adj.rearrange("(k g) n m -> k n g m", g=G)
        out_dram = out.rearrange("(k g) n d -> k n g d", g=G)

        def one_row(vector):
            n = vector.shape[0]
            return vector.rearrange("(a d) -> a d", a=1).to_broadcast([P, n])

        IDENT_SET = 3
        BN_POW = 4
        BN_VE = 1
        CONV_SCALED = 6
        WT_BANKS = -(-NT // G)
        SPLIT_ACT = WT_BANKS + 4
        DVE_SMALL = 17
        SPLIT_DVE = DVE_SMALL + WT_BANKS + 2

        def loads_of(T, engine):
            if isinstance(T.t, int):
                return 16 * ((T.t + 2) // 2 + 1)
            return engine.snap(8 * (T.t - T.slot1) + 32)

        block = ctx.enter_context(nc.Block())

        WEIGHT_LOADS = [
            (w1f[:], w["L0_gnn_W1"]),
            (w2[:], w["L0_gnn_W2"].rearrange("(c p) d -> p c d", p=P)),
            (b2_row[:], one_row(w["L0_gnn_b2"])),
            (eps0[:], w["L0_gnn_epsilon"].to_broadcast([P, 1])),
            (conv1_w[:], w["L1_gnn_conv1_w"].rearrange("o i k -> o (i k)")),
            (conv2_w, w["L1_gnn_conv2_w"]),
            (msg_w[:], w["L1_gnn_w_msg"]),
            (msg_row[:], one_row(w["L1_gnn_b_msg"])),
            (ih_w[:], w["L1_gnn_w_ih"].rearrange("(a o) (b i) -> o a b i", a=3, b=2)),
            (hh_w[:], w["L1_gnn_w_hh"].rearrange("(a o) i -> o a i", a=3)),
            (prop_w[:], w["L2_gnn_W"]),
            (prop_k[:], one_row(w["L2_gnn_conv_w"])),
            (prop_b[:], one_row(w["L2_gnn_conv_b"])),
            (eps3[:], one_row(w["L3_gnn_eps"])),
            (w31f[:], w["L3_gnn_W1"]),
            (w32[:], w["L3_gnn_W2"].rearrange("(c p) d -> p c d", p=P)),
            (b32_row[:], one_row(w["L3_gnn_b2"])),
        ]
        ALL_WEIGHTS = 16 * len(WEIGHT_LOADS)
        CODE_ROWS = (0, 32, 64)
        ALL_CODES = 16 * 2 * len(CODE_ROWS)

        @block.sync
        def _(sp):
            def load(group, slot, count):
                after(sp, sem["adj_t_ps"], count)
                after(sp, sem["row_sum"], count)
                sp.dma_start(adj_rows[slot][:], adj_dram[group]).then_inc(adj_in[slot], 16)
                after(sp, sem["nb_ps"], count)
                after(sp, sem["xb"], count)
                sp.dma_start(x_rows[slot][:], x_dram[group]).then_inc(x_in[slot], 16)

            def turn(T):
                if 1 in T.stages:
                    load(T.t + 3, 1 - T.slot1, T.was1)
                if 3 in T.stages:
                    sp.wait_ge(sem["out_rows"], T.now3)
                    sp.dma_start(out_dram[T.t], out_rows[T.slot3][:]).then_inc(stored[T.slot3], 16)

            load(0, 0, 0)
            sp.wait_ge(cleared, 1)
            for at_row in CODE_ROWS:
                sp.dma_start(codes_w[at_row:at_row + CODES, :], w["L1_gnn_w_se"]).then_inc(codes_in, 16)
                sp.dma_start(codes_b[at_row:at_row + CODES, :], w["L1_gnn_b_se"].rearrange("(p a) -> p a", a=1)).then_inc(codes_in, 16)
            for name, vector, count in vectors:
                r = first_row[name]
                sp.dma_start(vector_rows[r:r + count, :], vector.rearrange("(a p) -> a p", a=count)
                             ).then_inc(vectors_in, 16)
            for tile, source in WEIGHT_LOADS:
                sp.dma_start(tile, source).then_inc(weights_in, 16)

            turn(Turn(-2, 0, (1,)))
            turn(Turn(-1, 1, (1, 2)))
            with sp.Fori(0, GROUPS - 4, 2) as t:
                turn(Turn(t, 0, (1, 2, 3), sp))
                turn(Turn(t + 1, 1, (1, 2, 3), sp))
            turn(Turn(GROUPS - 4, 0, (1, 2, 3)))
            for t in (GROUPS - 3, GROUPS - 2, GROUPS - 1):
                turn(Turn(t, t % 2, (3,)))
            for slot in range(2):
                sp.wait_ge(stored[slot], 16 * (GROUPS // 2))

        @block.tensor
        def _(pe):
            def split_product(psum, hi, lo, moving_hi, moving_lo, start, stop):
                pe.matmul(psum, hi, moving_hi, start=start, stop=False)
                pe.matmul(psum, hi, moving_lo, start=False, stop=False)
                return pe.matmul(psum, lo, moving_hi, start=False, stop=stop)

            def weight(k):
                return wt_hi[:, k, :], wt_lo[:, k, :]

            def transposes(psum, tile):
                for g in range(G):
                    last = pe.transpose(psum[:, g, :], tile[:, g, :], ident[:])
                return last

            def by_graph(psum, lhs, rhs):
                for g in range(G):
                    last = pe.matmul(psum[:, g, :], lhs(g), rhs(g), start=True, stop=True)
                return last

            def adj_t(T):
                pe.wait_ge(adj_in[T.slot1], T.loads)
                after(pe, sem["hn3"], T.was1)
                transposes(bank[0], adj_rows[T.slot1]).then_inc(sem["adj_t_ps"], 1)

            def neighbours(T):
                pe.wait_ge(x_in[T.slot1], T.loads)
                pe.wait_ge(sem["at_eps"], T.now1)
                after(pe, sem["y0"], T.was1)
                by_graph(bank[1], lambda g: x_rows[T.slot1][:, g, :],
                         lambda g: at_eps[:, g, :]).then_inc(sem["nb_ps"], 1)

            def hidden(T, c):
                if c == 0:
                    pe.wait_ge(sem["agg_hi"], T.now1)
                    pe.wait_ge(sem["agg_lo"], T.now1)
                if c == 1:
                    pe.wait_ge(sem["at"], T.now1)
                if c >= 2:
                    pe.wait_ge((sem["h0"], sem["h1"])[c - 2], T.now1)
                    pe.wait_ge((sem["sq0"], sem["sq1"])[c - 2], T.now1)
                split_product(bank[1 - c % 2][:].rearrange("p g n -> p (g n)"),
                              w1_hi[:, c * P:(c + 1) * P], w1_lo[:, c * P:(c + 1) * P],
                              cols(agg_hi), cols(agg_lo), True, True
                              ).then_inc((sem["h_ps0"], sem["h_ps1"], sem["h_ps2"], sem["h_ps3"])[c], 1)

            def square_sums(T):
                pe.wait_ge(sem["sq_sum"], T.now1)
                pe.wait_ge(sem["h2"], T.now1)
                by_graph(bank[1], lambda g: sq_sum[:, g, :], lambda g: ones[:]).then_inc(sem["sq_ps"], 1)

            def spread_rms(T):
                pe.wait_ge(sem["r_rms"], T.now1)
                pe.wait_ge(sem["h3"], T.now1)
                pe.wait_ge(sem["sq3"], T.now1)
                for g in range(G):
                    last = pe.transpose(bank[0][:, g, :], r_rms[:, g:g + 1].to_broadcast([P, P]), ident[:])
                last.then_inc(sem["r_ps"], 1)

            def down(T, c):
                pe.wait_ge((sem["s0"], sem["s1"], sem["s2"], sem["s3"])[c], T.now1)
                if c == 0:
                    pe.wait_ge(sem["ms"], T.now1)
                for g in range(G):
                    last = pe.matmul(bank[1][:, g, :], s[c][:, g, :], w2[:, c, :],
                                     start=(c == 0 and g == 0), stop=(c == H0 - 1),
                                     skip_group_check=True)
                if c == H0 - 1:
                    last.then_inc(sem["y0_ps"], 1)

            def x1_t(T):
                pe.wait_ge(sem["x1_rows"], T.now2)
                after(pe, sem["tr"], T.was2)
                transposes(bank[3], x1_rows).then_inc(sem["x1_ps"], 1)

            def messages(T):
                pe.wait_ge(sem["x1"], T.now2)
                after(pe, sem["tz"], T.was2)
                by_graph(bank[4], lambda g: x1[:, g, :], lambda g: wt_full[:, 0, :]).then_inc(sem["msg_ps"], 1)

            def codes(T):
                pe.wait_ge(sem["x1_lo"], T.now2)
                pe.wait_ge(sem["x1_hi"], T.now2)
                after(pe, sem["v"], T.was2)
                split_product(cols(bank[5]), *weight(SE), cols(x1_hi), cols(x1_lo), True, True
                              ).then_inc(sem["pts_ps"], 1)

            def conv1(T):
                pe.wait_ge(sem["x1_lo"], T.now2)
                pe.wait_ge(sem["x1"], T.now2)
                split_product(cols(bank[3]), *weight(CONV1), cols(x1_hi), cols(x1_lo), True, True
                              ).then_inc(sem["c1_ps"], 1)

            def hidden_n(T):
                after(pe, sem["bn1"], T.was2)
                after(pe, sem["x2_rows"], T.was2)
                split_product(cols(bank[2]), *weight(HH + 2), cols(x1_hi), cols(x1_lo), True, True
                              ).then_inc(sem["ghn_ps"], 1)

            def distances(T):
                pe.wait_ge(sem["pts_l0"], T.now2)
                pe.wait_ge(sem["pts_r0"], T.now2)
                pe.wait_ge(sem["pts_l1"], T.now2)
                pe.wait_ge(sem["pts_r2"], T.now2)
                pe.wait_ge(sem["msg_pre"], T.now2)
                K = CODE_ROWS[2] + CODES
                by_graph(bank[4], lambda g: pts_l[0:K, g, :], lambda g: pts_r[0:K, g, :]
                         ).then_inc(sem["dist_ps"], 1)

            def conv2(T, first, end):
                if first == 0:
                    pe.wait_ge(sem["hc_lo"], T.now2)
                    pe.wait_ge(sem["hc_hi"], T.now2)
                    pe.wait_ge(sem["ghn"], T.now2)
                for k in range(first, end):
                    last = split_product(bank[2][:], *weight(CONV2 + k), hc_hi[:, :, k:k + N],
                                         hc_lo[:, :, k:k + N], k == 0, k == TAPS - 1)
                if end == TAPS:
                    last.then_inc(sem["c2_ps"], 1)

            def gather(T):
                pe.wait_ge(sem["msg"], T.now2)
                pe.wait_ge(sem["edge_adj"], T.now2)
                pe.wait_ge(sem["pts_l0"], T.now2)
                pe.wait_ge(sem["pts_r2"], T.now2)
                by_graph(bank[5], lambda g: msg[:, g, :], lambda g: edge_adj[:, g, :]).then_inc(sem["nmp_ps"], 1)

            def gates_x(T):
                pe.wait_ge(sem["hc_hi"], T.now2)
                pe.wait_ge(sem["hc"], T.now2)
                split_product(cols(bank[3]), *weight(HH + 0), cols(x1_hi), cols(x1_lo), True, False)

            def gates_x_z(T):
                pe.wait_ge(sem["edge"], T.now2)
                split_product(cols(bank[4]), *weight(HH + 1), cols(x1_hi), cols(x1_lo), True, False)

            def gates_nmp(T):
                pe.wait_ge(sem["xn_hi"], T.now2)
                pe.wait_ge(sem["xn_lo"], T.now2)
                split_product(cols(bank[3]), *weight(IH + 1), cols(xn_hi), cols(xn_lo), False, False)
                split_product(cols(bank[4]), *weight(IH + 3), cols(xn_hi), cols(xn_lo), False, False)
                split_product(cols(bank[5]), *weight(IH + 5), cols(xn_hi), cols(xn_lo), True, False)

            def gates_conv(T):
                pe.wait_ge(sem["xc_hi"], T.now2)
                pe.wait_ge(sem["xc_lo"], T.now2)
                split_product(cols(bank[3]), *weight(IH + 0), cols(xc_hi), cols(xc_lo), False, True
                              ).then_inc(sem["r_gate_ps"], 1)
                split_product(cols(bank[5]), *weight(IH + 4), cols(xc_hi), cols(xc_lo), False, True
                              ).then_inc(sem["n_gate_ps"], 1)
                split_product(cols(bank[4]), *weight(IH + 2), cols(xc_hi), cols(xc_lo), False, True
                              ).then_inc(sem["z_gate_ps"], 1)

            def y1_t(T):
                pe.wait_ge(sem["y1"], T.now2)
                pe.wait_ge(sem["c2_res"], T.now2)
                transposes(bank[2], y1).then_inc(sem["y1_ps"], 1)

            def x2_t(T):
                pe.wait_ge(sem["x2_rows"], T.now3)
                after(pe, sem["y3"], T.was3)
                transposes(bank[6], x2_rows).then_inc(sem["x2_ps"], 1)

            def prop_in(T):
                pe.wait_ge(sem["x2"], T.now3)
                after(pe, sem["z1"], T.was3)
                by_graph(bank[7], lambda g: x2[:, g, :], lambda g: wt_full[:, 1, :]).then_inc(sem["ht_ps"], 1)

            def hop(T, k):
                if k == 1:
                    pe.wait_ge(sem["w3h"], T.now3)
                if k == 2:
                    pe.wait_ge(sem["t2"], T.now3)
                    pe.wait_ge(sem["w0h"], T.now3)
                if k == 3:
                    pe.wait_ge(sem["t1"], T.now3)
                moving = (wh[3], t2, t1)[k - 1]
                by_graph(bank[(6, 7, 6)[k - 1]], lambda g: at[T.slot3][:, g, :], lambda g: moving[:, g, :]
                         ).then_inc((sem["hop1_ps"], sem["hop2_ps"], sem["hop3_ps"])[k - 1], 1)

            def gather3(T):
                pe.wait_ge(sem["x3_rows"], T.now3)
                pe.wait_ge(sem["at3"], T.now3)
                by_graph(bank[7], lambda g: x3_rows[:, g, :], lambda g: at3[:, g, :]).then_inc(sem["agg3_ps"], 1)

            def hidden3(T, c):
                if c == 0:
                    pe.wait_ge(sem["agg3_hi"], T.now3)
                    pe.wait_ge(sem["agg3_lo"], T.now3)
                    pe.wait_ge(sem["prop"], T.now3)
                split_product(cols(bank[6 + c]), w31_hi[:, c * P:(c + 1) * P], w31_lo[:, c * P:(c + 1) * P],
                              cols(agg3_hi), cols(agg3_lo), True, True
                              ).then_inc((sem["z_ps0"], sem["z_ps1"])[c], 1)

            def down3(T):
                pe.wait_ge(sem["z0"], T.now3)
                for c in range(H3):
                    if c == 1:
                        pe.wait_ge(sem["z1"], T.now3)
                    for g in range(G):
                        last = pe.matmul(bank[6][:, g, :], z3[c][:, g, :], w32[:, c, :],
                                         start=(c == 0 and g == 0), stop=(c == H3 - 1),
                                         skip_group_check=True)
                last.then_inc(sem["y3_ps"], 1)

            def turn(T):
                one, two, three = (k in T.stages for k in (1, 2, 3))
                T.loads = loads_of(T, pe)
                if one: adj_t(T)
                if two: x1_t(T)
                if one: neighbours(T)
                if three: x2_t(T)
                if two: messages(T); codes(T)
                if three: prop_in(T)
                if two: conv1(T); hidden_n(T)
                if three: hop(T, 1)
                if two: gates_x(T); distances(T); gates_x_z(T); conv2(T, 0, 3)
                if three: hop(T, 2)
                if two: conv2(T, 3, 5)
                if three: hop(T, 3)
                if two: gather(T); conv2(T, 5, 8)
                if one: hidden(T, 0); hidden(T, 1)
                if two: conv2(T, 8, 10); gates_nmp(T)
                if one: hidden(T, 2)
                if two: conv2(T, 10, 12)
                if one: hidden(T, 3)
                if two: conv2(T, 12, 15)
                if three: gather3(T)
                if one: square_sums(T)
                if two: conv2(T, 15, TAPS)
                if three: hidden3(T, 0)
                if one: spread_rms(T)
                if three: hidden3(T, 1)
                if one: down(T, 0)
                if two: gates_conv(T)
                if one: down(T, 1); down(T, 2); down(T, 3)
                if three: down3(T)
                if two: y1_t(T)

            pe.wait_ge(vectors_in, 16 * len(vectors))
            pe.wait_ge(set_pool, IDENT_SET)
            pe.transpose(bank[7][:, G - 1, 0:VR], vector_rows[:], ident[0:VR, 0:VR]).then_inc(set_pe, 1)
            pe.wait_ge(weights_in, ALL_WEIGHTS)
            pe.wait_ge(codes_in, ALL_CODES)
            pe.wait_ge(set_dve, CONV_SCALED)
            sources = [conv2_w[:, :, k] for k in range(TAPS)] + [conv1_w[:], codes_w[:]]
            sources += [ih_w[:, a, b, :] for a in range(3) for b in range(2)]
            sources += [hh_w[:, a, :] for a in range(3)] + [msg_w[:], prop_w[:]]
            for k, source in enumerate(sources):
                last = pe.transpose(bank[k // G][:, k % G, :], source, ident[:])
                if k % G == G - 1 or k == NT - 1:
                    last.then_inc(set_pe, 1)
            pe.wait_ge(set_act, SPLIT_ACT)
            pe.wait_ge(set_dve, SPLIT_DVE)
            run_turns(pe, turn, GROUPS)

        @block.scalar
        def _(act):
            def copy(out, in_):
                return nc.scalar.activation(out, in_, ACT.Copy)

            def a_t(T):
                pe_at = at[T.slot1]
                act.wait_ge(sem["adj_t_ps"], T.now1)
                after(act, sem["hop3_ps"], T.old1)
                after(act, sem["at3"], T.old1)
                after(act, sem["edge_adj"], T.old1)
                act.wait_ge(sem["at_eps"], T.now1)
                copy(pe_at[:], bank[0][:]).then_inc(sem["at"], 1)

            def agg(T):
                act.wait_ge(sem["nb_ps"], T.now1)
                after(act, sem["h_ps3"], T.was1)
                copy(agg_hi[:], bank[1][:]).then_inc(sem["agg_hi"], 1)

            def hidden(T, c):
                act.wait_ge((sem["h_ps0"], sem["h_ps1"], sem["h_ps2"], sem["h_ps3"])[c], T.now1)
                after(act, (sem["sq01"], sem["sq_sum"], sem["sq23"], sem["sq_sum"])[c], T.was1)
                after(act, sem["sq_ps"], T.was1)
                nc.scalar.activation(sq[c][:], bank[1 - c % 2][:], ACT.Square, bias=b1_col[:, c:c + 1]
                                     ).then_inc((sem["sq0"], sem["sq1"], sem["sq2"], sem["sq3"])[c], 1)
                after(act, sem["y0_ps"], T.was1)
                nc.scalar.activation(h[c][:], bank[1 - c % 2][:], ACT.Identity, bias=b1_col[:, c:c + 1]
                                     ).then_inc((sem["h0"], sem["h1"], sem["h2"], sem["h3"])[c], 1)

            def tanh0(T, c):
                act.wait_ge((sem["hn0"], sem["hn1"], sem["hn2"], sem["hn3"])[c], T.now1)
                after(act, (sem["s0"], sem["s1"], sem["s2"], sem["s3"])[c], T.was1)
                nc.scalar.activation(th[c][:], hn[c][:], ACT.Tanh, scale=half_rms[:, c:c + 1]
                                     ).then_inc((sem["th0"], sem["th1"], sem["th2"], sem["th3"])[c], 1)

            def x1_parts(T):
                act.wait_ge(sem["x1_ps"], T.now2)
                after(act, sem["z_gate_ps"], T.was2)
                copy(x1_hi[:], bank[3][:]).then_inc(sem["x1_hi"], 1)
                after(act, sem["x_plus_n"], T.was2)
                after(act, sem["x_minus_n"], T.was2)
                copy(x1[:], bank[3][:]).then_inc(sem["x1"], 1)

            def points(T):
                act.wait_ge(sem["pts_ps"], T.now2)
                after(act, sem["dist_ps"], T.was2)
                r0, r1, r2 = (slice(a, a + CODES) for a in CODE_ROWS)
                nc.scalar.activation(pts_r[r0], bank[5][r0], ACT.Identity, bias=codes_b[r0]
                                     ).then_inc(sem["pts_r0"], 1)
                nc.scalar.activation(pts_l[r1], bank[5][r1], ACT.Square, bias=codes_b[r1]
                                     ).then_inc(sem["pts_l1"], 1)
                nc.scalar.activation(pts_r[r2], bank[5][r2], ACT.Square, bias=codes_b[r2]
                                     ).then_inc(sem["pts_r2"], 1)

            def conv1_hi(T):
                act.wait_ge(sem["c1_ps"], T.now2)
                after(act, sem["c2_ps"], T.was2)
                nc.scalar.activation(hc_hi[:, :, PAD:PAD + N], bank[3][:], ACT.Relu, bias=bn_shift[:, 0:1]
                                     ).then_inc(sem["hc_hi"], 1)

            def message(T):
                act.wait_ge(sem["msg_pre"], T.now2)
                after(act, sem["nmp_ps"], T.was2)
                nc.scalar.activation(msg[:], msg_pre[:], ACT.Relu).then_inc(sem["msg"], 1)

            def hidden_n(T):
                act.wait_ge(sem["ghn_ps"], T.now2)
                after(act, sem["u"], T.was2)
                nc.scalar.activation(ghn[:], bank[2][:], ACT.Identity, bias=half_bhn[:], scale=0.5
                                     ).then_inc(sem["ghn"], 1)

            def edges(T):
                act.wait_ge(sem["dist_ps"], T.now2)
                after(act, sem["edge_adj"], T.was2)
                nc.scalar.activation(edge[:], bank[4][:], ACT.Exp, scale=-1.0).then_inc(sem["edge"], 1)

            def nmp_hi(T):
                act.wait_ge(sem["nmp_ps"], T.now2)
                after(act, sem["z_gate_ps"], T.was2)
                copy(xn_hi[:], bank[5][:]).then_inc(sem["xn_hi"], 1)

            def conv_hi(T):
                act.wait_ge(sem["c2_res"], T.now2)
                after(act, sem["z_gate_ps"], T.was2)
                nc.scalar.activation(xc_hi[:], c2_res[:], ACT.Relu, bias=bn_shift[:, 1:2]
                                     ).then_inc(sem["xc_hi"], 1)

            def gate_r(T):
                act.wait_ge(sem["r_gate_ps"], T.now2)
                after(act, sem["u"], T.was2)
                nc.scalar.activation(tr[:], bank[3][:], ACT.Tanh, bias=half_gate_b[:, 0:1], scale=0.5
                                     ).then_inc(sem["tr"], 1)

            def gate_z(T):
                act.wait_ge(sem["z_gate_ps"], T.now2)
                after(act, sem["zq"], T.was2)
                nc.scalar.activation(tz[:], bank[4][:], ACT.Tanh, bias=half_gate_b[:, 1:2], scale=0.5
                                     ).then_inc(sem["tz"], 1)

            def gate_n(T):
                act.wait_ge(sem["v"], T.now2)
                after(act, sem["x_minus_n"], T.was2)
                after(act, sem["x_plus_n"], T.was2)
                nc.scalar.activation(nn[:], v[:], ACT.Tanh, bias=gate_bi[:, 2:3]).then_inc(sem["nn"], 1)

            def x2_cols(T):
                act.wait_ge(sem["x2_ps"], T.now3)
                after(act, sem["ht_ps"], T.was3)
                copy(x2[:], bank[6][:]).then_inc(sem["x2"], 1)

            def multiples(T):
                act.wait_ge(sem["ht_ps"], T.now3)
                after(act, sem["hop1_ps"], T.was3)
                after(act, sem["prop"], T.was3)
                for k in (3, 2, 1):
                    nc.scalar.activation(wh[k][:], bank[7][:], ACT.Copy, scale=prop_k[:, k:k + 1]
                                         ).then_inc({3: sem["w3h"], 2: sem["w2h"], 1: sem["w1h"]}[k], 1)
                nc.scalar.activation(wh[0][:], bank[7][:], ACT.Identity, bias=prop_b[:],
                                     scale=prop_k[:, 0:1]).then_inc(sem["w0h"], 1)

            def agg3(T):
                act.wait_ge(sem["agg3_ps"], T.now3)
                after(act, sem["z_ps1"], T.was3)
                copy(agg3_hi[:], bank[7][:]).then_inc(sem["agg3_hi"], 1)

            def hidden3(T, c):
                act.wait_ge((sem["z_ps0"], sem["z_ps1"])[c], T.now3)
                after(act, sem["y3_ps"], T.was3)
                nc.scalar.activation(z3[c][:], bank[6 + c][:], ACT.Relu, bias=b31_col[:, c:c + 1]
                                     ).then_inc((sem["z0"], sem["z1"])[c], 1)

            def turn(T):
                one, two, three = (k in T.stages for k in (1, 2, 3))
                if two: x1_parts(T)
                if one: agg(T)
                if three: x2_cols(T)
                if two: points(T)
                if three: multiples(T)
                if two: conv1_hi(T); message(T); hidden_n(T); edges(T)
                if one: a_t(T)
                if two: nmp_hi(T)
                if one: hidden(T, 0); hidden(T, 1); hidden(T, 2); hidden(T, 3)
                if three: agg3(T); hidden3(T, 0); hidden3(T, 1)
                if one: tanh0(T, 0)
                if two: conv_hi(T)
                if one: tanh0(T, 1)
                if two: gate_r(T)
                if one: tanh0(T, 2)
                if two: gate_z(T)
                if one: tanh0(T, 3)
                if two: gate_n(T)

            act.wait_ge(set_pe, 1)
            copy(vector_cols[:], bank[7][:, G - 1, 0:VR]).then_inc(set_act, 1)
            act.wait_ge(weights_in, ALL_WEIGHTS)
            copy(w1_hi[:], w1f[:]).then_inc(set_act, 1)
            copy(w31_hi[:], w31f[:]).then_inc(set_act, 1)
            for b in range(WT_BANKS):
                n = min(G, NT - b * G)
                act.wait_ge(set_pe, 1 + b + 1)
                copy(wt_hi[:, b * G:b * G + n, :], bank[b][:, 0:n, :]).then_inc(set_act, 1)
            k = MSG % G
            copy(wt_full[:], bank[MSG // G][:, k:k + 2, :]).then_inc(set_act, 1)
            act.wait_ge(set_dve, DVE_SMALL)
            act.wait_ge(codes_in, ALL_CODES)
            run_turns(act, turn, GROUPS)

        @block.vector
        def _(dve):
            V = nc.vector

            def norm_stats(k, y, y_ready, bn_done, mv_done, ve_done, count, was):
                dve.wait_ge(y_ready, count)
                for g in range(G):
                    last = V.bn_stats(stats[k][:, g, :], y[:, g, :])
                last.then_inc(bn_done, 1)
                dve.wait_ge(set_dve, SPLIT_DVE)
                dve.wait_ge(bn_done, count)
                after(dve, (sem["x1_rows"], sem["x2_rows"], sem["x3_rows"], sem["out_rows"])[k], was)
                for g in range(G):
                    last = V.bn_aggr(mv[k][:, g, :], stats[k][:, g, :])
                last.then_inc(mv_done, 1)
                dve.wait_ge(mv_done, count)
                V.tensor_scalar(ve[k][:], mv[k][:, :, 1], LN_EPS, None, ALU.add).then_inc(ve_done, 1)

            def a_t_eps(T):
                dve.wait_ge(sem["adj_t_ps"], T.now1)
                after(dve, sem["nb_ps"], T.was1)
                V.scalar_tensor_tensor(out=at_eps[:], in0=over_graphs(ident), scalar=eps0[:],
                                       in1=bank[0][:], op0=ALU.mult, op1=ALU.add).then_inc(sem["at_eps"], 1)

            def row_sums(T):
                dve.wait_ge(adj_in[T.slot1], T.loads)
                after(dve, sem["prop"], T.old1)
                V.tensor_reduce(row_sum[:], adj_rows[T.slot1][:], AX_X, ALU.add).then_inc(sem["row_sum"], 1)
                dve.wait_ge(sem["row_sum"], T.now1)
                V.tensor_scalar(row_sum_eps[:], row_sum[:], ROW_SUM_EPS, None, ALU.add
                                ).then_inc(sem["row_inv"], 1)
                dve.wait_ge(sem["row_inv"], T.twice1)
                V.reciprocal(row_inv[T.slot1][:], row_sum_eps[:]).then_inc(sem["row_inv"], 1)

            def agg(T):
                dve.wait_ge(sem["agg_hi"], T.now1)
                after(dve, sem["h_ps3"], T.was1)
                V.tensor_tensor(agg_lo[:], bank[1][:], agg_hi[:].bitcast(F32), ALU.subtract
                                ).then_inc(sem["agg_lo"], 1)

            def sum_squares(T):
                dve.wait_ge(sem["sq01"], T.now1)
                dve.wait_ge(sem["sq23"], T.now1)
                V.tensor_tensor(sq_sum[:], sq01[:], sq23[:], ALU.add).then_inc(sem["sq_sum"], 1)

            def mean_square(T):
                dve.wait_ge(sem["sq_ps"], T.now1)
                V.tensor_scalar(ms[:], bank[1][:, :, 0], 1.0 / (H0 * P), RMS_EPS, ALU.mult, ALU.add
                                ).then_inc(sem["ms"], 1)

            def normalise(T, c):
                dve.wait_ge(sem["r_ps"], T.now1)
                V.tensor_tensor(hn[c][:], bank[0][:], h[c][:], ALU.mult
                                ).then_inc((sem["hn0"], sem["hn1"], sem["hn2"], sem["hn3"])[c], 1)

            def silu(T, c):
                dve.wait_ge((sem["th0"], sem["th1"], sem["th2"], sem["th3"])[c], T.now1)
                V.scalar_tensor_tensor(out=s[c][:], in0=th[c][:], scalar=1.0, in1=hn[c][:],
                                       op0=ALU.add, op1=ALU.mult
                                       ).then_inc((sem["s0"], sem["s1"], sem["s2"], sem["s3"])[c], 1)

            def residual0(T):
                dve.wait_ge(sem["y0_ps"], T.now1)
                dve.wait_ge(sem["xb"], T.now1)
                after(dve, sem["x1_rows"], T.was1)
                V.tensor_tensor(y0[:], bank[1][:], xb[:], ALU.add).then_inc(sem["y0"], 1)
                norm_stats(0, y0, sem["y0"], sem["bn0"], sem["mv0"], sem["ve0"], T.now1, T.was1)

            def x1_low(T):
                dve.wait_ge(sem["x1"], T.now2)
                after(dve, sem["z_gate_ps"], T.was2)
                V.tensor_tensor(x1_lo[:], bank[3][:], x1_hi[:].bitcast(F32), ALU.subtract
                                ).then_inc(sem["x1_lo"], 1)

            def message_bias(T):
                dve.wait_ge(sem["msg_ps"], T.now2)
                after(dve, sem["msg"], T.was2)
                V.tensor_tensor(msg_pre[:], bank[4][:], over_graphs(msg_row), ALU.add
                                ).then_inc(sem["msg_pre"], 1)

            def points(T):
                dve.wait_ge(sem["pts_r0"], T.now2)
                after(dve, sem["dist_ps"], T.was2)
                V.tensor_scalar(pts_l[0:CODES], bank[5][0:CODES], codes_b[0:CODES], -2.0, ALU.add,
                                ALU.mult).then_inc(sem["pts_l0"], 1)

            def conv1_full(T):
                dve.wait_ge(sem["hc_hi"], T.now2)
                after(dve, sem["hc_lo"], T.was2)
                V.tensor_scalar(hc[:], bank[3][:], bn_shift[:, 0:1], 0.0, ALU.add, ALU.max
                                ).then_inc(sem["hc"], 1)

            def nmp_low(T):
                dve.wait_ge(sem["xn_hi"], T.now2)
                after(dve, sem["z_gate_ps"], T.was2)
                V.tensor_tensor(xn_lo[:], bank[5][:], xn_hi[:].bitcast(F32), ALU.subtract
                                ).then_inc(sem["xn_lo"], 1)

            def conv_residual(T):
                dve.wait_ge(sem["c2_ps"], T.now2)
                dve.wait_ge(sem["x1"], T.now2)
                after(dve, sem["xc_hi"], T.was2)
                V.tensor_tensor(c2_res[:], bank[2][:], x1[:], ALU.add).then_inc(sem["c2_res"], 1)
                dve.wait_ge(sem["c2_res"], T.now2)
                after(dve, sem["xc_lo"], T.was2)
                V.tensor_scalar(xc[:], c2_res[:], bn_shift[:, 1:2], 0.0, ALU.add, ALU.max
                                ).then_inc(sem["xc"], 1)

            def conv_low(T):
                dve.wait_ge(sem["xc"], T.now2)
                dve.wait_ge(sem["xc_hi"], T.now2)
                after(dve, sem["z_gate_ps"], T.was2)
                V.tensor_tensor(xc_lo[:], xc[:], xc_hi[:].bitcast(F32), ALU.subtract
                                ).then_inc(sem["xc_lo"], 1)

            def gate_n(T):
                dve.wait_ge(sem["tr"], T.now2)
                dve.wait_ge(sem["ghn"], T.now2)
                after(dve, sem["nn"], T.was2)
                V.scalar_tensor_tensor(out=u[:], in0=tr[:], scalar=1.0, in1=ghn[:], op0=ALU.add,
                                       op1=ALU.mult).then_inc(sem["u"], 1)
                dve.wait_ge(sem["u"], T.now2)
                dve.wait_ge(sem["n_gate_ps"], T.now2)
                V.tensor_tensor(v[:], bank[5][:], u[:], ALU.add).then_inc(sem["v"], 1)

            def residual1(T):
                dve.wait_ge(sem["nn"], T.now2)
                V.tensor_tensor(x_plus_n[:], x1[:], nn[:], ALU.add).then_inc(sem["x_plus_n"], 1)
                dve.wait_ge(sem["x_minus_n"], T.now2)
                dve.wait_ge(sem["tz"], T.now2)
                after(dve, sem["y1_ps"], T.was2)
                V.scalar_tensor_tensor(out=zq[:], in0=tz[:], scalar=1.0, in1=x_minus_n[:],
                                       op0=ALU.add, op1=ALU.mult).then_inc(sem["zq"], 1)
                dve.wait_ge(sem["zq"], T.now2)
                V.scalar_tensor_tensor(out=y1[:], in0=zq[:], scalar=0.5, in1=x_plus_n[:],
                                       op0=ALU.mult, op1=ALU.add).then_inc(sem["y1"], 1)

            def norm1(T):
                norm_stats(1, bank[2], sem["y1_ps"], sem["bn1"], sem["mv1"], sem["ve1"], T.now2, T.was2)

            def apply1(T):
                dve.wait_ge(sem["r1"], T.now2)
                after(dve, sem["x2_ps"], T.was2)
                after(dve, sem["y2"], T.was2)
                for g in range(G):
                    last = V.tensor_scalar(x2_rows[:, g, :], bank[2][:, g, :], mv[1][:, g, 0:1],
                                           rstd[1][:, g:g + 1], ALU.subtract, ALU.mult)
                last.then_inc(sem["x2_rows"], 1)

            def hop(T, k):
                hop_ps = (sem["hop1_ps"], sem["hop2_ps"], sem["hop3_ps"])[k - 1]
                to = (t2, t1, prop)[k - 1]
                dve.wait_ge(hop_ps, T.now3)
                dve.wait_ge((sem["w2h"], sem["w1h"], sem["w0h"])[k - 1], T.now3)
                after(dve, (sem["hop2_ps"], sem["hop3_ps"], sem["y2"])[k - 1], T.was3)
                dve.wait_ge(sem["row_inv"], T.twice3)
                for g in range(G):
                    last = V.scalar_tensor_tensor(
                        out=to[:, g, :], in0=bank[(6, 7, 6)[k - 1]][:, g, :],
                        scalar=row_inv[T.slot3][:, g:g + 1], in1=wh[3 - k][:, g, :], op0=ALU.mult,
                        op1=ALU.add)
                last.then_inc((sem["t2"], sem["t1"], sem["prop"])[k - 1], 1)

            def leaky_relu(T):
                dve.wait_ge(sem["prop"], T.now3)
                V.scalar_tensor_tensor(out=leaky[:], in0=prop[:], scalar=LEAKY_SLOPE, in1=prop[:],
                                       op0=ALU.mult, op1=ALU.max).then_inc(sem["leaky"], 1)

            def norm2(T):
                norm_stats(2, y2, sem["y2"], sem["bn2"], sem["mv2"], sem["ve2"], T.now3, T.was3)

            def a_t3(T):
                dve.wait_ge(sem["at"], T.now3)
                after(dve, sem["agg3_ps"], T.was3)
                V.scalar_tensor_tensor(out=at3, in0=over_graphs(ident), scalar=one_eps3[:],
                                       in1=at[T.slot3][:], op0=ALU.mult, op1=ALU.add).then_inc(sem["at3"], 1)

            def agg3(T):
                dve.wait_ge(sem["agg3_hi"], T.now3)
                after(dve, sem["z_ps1"], T.was3)
                V.tensor_tensor(agg3_lo[:], bank[7][:], agg3_hi[:].bitcast(F32), ALU.subtract
                                ).then_inc(sem["agg3_lo"], 1)

            def residual3(T):
                dve.wait_ge(sem["y3_ps"], T.now3)
                dve.wait_ge(sem["x3b"], T.now3)
                after(dve, sem["out_rows"], T.was3)
                V.tensor_tensor(y3, bank[6][:], x3b, ALU.add).then_inc(sem["y3"], 1)
                norm_stats(3, y3, sem["y3"], sem["bn3"], sem["mv3"], sem["ve3"], T.now3, T.was3)

            def turn(T):
                one, two, three = (k in T.stages for k in (1, 2, 3))
                T.loads = loads_of(T, dve)
                if isinstance(T.t, int):
                    T.twice1, T.twice3 = 2 * (T.t + 2) + 1, 2 * T.t + 2
                else:
                    T.twice1, T.twice3 = dve.snap(2 * T.t + 5), dve.snap(2 * T.t + 2)
                if one: a_t_eps(T)
                if two: x1_low(T)
                if one: agg(T)
                if two: message_bias(T); points(T); conv1_full(T)
                if three: a_t3(T); hop(T, 1); hop(T, 2); hop(T, 3); leaky_relu(T)
                if two: nmp_low(T)
                if one: row_sums(T)
                if three: norm2(T)
                if one: sum_squares(T); mean_square(T)
                if three: agg3(T)
                if one: normalise(T, 0); normalise(T, 1); silu(T, 0)
                if two: conv_residual(T); conv_low(T)
                if one: normalise(T, 2); silu(T, 1); normalise(T, 3); silu(T, 2); silu(T, 3)
                if two: gate_n(T)
                if one: residual0(T)
                if two: residual1(T)
                if three: residual3(T)
                if two: norm1(T); apply1(T)

            done = 0

            def step(instruction):
                nonlocal done
                instruction.then_inc(set_dve, 1)
                done += 1

            dve.wait_ge(weights_in, ALL_WEIGHTS)
            dve.wait_ge(set_act, 1)
            step(V.tensor_scalar(bn_ve[:], bn_v, BN_EPS, None, ALU.add))
            assert done == BN_VE
            dve.wait_ge(set_pool, BN_POW)
            step(V.tensor_tensor(bn_scale[:], bn_g, bn_r[:], ALU.mult))
            dve.wait_ge(set_dve, done)
            step(V.tensor_tensor(bn_ms[:], bn_m, bn_scale[:], ALU.mult))
            dve.wait_ge(set_dve, done)
            step(V.tensor_tensor(bn_shift[:], bn_b, bn_ms[:], ALU.subtract))
            step(V.tensor_scalar(conv1_w[:], conv1_w[:], bn_scale[:, 0:1], None, ALU.mult))
            step(V.tensor_scalar(conv2_w, conv2_w, bn_scale[:, 1:2], None, ALU.mult))
            assert done == CONV_SCALED
            step(V.tensor_scalar(half_rms[:], rms_col, 0.5, None, ALU.mult))
            dve.wait_ge(set_dve, done)
            for c in range(H0):
                step(V.tensor_scalar(w2[:, c, :], w2[:, c, :], half_rms[:, c:c + 1], None, ALU.mult))
            step(V.tensor_tensor(gate_b[:], gate_bi[:, 0:2], gate_bh[:, 0:2], ALU.add))
            dve.wait_ge(set_dve, done)
            step(V.tensor_scalar(half_gate_b[:], gate_b[:], 0.5, None, ALU.mult))
            step(V.tensor_scalar(half_bhn[:], gate_bh[:, 2:3], 0.5, None, ALU.mult))
            step(V.tensor_scalar(one_eps3[:], eps3[:], 1.0, None, ALU.add))
            step(V.memset(pts_l[CODE_ROWS[2]:CODE_ROWS[2] + CODES], 1.0))
            step(V.memset(pts_r[CODE_ROWS[1]:CODE_ROWS[1] + CODES], 1.0))
            assert done == DVE_SMALL
            dve.wait_ge(set_act, 3)
            step(V.tensor_tensor(w1_lo[:], w1f[:], w1_hi[:].bitcast(F32), ALU.subtract))
            step(V.tensor_tensor(w31_lo[:], w31f[:], w31_hi[:].bitcast(F32), ALU.subtract))
            for b in range(WT_BANKS):
                n = min(G, NT - b * G)
                dve.wait_ge(set_act, SPLIT_ACT if b == WT_BANKS - 1 else 3 + b + 1)
                step(V.tensor_tensor(wt_lo[:, b * G:b * G + n, :], bank[b][:, 0:n, :],
                                     wt_hi[:, b * G:b * G + n, :].bitcast(F32), ALU.subtract))
            assert done == SPLIT_DVE
            dve.wait_ge(set_dve, done)
            dve.wait_ge(set_pool, BN_POW)
            dve.wait_ge(codes_in, ALL_CODES)
            run_turns(dve, turn, GROUPS)

        @block.gpsimd
        def _(pool):
            Q = nc.gpsimd

            def power(k, ready, done, count, was, base, to):
                pool.wait_ge(ready, count)
                Q.tensor_tensor(to[:], base[:], minus_half[:], ALU.pow).then_inc(done, 1)

            def apply(k, y, to, r_done, done, count):
                pool.wait_ge(r_done, count)
                for g in range(G):
                    last = Q.tensor_scalar(to[:, g, :], y[:, g, :], mv[k][:, g, 0:1],
                                           rstd[k][:, g:g + 1], ALU.subtract, ALU.mult)
                last.then_inc(done, 1)

            def x_bias(T):
                pool.wait_ge(x_in[T.slot1], T.loads)
                after(pool, sem["y0"], T.was1)
                Q.tensor_tensor(xb[:], x_rows[T.slot1][:], over_graphs(b2_row), ALU.add).then_inc(sem["xb"], 1)

            def add_squares(T):
                pool.wait_ge(sem["sq0"], T.now1)
                pool.wait_ge(sem["sq1"], T.now1)
                Q.tensor_tensor(sq01[:], sq[0][:], sq[1][:], ALU.add).then_inc(sem["sq01"], 1)
                pool.wait_ge(sem["sq2"], T.now1)
                pool.wait_ge(sem["sq3"], T.now1)
                Q.tensor_tensor(sq23[:], sq[2][:], sq[3][:], ALU.add).then_inc(sem["sq23"], 1)

            def rms(T):
                power(0, sem["ms"], sem["r_rms"], T.now1, T.was1, ms, r_rms)

            def norm0(T):
                power(0, sem["ve0"], sem["r0"], T.now1, T.was1, ve[0], rstd[0])
                pool.wait_ge(set_pool, BN_POW)
                after(pool, sem["x1_ps"], T.was1)
                apply(0, y0, x1_rows, sem["r0"], sem["x1_rows"], T.now1)

            def edge_weights(T):
                pool.wait_ge(sem["edge"], T.now2)
                pool.wait_ge(sem["at"], T.now2)
                after(pool, sem["nmp_ps"], T.was2)
                Q.tensor_tensor(edge_adj[:], edge[:], at[T.slot2][:], ALU.mult).then_inc(sem["edge_adj"], 1)

            def conv1_low(T):
                pool.wait_ge(sem["hc"], T.now2)
                pool.wait_ge(sem["hc_hi"], T.now2)
                after(pool, sem["c2_ps"], T.was2)
                Q.tensor_tensor(hc_lo[:, :, PAD:PAD + N], hc[:], hc_hi[:, :, PAD:PAD + N].bitcast(F32),
                                ALU.subtract).then_inc(sem["hc_lo"], 1)

            def minus(T):
                pool.wait_ge(sem["nn"], T.now2)
                after(pool, sem["zq"], T.was2)
                Q.tensor_tensor(x_minus_n[:], x1[:], nn[:], ALU.subtract).then_inc(sem["x_minus_n"], 1)

            def norm1(T):
                power(1, sem["ve1"], sem["r1"], T.now2, T.was2, ve[1], rstd[1])

            def residual2(T):
                pool.wait_ge(sem["leaky"], T.now3)
                after(pool, sem["x3_rows"], T.was3)
                Q.tensor_tensor(y2, leaky[:], x2_rows[:], ALU.add).then_inc(sem["y2"], 1)

            def norm2(T):
                power(2, sem["ve2"], sem["r2"], T.now3, T.was3, ve[2], rstd[2])
                pool.wait_ge(set_pool, BN_POW)
                after(pool, sem["agg3_ps"], T.was3)
                apply(2, y2, x3_rows, sem["r2"], sem["x3_rows"], T.now3)
                pool.wait_ge(sem["x3_rows"], T.now3)
                after(pool, sem["y3"], T.was3)
                Q.tensor_tensor(x3b, x3_rows, over_graphs(b32_row), ALU.add).then_inc(sem["x3b"], 1)

            def norm3(T):
                power(3, sem["ve3"], sem["r3"], T.now3, T.was3, ve[3], rstd[3])
                pool.wait_ge(set_pool, BN_POW)
                after(pool, stored[T.slot3], T.stores)
                apply(3, y3, out_rows[T.slot3], sem["r3"], sem["out_rows"], T.now3)

            def turn(T):
                one, two, three = (k in T.stages for k in (1, 2, 3))
                T.loads = loads_of(T, pool)
                if isinstance(T.t, int):
                    T.stores = 16 * (T.t // 2)
                else:
                    T.stores = pool.snap(8 * (T.t - T.slot3))
                if two: conv1_low(T); edge_weights(T)
                if three: residual2(T)
                if one: x_bias(T)
                if three: norm2(T)
                if one: add_squares(T); rms(T)
                if one and not two: norm0(T)
                if two: minus(T)
                if one and two: norm0(T)
                if three: norm3(T)
                if two: norm1(T)

            Q.memset(codes_w[:], 0.0).then_inc(cleared, 1)
            Q.memset(ident[:], 0.0).then_inc(set_pool, 1)
            pool.wait_ge(set_pool, 1)
            Q.affine_select(out=ident[:], in_=ident[:], compare_op=ALU.not_equal, fill=1.0, base=0,
                            pattern=[[-1, P]], channel_multiplier=1).then_inc(set_pool, 1)
            Q.memset(ones[:], 1.0)
            Q.memset(minus_half[:], -0.5)
            Q.memset(pts_l[:], 0.0)
            Q.memset(pts_r[:], 0.0)
            for tile in (hc_hi, hc_lo):
                Q.memset(tile[:, :, 0:PAD].bitcast(F32), 0.0)
                last = Q.memset(tile[:, :, PAD + N:NP].bitcast(F32), 0.0)
            last.then_inc(set_pool, 1)
            pool.wait_ge(set_dve, BN_VE)
            pool.wait_ge(set_pool, IDENT_SET)
            Q.tensor_tensor(bn_r[:], bn_ve[:], minus_half[:, 0:2], ALU.pow).then_inc(set_pool, 1)
            pool.wait_ge(weights_in, ALL_WEIGHTS)
            run_turns(pool, turn, GROUPS)


_INS = ['x', 'adj', 'L0_gnn_epsilon', 'L0_gnn_W1', 'L0_gnn_b1', 'L0_gnn_rms_weight', 'L0_gnn_W2',
        'L0_gnn_b2', 'L1_gnn_w_se', 'L1_gnn_b_se', 'L1_gnn_conv1_w', 'L1_gnn_bn1_g', 'L1_gnn_bn1_b',
        'L1_gnn_bn1_m', 'L1_gnn_bn1_v', 'L1_gnn_conv2_w', 'L1_gnn_bn2_g', 'L1_gnn_bn2_b',
        'L1_gnn_bn2_m', 'L1_gnn_bn2_v', 'L1_gnn_w_msg', 'L1_gnn_b_msg', 'L1_gnn_w_ih',
        'L1_gnn_b_ih', 'L1_gnn_w_hh', 'L1_gnn_b_hh', 'L2_gnn_W', 'L2_gnn_conv_w', 'L2_gnn_conv_b',
        'L3_gnn_eps', 'L3_gnn_W1', 'L3_gnn_b1', 'L3_gnn_W2', 'L3_gnn_b2']


def kernel(**inputs):
    import numpy as np
    import concourse.bacc as bacc
    from concourse.bass_utils import run_bass_kernel_spmd

    nc = bacc.Bacc("TRN2", target_bir_lowering=False, num_devices=1)
    arrays, args = {}, {}
    for name in _INS:
        a = np.ascontiguousarray(inputs[name])
        if name == 'L0_gnn_epsilon':
            a = a.reshape(1, 1)
        arrays[f"in_{name}"] = a
        args[name] = nc.dram_tensor(f"in_{name}", a.shape, mybir.dt.from_np(a.dtype),
                                    kind="ExternalInput").ap()
    out = nc.dram_tensor("out", inputs['x'].shape, F32, kind="ExternalOutput").ap()
    graph_layers(nc, args.pop('x'), args.pop('adj'), out, args)
    result = run_bass_kernel_spmd(nc, [arrays], core_ids=[0])
    return result.results[0]["out"]
```

```python
from contextlib import ExitStack

import concourse.bass as bass
from concourse import mybir

F32 = mybir.dt.float32
F32R = mybir.dt.float32r
ALU = mybir.AluOpType
ACT = mybir.ActivationFunctionType
AX_X = mybir.AxisListType.X

P = 128
LN_EPS = 1e-5
RMS_EPS = 1e-6
BN_EPS = 1e-5
ROW_SUM_EPS = 1e-9
LEAKY_SLOPE = 0.2

STEPS = """
adj_t_ps at_eps at row_inv nb_ps agg_hi agg_lo h_ps0 h_ps1 h_ps2 h_ps3 h0 h1 h2 h3 sq0 sq1 sq2 sq3
sq01 sq23 sq_sum sq_ps ms r_rms r_ps hn0 hn1 hn2 hn3 th0 th1 th2 th3 s0 s1 s2 s3 row_sum
xb y0_ps y0 bn0 mv0 ve0 r0 x1_rows
x1_ps x1 x1_hi x1_lo msg_ps msg_pre msg pts_ps pts_r0 pts_l1 pts_r2 pts_l0 c1_ps hc_hi hc hc_lo
ghn_ps ghn dist_ps edge edge_adj nmp_ps xn_hi xn_lo c2_ps c2_res xc_hi xc xc_lo
r_gate_ps z_gate_ps n_gate_ps tr tz u v nn x_minus_n x_plus_n zq y1
at_now y1_ps bn1 mv1 ve1 r1 x2_rows x2_ps x2 ht_ps w3h w2h w1h w0h hop1_ps t2 hop2_ps t1 hop3_ps prop leaky y2 bn2 mv2 ve2 r2 x3_rows
x3b at3 agg3_ps agg3_hi agg3_lo z_ps0 z_ps1 z0 z1 y3_ps y3 bn3 mv3 ve3 r3 out_rows
""".split()


def after(engine, semaphore, count):
    if isinstance(count, int) and count <= 0:
        return
    engine.wait_ge(semaphore, count)


class Turn:

    def __init__(self, t, parity, stages, engine=None):
        at = [t + k for k in range(4)]
        if engine is not None:
            at = [engine.snap(a) for a in at]
        self.t, self.stages = t, stages
        self.now1, self.was1, self.old1 = at[3], at[2], at[1]
        self.now2, self.was2, self.old2 = at[2], at[1], at[0]
        self.now3, self.was3 = at[1], at[0]
        self.slot1, self.slot2, self.slot3 = parity, 1 - parity, parity


def run_turns(engine, turn, groups):
    turn(Turn(-1, 1, (1, 2)))
    turn(Turn(0, 0, (1, 2, 3)))
    turn(Turn(1, 1, (1, 2, 3)))
    with engine.Fori(2, groups - 2, 2) as t:
        turn(Turn(t, 0, (1, 2, 3), engine))
        turn(Turn(t + 1, 1, (1, 2, 3), engine))
    turn(Turn(groups - 2, 0, (2, 3)))
    turn(Turn(groups - 1, 1, (3,)))


def graph_layers(nc, x, adj, out, w):
    B, N, D = x.shape
    G = 4
    GROUPS = B // G
    W = G * N
    assert N == P and D == P and GROUPS % 2 == 0
    H0 = w["L0_gnn_W1"].shape[1] // P
    H3 = w["L3_gnn_W1"].shape[1] // P
    TAPS = w["L1_gnn_conv2_w"].shape[2]
    PAD = TAPS // 2
    NP = N + 2 * PAD
    CODES = w["L1_gnn_w_se"].shape[0]

    CONV2, CONV1, SE = 0, TAPS, TAPS + 1
    IH = TAPS + 2
    HH = IH + 6
    MSG = HH + 3
    R_GATE, Z_GATE, N_GATE = range(3)
    PROP = MSG + 1
    NT = PROP + 1
    assert NT < 8 * G

    with ExitStack() as ctx:
        def sb(name, shape, dt=F32):
            return ctx.enter_context(nc.sbuf_tensor(name, shape, dt))

        def rows(name, dt=F32):
            return sb(name, [P, G, P], dt)

        bank = [ctx.enter_context(nc.psum_tensor(f"bank{i}", [P, G, P], F32)) for i in range(8)]
        sem = {n: ctx.enter_context(nc.semaphore(n)) for n in STEPS}
        x_in = [ctx.enter_context(nc.semaphore(f"x_in{i}")) for i in range(2)]
        adj_in = [ctx.enter_context(nc.semaphore(f"adj_in{i}")) for i in range(2)]
        stored = [ctx.enter_context(nc.semaphore(f"stored{i}")) for i in range(2)]
        vectors_in = ctx.enter_context(nc.semaphore("vectors_in"))
        eps0_in = ctx.enter_context(nc.semaphore("eps0_in"))
        w1_in = ctx.enter_context(nc.semaphore("w1_in"))
        layer0_in = ctx.enter_context(nc.semaphore("layer0_in"))
        weights_in = ctx.enter_context(nc.semaphore("weights_in"))
        codes_in = ctx.enter_context(nc.semaphore("codes_in"))
        cleared = ctx.enter_context(nc.semaphore("cleared"))
        set_pool = ctx.enter_context(nc.semaphore("set_pool"))
        set_dve = ctx.enter_context(nc.semaphore("set_dve"))
        set_pe = ctx.enter_context(nc.semaphore("set_pe"))
        set_act = ctx.enter_context(nc.semaphore("set_act"))

        ident = sb("ident", [P, P])
        ones = sb("ones", [P, P])
        minus_half = sb("minus_half", [P, G])
        w1f = sb("w1f", [P, H0 * P])
        w1_hi = sb("w1_hi", [P, H0 * P], F32R)
        w1_lo = sb("w1_lo", [P, H0 * P], F32R)
        w2 = sb("w2", [P, H0, D])
        w31f = sb("w31f", [P, H3 * P])
        w31_hi = sb("w31_hi", [P, H3 * P], F32R)
        w31_lo = sb("w31_lo", [P, H3 * P], F32R)
        w32 = sb("w32", [P, H3, D])
        arena = sb("arena", [P, 5, G, P])
        assert P * TAPS <= 5 * G * P
        conv2_w = arena[:].rearrange("p a g n -> p (a g n)")[:, 0:P * TAPS].rearrange(
            "p (i k) -> p i k", k=TAPS)
        conv1_w = sb("conv1_w", [P, P])
        codes_w = sb("codes_w", [P, P])
        msg_w = sb("msg_w", [P, P])
        ih_w = sb("ih_w", [P, 3, 2, P])
        hh_w = sb("hh_w", [P, 3, P])
        prop_w = sb("prop_w", [P, P])
        wt_hi = sb("wt_hi", [P, NT, P], F32R)
        wt_lo = sb("wt_lo", [P, NT, P], F32R)
        wt_full = sb("wt_full", [P, 2, P])
        vectors = [("b1", w["L0_gnn_b1"], H0), ("rms", w["L0_gnn_rms_weight"], H0), ("g1", w["L1_gnn_bn1_g"], 1),
                   ("g2", w["L1_gnn_bn2_g"], 1), ("b1n", w["L1_gnn_bn1_b"], 1), ("b2n", w["L1_gnn_bn2_b"], 1),
                   ("m1", w["L1_gnn_bn1_m"], 1), ("m2", w["L1_gnn_bn2_m"], 1), ("v1", w["L1_gnn_bn1_v"], 1),
                   ("v2", w["L1_gnn_bn2_v"], 1), ("bi", w["L1_gnn_b_ih"], 3), ("bh", w["L1_gnn_b_hh"], 3),
                   ("b31", w["L3_gnn_b1"], H3)]
        first_row, VR = {}, 0
        for name, _, count in vectors:
            first_row[name] = VR
            VR += count
        vector_rows = sb("vector_rows", [VR, P])
        vector_cols = sb("vector_cols", [P, VR])

        def columns(name, count):
            return vector_cols[:, first_row[name]:first_row[name] + count]

        b1_col = columns("b1", H0)
        rms_col = columns("rms", H0)
        half_rms = sb("half_rms", [P, H0])
        b31_col = columns("b31", H3)
        codes_b = sb("codes_b", [P, 1])
        bn_g, bn_b, bn_m, bn_v = (columns(n, 2) for n in ("g1", "b1n", "m1", "v1"))
        bn_ve = sb("bn_ve", [P, 2])
        bn_r = sb("bn_r", [P, 2])
        bn_scale = sb("bn_scale", [P, 2])
        bn_ms = sb("bn_ms", [P, 2])
        bn_shift = sb("bn_shift", [P, 2])
        gate_bi = columns("bi", 3)
        gate_bh = columns("bh", 3)
        gate_b = sb("gate_b", [P, 2])
        half_gate_b = sb("half_gate_b", [P, 2])
        half_bhn = sb("half_bhn", [P, 1])
        b2_row = sb("b2_row", [P, D])
        msg_row = sb("msg_row", [P, D])
        b32_row = sb("b32_row", [P, D])
        eps0 = sb("eps0", [P, 1])
        eps3 = sb("eps3", [P, 1])
        one_eps3 = sb("one_eps3", [P, 1])
        prop_k = sb("prop_k", [P, 4])
        prop_b = sb("prop_b", [P, 1])

        x_rows = [rows(f"x_rows{i}") for i in range(2)]
        adj_rows = [rows(f"adj_rows{i}") for i in range(2)]
        at = [rows(f"at{i}") for i in range(2)]
        row_inv = [sb(f"row_inv{i}", [P, G]) for i in range(2)]
        row_sum = sb("row_sum", [P, G])
        row_sum_eps = sb("row_sum_eps", [P, G])
        at_now = w1f[:].rearrange("p (g n) -> p g n", g=G)
        at_eps = rows("at_eps")
        agg_hi, agg_lo = rows("agg_hi", F32R), rows("agg_lo", F32R)
        h = [rows(f"h{c}") for c in range(H0)]
        sq = [rows(f"sq{c}") for c in range(H0)]
        hn = [rows(f"hn{c}") for c in range(H0)]
        th = [rows(f"th{c}") for c in range(H0)]
        s = h
        sq01, sq23, sq_sum = sq[0], sq[2], sq[1]
        ms = sb("ms", [P, G])
        r_rms = sb("r_rms", [P, G])
        xb = rows("xb")
        y0 = rows("y0")
        x1_rows = rows("x1_rows")
        x1 = rows("x1")
        x1_hi, x1_lo = rows("x1_hi", F32R), rows("x1_lo", F32R)
        msg_pre, msg = rows("msg_pre"), rows("msg")
        pts_l, pts_r = rows("pts_l"), rows("pts_r")
        hc = rows("hc")
        hc_hi, hc_lo = sb("hc_hi", [P, G, NP], F32R), sb("hc_lo", [P, G, NP], F32R)
        ghn = rows("ghn")
        edge, edge_adj = rows("edge"), rows("edge_adj")
        xn_hi, xn_lo = rows("xn_hi", F32R), rows("xn_lo", F32R)
        c2_res, xc = rows("c2_res"), rows("xc")
        xc_hi, xc_lo = rows("xc_hi", F32R), rows("xc_lo", F32R)
        tr, tz, u, nn = rows("tr"), rows("tz"), rows("u"), rows("nn")
        v = u
        x_minus_n, x_plus_n, zq = rows("x_minus_n"), rows("x_plus_n"), rows("zq")
        y1 = zq
        x2_rows, x2 = rows("x2_rows"), rows("x2")
        wh = [rows(f"w{k}h") for k in range(4)]
        t2, t1, prop = rows("t2"), rows("t1"), rows("prop")
        leaky = prop
        y2, x3_rows, x3b, at3, y3 = (arena[:, i] for i in range(5))
        agg3_hi, agg3_lo = rows("agg3_hi", F32R), rows("agg3_lo", F32R)
        z3 = [rows(f"z3_{c}") for c in range(H3)]
        out_rows = [rows(f"out_rows{i}") for i in range(2)]
        stats = [sb(f"stats{i}", [P, G, 6]) for i in range(4)]
        mv = [sb(f"mv{i}", [P, G, 2]) for i in range(4)]
        ve = [sb(f"ve{i}", [P, G]) for i in range(4)]
        rstd = [sb(f"rstd{i}", [P, G]) for i in range(4)]

        def cols(tile):
            return tile[:].rearrange("p g n -> p (g n)")

        def over_graphs(tile):
            return tile[:].unsqueeze(1).to_broadcast([P, G, P])

        x_dram = x.rearrange("(k g) n d -> k n g d", g=G)
        adj_dram = adj.rearrange("(k g) n m -> k n g m", g=G)
        out_dram = out.rearrange("(k g) n d -> k n g d", g=G)

        def one_row(vector):
            n = vector.shape[0]
            return vector.rearrange("(a d) -> a d", a=1).to_broadcast([P, n])

        IDENT_SET = 2
        TILES_SET = 3
        BN_POW = 4
        WT_BANKS = -(-NT // G)
        W1_HIGH = 1
        VECTORS_ACT = 2
        HIGHS = 3
        SPLIT_ACT = HIGHS + WT_BANKS + 1
        W1_LOW = 1
        BN_VE = 2
        HALF_RMS = 3
        LAYER0_DVE = HALF_RMS + H0
        CONV_SCALED = LAYER0_DVE + 5
        LOWS = CONV_SCALED + 7
        SPLIT_DVE = LOWS + WT_BANKS

        def setup_bank(b):
            return bank[2 + b % (8 - 2)]

        def loads_of(T, engine):
            if isinstance(T.t, int):
                return 16 * ((T.t + 2) // 2 + 1)
            return engine.snap(8 * (T.t - T.slot1) + 32)

        block = ctx.enter_context(nc.Block())

        LAYER0_LOADS = [
            (b2_row[:], one_row(w["L0_gnn_b2"])),
            (w2[:], w["L0_gnn_W2"].rearrange("(c p) d -> p c d", p=P)),
        ]
        WEIGHT_LOADS = [
            (conv1_w[:], w["L1_gnn_conv1_w"].rearrange("o i k -> o (i k)")),
            (conv2_w, w["L1_gnn_conv2_w"]),
            (msg_w[:], w["L1_gnn_w_msg"]),
            (msg_row[:], one_row(w["L1_gnn_b_msg"])),
            (ih_w[:], w["L1_gnn_w_ih"].rearrange("(a o) (b i) -> o a b i", a=3, b=2)),
            (hh_w[:], w["L1_gnn_w_hh"].rearrange("(a o) i -> o a i", a=3)),
            (prop_w[:], w["L2_gnn_W"]),
            (prop_k[:], one_row(w["L2_gnn_conv_w"])),
            (prop_b[:], one_row(w["L2_gnn_conv_b"])),
            (eps3[:], one_row(w["L3_gnn_eps"])),
            (w31f[:], w["L3_gnn_W1"]),
            (w32[:], w["L3_gnn_W2"].rearrange("(c p) d -> p c d", p=P)),
            (b32_row[:], one_row(w["L3_gnn_b2"])),
        ]
        ALL_LAYER0 = 16 * len(LAYER0_LOADS)
        ALL_WEIGHTS = 16 * len(WEIGHT_LOADS)
        CODE_ROWS = (0, 32, 64)
        ALL_CODES = 16 * 2 * len(CODE_ROWS)

        @block.sync
        def _(sp):
            def load(group, slot, count):
                after(sp, sem["adj_t_ps"], count)
                after(sp, sem["row_sum"], count)
                sp.dma_start(adj_rows[slot][:], adj_dram[group]).then_inc(adj_in[slot], 16)
                after(sp, sem["nb_ps"], count)
                after(sp, sem["xb"], count)
                sp.dma_start(x_rows[slot][:], x_dram[group]).then_inc(x_in[slot], 16)

            def turn(T):
                if 1 in T.stages:
                    load(T.t + 3, 1 - T.slot1, T.was1)
                if 3 in T.stages:
                    sp.wait_ge(sem["out_rows"], T.now3)
                    sp.dma_start(out_dram[T.t], out_rows[T.slot3][:]).then_inc(stored[T.slot3], 16)

            sp.dma_start(eps0[:], w["L0_gnn_epsilon"].to_broadcast([P, 1])).then_inc(eps0_in, 16)
            load(0, 0, 0)
            sp.dma_start(w1f[:], w["L0_gnn_W1"]).then_inc(w1_in, 16)
            for name, vector, count in vectors:
                r = first_row[name]
                sp.dma_start(vector_rows[r:r + count, :], vector.rearrange("(a p) -> a p", a=count)
                             ).then_inc(vectors_in, 16)
            for tile, source in LAYER0_LOADS:
                sp.dma_start(tile, source).then_inc(layer0_in, 16)
            for tile, source in WEIGHT_LOADS:
                sp.dma_start(tile, source).then_inc(weights_in, 16)
            sp.wait_ge(cleared, 1)
            for at_row in CODE_ROWS:
                sp.dma_start(codes_w[at_row:at_row + CODES, :], w["L1_gnn_w_se"]).then_inc(codes_in, 16)
                sp.dma_start(codes_b[at_row:at_row + CODES, :], w["L1_gnn_b_se"].rearrange("(p a) -> p a", a=1)).then_inc(codes_in, 16)

            turn(Turn(-2, 0, (1,)))
            turn(Turn(-1, 1, (1, 2)))
            with sp.Fori(0, GROUPS - 4, 2) as t:
                turn(Turn(t, 0, (1, 2, 3), sp))
                turn(Turn(t + 1, 1, (1, 2, 3), sp))
            turn(Turn(GROUPS - 4, 0, (1, 2, 3)))
            for t in (GROUPS - 3, GROUPS - 2, GROUPS - 1):
                turn(Turn(t, t % 2, (3,)))
            for slot in range(2):
                sp.wait_ge(stored[slot], 16 * (GROUPS // 2))

        @block.tensor
        def _(pe):
            def split_product(psum, hi, lo, moving_hi, moving_lo, start, stop):
                pe.matmul(psum, hi, moving_hi, start=start, stop=False)
                pe.matmul(psum, hi, moving_lo, start=False, stop=False)
                return pe.matmul(psum, lo, moving_hi, start=False, stop=stop)

            def weight(k):
                return wt_hi[:, k, :], wt_lo[:, k, :]

            def transposes(psum, tile):
                for g in range(G):
                    last = pe.transpose(psum[:, g, :], tile[:, g, :], ident[:])
                return last

            def by_graph(psum, lhs, rhs):
                for g in range(G):
                    last = pe.matmul(psum[:, g, :], lhs(g), rhs(g), start=True, stop=True)
                return last

            def adj_t(T):
                pe.wait_ge(adj_in[T.slot1], T.loads)
                after(pe, sem["hn3"], T.was1)
                transposes(bank[0], adj_rows[T.slot1]).then_inc(sem["adj_t_ps"], 1)

            def neighbours(T):
                pe.wait_ge(x_in[T.slot1], T.loads)
                pe.wait_ge(sem["at_eps"], T.now1)
                after(pe, sem["y0"], T.was1)
                by_graph(bank[1], lambda g: x_rows[T.slot1][:, g, :],
                         lambda g: at_eps[:, g, :]).then_inc(sem["nb_ps"], 1)

            def hidden(T, c):
                if c == 0:
                    pe.wait_ge(sem["agg_hi"], T.now1)
                    pe.wait_ge(sem["agg_lo"], T.now1)
                if c == 1:
                    pe.wait_ge(sem["at"], T.now1)
                if c >= 2:
                    pe.wait_ge((sem["h0"], sem["h1"])[c - 2], T.now1)
                    pe.wait_ge((sem["sq0"], sem["sq1"])[c - 2], T.now1)
                split_product(bank[1 - c % 2][:].rearrange("p g n -> p (g n)"),
                              w1_hi[:, c * P:(c + 1) * P], w1_lo[:, c * P:(c + 1) * P],
                              cols(agg_hi), cols(agg_lo), True, True
                              ).then_inc((sem["h_ps0"], sem["h_ps1"], sem["h_ps2"], sem["h_ps3"])[c], 1)

            def square_sums(T):
                pe.wait_ge(sem["sq_sum"], T.now1)
                pe.wait_ge(sem["h2"], T.now1)
                by_graph(bank[1], lambda g: sq_sum[:, g, :], lambda g: ones[:]).then_inc(sem["sq_ps"], 1)

            def spread_rms(T):
                pe.wait_ge(sem["r_rms"], T.now1)
                pe.wait_ge(sem["h3"], T.now1)
                pe.wait_ge(sem["sq3"], T.now1)
                for g in range(G):
                    last = pe.transpose(bank[0][:, g, :], r_rms[:, g:g + 1].to_broadcast([P, P]), ident[:])
                last.then_inc(sem["r_ps"], 1)

            def down(T, c):
                pe.wait_ge((sem["s0"], sem["s1"], sem["s2"], sem["s3"])[c], T.now1)
                if c == 0:
                    pe.wait_ge(sem["ms"], T.now1)
                for g in range(G):
                    last = pe.matmul(bank[1][:, g, :], s[c][:, g, :], w2[:, c, :],
                                     start=(c == 0 and g == 0), stop=(c == H0 - 1),
                                     skip_group_check=True)
                if c == H0 - 1:
                    last.then_inc(sem["y0_ps"], 1)

            def x1_t(T):
                pe.wait_ge(sem["x1_rows"], T.now2)
                after(pe, sem["tr"], T.was2)
                transposes(bank[3], x1_rows).then_inc(sem["x1_ps"], 1)

            def messages(T):
                pe.wait_ge(sem["x1"], T.now2)
                after(pe, sem["tz"], T.was2)
                by_graph(bank[4], lambda g: x1[:, g, :], lambda g: wt_full[:, 0, :]).then_inc(sem["msg_ps"], 1)

            def codes(T):
                pe.wait_ge(sem["x1_lo"], T.now2)
                pe.wait_ge(sem["x1_hi"], T.now2)
                after(pe, sem["v"], T.was2)
                split_product(cols(bank[5]), *weight(SE), cols(x1_hi), cols(x1_lo), True, True
                              ).then_inc(sem["pts_ps"], 1)

            def conv1(T):
                pe.wait_ge(sem["x1_lo"], T.now2)
                pe.wait_ge(sem["x1"], T.now2)
                split_product(cols(bank[3]), *weight(CONV1), cols(x1_hi), cols(x1_lo), True, True
                              ).then_inc(sem["c1_ps"], 1)

            def hidden_n(T):
                pe.wait_ge(sem["x1_hi"], T.now2)
                pe.wait_ge(sem["x1_lo"], T.now2)
                after(pe, sem["c2_res"], T.was2)
                split_product(cols(bank[2]), *weight(HH + 2), cols(x1_hi), cols(x1_lo), True, True
                              ).then_inc(sem["ghn_ps"], 1)

            def distances(T):
                pe.wait_ge(sem["pts_l0"], T.now2)
                pe.wait_ge(sem["pts_r0"], T.now2)
                pe.wait_ge(sem["pts_l1"], T.now2)
                pe.wait_ge(sem["pts_r2"], T.now2)
                pe.wait_ge(sem["msg_pre"], T.now2)
                K = CODE_ROWS[2] + CODES
                by_graph(bank[4], lambda g: pts_l[0:K, g, :], lambda g: pts_r[0:K, g, :]
                         ).then_inc(sem["dist_ps"], 1)

            def conv2(T, first, end):
                if first == 0:
                    pe.wait_ge(sem["hc_lo"], T.now2)
                    pe.wait_ge(sem["hc_hi"], T.now2)
                    pe.wait_ge(sem["ghn"], T.now2)
                for k in range(first, end):
                    last = split_product(bank[2][:], *weight(CONV2 + k), hc_hi[:, :, k:k + N],
                                         hc_lo[:, :, k:k + N], k == 0, k == TAPS - 1)
                if end == TAPS:
                    last.then_inc(sem["c2_ps"], 1)

            def gather(T):
                pe.wait_ge(sem["msg"], T.now2)
                pe.wait_ge(sem["edge_adj"], T.now2)
                pe.wait_ge(sem["pts_l0"], T.now2)
                pe.wait_ge(sem["pts_r2"], T.now2)
                by_graph(bank[5], lambda g: msg[:, g, :], lambda g: edge_adj[:, g, :]).then_inc(sem["nmp_ps"], 1)

            def gate_x(T, gate):
                if gate == R_GATE:
                    pe.wait_ge(sem["hc_hi"], T.now2)
                    pe.wait_ge(sem["hc"], T.now2)
                if gate == Z_GATE:
                    pe.wait_ge(sem["edge"], T.now2)
                split_product(cols(bank[3 + gate]), *weight(HH + gate), cols(x1_hi), cols(x1_lo),
                              True, False)

            def gate_nmp(T, gate):
                pe.wait_ge(sem["xn_hi"], T.now2)
                pe.wait_ge(sem["xn_lo"], T.now2)
                split_product(cols(bank[3 + gate]), *weight(IH + 2 * gate + 1), cols(xn_hi),
                              cols(xn_lo), gate == N_GATE, False)

            def gate_conv(T, gate):
                pe.wait_ge(sem["xc_hi"], T.now2)
                pe.wait_ge(sem["xc_lo"], T.now2)
                split_product(cols(bank[3 + gate]), *weight(IH + 2 * gate), cols(xc_hi), cols(xc_lo),
                              False, True
                              ).then_inc(sem[("r_gate_ps", "z_gate_ps", "n_gate_ps")[gate]], 1)

            def y1_t(T):
                pe.wait_ge(sem["y1"], T.now3)
                after(pe, sem["z1"], T.was3)
                transposes(bank[6], y1).then_inc(sem["y1_ps"], 1)

            def x2_t(T):
                pe.wait_ge(sem["x2_rows"], T.now3)
                after(pe, sem["y3"], T.was3)
                transposes(bank[7], x2_rows).then_inc(sem["x2_ps"], 1)

            def prop_in(T):
                pe.wait_ge(sem["x2"], T.now3)
                pe.wait_ge(sem["x2_rows"], T.now3)
                by_graph(bank[6], lambda g: x2[:, g, :], lambda g: wt_full[:, 1, :]).then_inc(sem["ht_ps"], 1)

            def hop(T, k):
                if k == 1:
                    pe.wait_ge(sem["w3h"], T.now3)
                    pe.wait_ge(sem["at_now"], T.now3)
                if k == 2:
                    pe.wait_ge(sem["t2"], T.now3)
                    for k_h in range(3):
                        pe.wait_ge(sem[("w0h", "w1h", "w2h")[k_h]], T.now3)
                if k == 3:
                    pe.wait_ge(sem["t1"], T.now3)
                moving = (wh[3], t2, t1)[k - 1]
                by_graph(bank[(7, 6, 7)[k - 1]], lambda g: at_now[:, g, :], lambda g: moving[:, g, :]
                         ).then_inc((sem["hop1_ps"], sem["hop2_ps"], sem["hop3_ps"])[k - 1], 1)

            def gather3(T):
                pe.wait_ge(sem["x3_rows"], T.now3)
                pe.wait_ge(sem["at3"], T.now3)
                by_graph(bank[6], lambda g: x3_rows[:, g, :], lambda g: at3[:, g, :]).then_inc(sem["agg3_ps"], 1)

            def hidden3(T, c):
                if c == 0:
                    pe.wait_ge(sem["agg3_hi"], T.now3)
                    pe.wait_ge(sem["agg3_lo"], T.now3)
                    pe.wait_ge(sem["prop"], T.now3)
                split_product(cols(bank[7 - c]), w31_hi[:, c * P:(c + 1) * P], w31_lo[:, c * P:(c + 1) * P],
                              cols(agg3_hi), cols(agg3_lo), True, True
                              ).then_inc((sem["z_ps0"], sem["z_ps1"])[c], 1)

            def down3(T):
                pe.wait_ge(sem["z0"], T.now3)
                for c in range(H3):
                    if c == 1:
                        pe.wait_ge(sem["z1"], T.now3)
                    for g in range(G):
                        last = pe.matmul(bank[7][:, g, :], z3[c][:, g, :], w32[:, c, :],
                                         start=(c == 0 and g == 0), stop=(c == H3 - 1),
                                         skip_group_check=True)
                last.then_inc(sem["y3_ps"], 1)

            def turn(T):
                one, two, three = (k in T.stages for k in (1, 2, 3))
                T.loads = loads_of(T, pe)
                if two: x1_t(T)
                if one: adj_t(T)
                if two: messages(T)
                if three: y1_t(T)
                if two: codes(T)
                if one: neighbours(T)
                if two: hidden_n(T); conv1(T); distances(T)
                if one: hidden(T, 0); hidden(T, 1)
                if three: x2_t(T)
                if two: gate_x(T, R_GATE)
                if one: hidden(T, 2)
                if three: prop_in(T)
                if two: conv2(T, 0, 2)
                if three: hop(T, 1)
                if one: hidden(T, 3)
                if two: conv2(T, 2, 4)
                if three: hop(T, 2)
                if two: conv2(T, 4, 7)
                if three: hop(T, 3)
                if one: square_sums(T)
                if two: gather(T); conv2(T, 7, 9)
                if one: spread_rms(T)
                if two: conv2(T, 9, 13); gate_nmp(T, R_GATE); conv2(T, 13, TAPS)
                if three: gather3(T)
                if one: down(T, 0); down(T, 1); down(T, 2); down(T, 3)
                if three: hidden3(T, 0)
                if two: gate_conv(T, R_GATE); gate_nmp(T, N_GATE)
                if three: hidden3(T, 1)
                if two: gate_conv(T, N_GATE)
                if three: down3(T)
                if two: gate_x(T, Z_GATE); gate_nmp(T, Z_GATE); gate_conv(T, Z_GATE)

            def transposed_weights(first, end):
                for b in range(first, end):
                    if b == 0:
                        pe.wait_ge(weights_in, ALL_WEIGHTS)
                        pe.wait_ge(codes_in, ALL_CODES)
                        pe.wait_ge(set_dve, CONV_SCALED)
                    if b >= 6:
                        pe.wait_ge(set_act, HIGHS + b - 6 + 1)
                        pe.wait_ge(set_dve, LOWS + b - 6 + 1)
                    for k in range(b * G, min(NT, (b + 1) * G)):
                        last = pe.transpose(setup_bank(b)[:, k % G, :], sources[k], ident[:])
                    last.then_inc(set_pe, 1)

            sources = [conv2_w[:, :, k] for k in range(TAPS)] + [conv1_w[:], codes_w[:]]
            sources += [ih_w[:, a, b, :] for a in range(3) for b in range(2)]
            sources += [hh_w[:, a, :] for a in range(3)] + [msg_w[:], prop_w[:]]
            T = Turn(-2, 0, (1,))
            T.loads = loads_of(T, pe)
            pe.wait_ge(set_pool, IDENT_SET)
            adj_t(T)
            neighbours(T)
            pe.wait_ge(vectors_in, 16 * len(vectors))
            pe.transpose(bank[7][:, G - 1, 0:VR], vector_rows[:], ident[0:VR, 0:VR]).then_inc(set_pe, 1)
            pe.wait_ge(set_act, VECTORS_ACT)
            pe.wait_ge(set_dve, W1_LOW)
            hidden(T, 0); hidden(T, 1); hidden(T, 2); hidden(T, 3)
            pe.wait_ge(set_pool, TILES_SET)
            square_sums(T); spread_rms(T)
            transposed_weights(0, 6)
            pe.wait_ge(set_dve, LAYER0_DVE)
            down(T, 0); down(T, 1); down(T, 2); down(T, 3)
            transposed_weights(6, WT_BANKS)
            pe.wait_ge(set_act, SPLIT_ACT)
            pe.wait_ge(set_dve, SPLIT_DVE)
            run_turns(pe, turn, GROUPS)

        @block.scalar
        def _(act):
            def copy(out, in_):
                return nc.scalar.activation(out, in_, ACT.Copy)

            def a_t(T):
                pe_at = at[T.slot1]
                act.wait_ge(sem["adj_t_ps"], T.now1)
                after(act, sem["at_now"], T.old1)
                after(act, sem["edge_adj"], T.old1)
                act.wait_ge(sem["at_eps"], T.now1)
                copy(pe_at[:], bank[0][:]).then_inc(sem["at"], 1)

            def agg(T):
                act.wait_ge(sem["nb_ps"], T.now1)
                after(act, sem["h_ps3"], T.was1)
                copy(agg_hi[:], bank[1][:]).then_inc(sem["agg_hi"], 1)

            def hidden(T, c):
                act.wait_ge((sem["h_ps0"], sem["h_ps1"], sem["h_ps2"], sem["h_ps3"])[c], T.now1)
                after(act, (sem["sq01"], sem["sq_sum"], sem["sq23"], sem["sq_sum"])[c], T.was1)
                after(act, sem["sq_ps"], T.was1)
                nc.scalar.activation(sq[c][:], bank[1 - c % 2][:], ACT.Square, bias=b1_col[:, c:c + 1]
                                     ).then_inc((sem["sq0"], sem["sq1"], sem["sq2"], sem["sq3"])[c], 1)
                after(act, sem["y0_ps"], T.was1)
                nc.scalar.activation(h[c][:], bank[1 - c % 2][:], ACT.Identity, bias=b1_col[:, c:c + 1]
                                     ).then_inc((sem["h0"], sem["h1"], sem["h2"], sem["h3"])[c], 1)

            def tanh0(T, c):
                act.wait_ge((sem["hn0"], sem["hn1"], sem["hn2"], sem["hn3"])[c], T.now1)
                after(act, (sem["s0"], sem["s1"], sem["s2"], sem["s3"])[c], T.was1)
                nc.scalar.activation(th[c][:], hn[c][:], ACT.Tanh, scale=half_rms[:, c:c + 1]
                                     ).then_inc((sem["th0"], sem["th1"], sem["th2"], sem["th3"])[c], 1)

            def x1_parts(T):
                act.wait_ge(sem["x1_ps"], T.now2)
                after(act, sem["z_gate_ps"], T.was2)
                copy(x1_hi[:], bank[3][:]).then_inc(sem["x1_hi"], 1)
                after(act, sem["x_plus_n"], T.was2)
                after(act, sem["x_minus_n"], T.was2)
                copy(x1[:], bank[3][:]).then_inc(sem["x1"], 1)

            def points(T):
                act.wait_ge(sem["pts_ps"], T.now2)
                after(act, sem["dist_ps"], T.was2)
                r0, r1, r2 = (slice(a, a + CODES) for a in CODE_ROWS)
                nc.scalar.activation(pts_r[r0], bank[5][r0], ACT.Identity, bias=codes_b[r0]
                                     ).then_inc(sem["pts_r0"], 1)
                nc.scalar.activation(pts_l[r1], bank[5][r1], ACT.Square, bias=codes_b[r1]
                                     ).then_inc(sem["pts_l1"], 1)
                nc.scalar.activation(pts_r[r2], bank[5][r2], ACT.Square, bias=codes_b[r2]
                                     ).then_inc(sem["pts_r2"], 1)

            def conv1_hi(T):
                act.wait_ge(sem["c1_ps"], T.now2)
                after(act, sem["c2_ps"], T.was2)
                nc.scalar.activation(hc_hi[:, :, PAD:PAD + N], bank[3][:], ACT.Relu, bias=bn_shift[:, 0:1]
                                     ).then_inc(sem["hc_hi"], 1)

            def message(T):
                act.wait_ge(sem["msg_pre"], T.now2)
                after(act, sem["nmp_ps"], T.was2)
                nc.scalar.activation(msg[:], msg_pre[:], ACT.Relu).then_inc(sem["msg"], 1)

            def hidden_n(T):
                act.wait_ge(sem["ghn_ps"], T.now2)
                after(act, sem["u"], T.was2)
                nc.scalar.activation(ghn[:], bank[2][:], ACT.Identity, bias=half_bhn[:], scale=0.5
                                     ).then_inc(sem["ghn"], 1)

            def edges(T):
                act.wait_ge(sem["dist_ps"], T.now2)
                after(act, sem["edge_adj"], T.was2)
                nc.scalar.activation(edge[:], bank[4][:], ACT.Exp, scale=-1.0).then_inc(sem["edge"], 1)

            def nmp_hi(T):
                act.wait_ge(sem["nmp_ps"], T.now2)
                after(act, sem["z_gate_ps"], T.was2)
                copy(xn_hi[:], bank[5][:]).then_inc(sem["xn_hi"], 1)

            def conv_hi(T):
                act.wait_ge(sem["c2_res"], T.now2)
                after(act, sem["z_gate_ps"], T.was2)
                nc.scalar.activation(xc_hi[:], c2_res[:], ACT.Relu, bias=bn_shift[:, 1:2]
                                     ).then_inc(sem["xc_hi"], 1)

            def gate_r(T):
                act.wait_ge(sem["r_gate_ps"], T.now2)
                after(act, sem["u"], T.was2)
                nc.scalar.activation(tr[:], bank[3][:], ACT.Tanh, bias=half_gate_b[:, 0:1], scale=0.5
                                     ).then_inc(sem["tr"], 1)

            def gate_z(T):
                act.wait_ge(sem["z_gate_ps"], T.now2)
                after(act, sem["zq"], T.was2)
                nc.scalar.activation(tz[:], bank[4][:], ACT.Tanh, bias=half_gate_b[:, 1:2], scale=0.5
                                     ).then_inc(sem["tz"], 1)

            def gate_n(T):
                act.wait_ge(sem["v"], T.now2)
                after(act, sem["x_minus_n"], T.was2)
                after(act, sem["x_plus_n"], T.was2)
                nc.scalar.activation(nn[:], v[:], ACT.Tanh, bias=gate_bi[:, 2:3]).then_inc(sem["nn"], 1)

            def a_now(T):
                act.wait_ge(sem["at"], T.now3)
                after(act, sem["hop3_ps"], T.was3)
                after(act, sem["at3"], T.was3)
                copy(at_now, at[T.slot3][:]).then_inc(sem["at_now"], 1)

            def x2_cols(T):
                act.wait_ge(sem["x2_ps"], T.now3)
                after(act, sem["ht_ps"], T.was3)
                copy(x2[:], bank[7][:]).then_inc(sem["x2"], 1)

            def multiple(T, k):
                act.wait_ge(sem["ht_ps"], T.now3)
                after(act, sem[("prop", "t1", "t2", "hop1_ps")[k]], T.was3)
                if k > 0:
                    nc.scalar.activation(wh[k][:], bank[6][:], ACT.Copy, scale=prop_k[:, k:k + 1]
                                         ).then_inc(sem[("w0h", "w1h", "w2h", "w3h")[k]], 1)
                else:
                    nc.scalar.activation(wh[0][:], bank[6][:], ACT.Identity, bias=prop_b[:],
                                         scale=prop_k[:, 0:1]).then_inc(sem["w0h"], 1)

            def agg3(T):
                act.wait_ge(sem["agg3_ps"], T.now3)
                after(act, sem["z_ps1"], T.was3)
                copy(agg3_hi[:], bank[6][:]).then_inc(sem["agg3_hi"], 1)

            def hidden3(T, c):
                act.wait_ge((sem["z_ps0"], sem["z_ps1"])[c], T.now3)
                after(act, sem["y3_ps"], T.was3)
                nc.scalar.activation(z3[c][:], bank[7 - c][:], ACT.Relu, bias=b31_col[:, c:c + 1]
                                     ).then_inc((sem["z0"], sem["z1"])[c], 1)

            def turn(T):
                one, two, three = (k in T.stages for k in (1, 2, 3))
                if two: x1_parts(T)
                if three: a_now(T)
                if two: points(T)
                if one: agg(T)
                if two: hidden_n(T); conv1_hi(T)
                if one: a_t(T); hidden(T, 0)
                if three: x2_cols(T)
                if one: hidden(T, 1)
                if three: multiple(T, 3); multiple(T, 2); multiple(T, 1); multiple(T, 0)
                if one: hidden(T, 3); hidden(T, 2)
                if two: message(T); edges(T); nmp_hi(T)
                if one: tanh0(T, 0); tanh0(T, 3); tanh0(T, 1); tanh0(T, 2)
                if three: agg3(T)
                if two: conv_hi(T)
                if three: hidden3(T, 0)
                if two: gate_r(T)
                if three: hidden3(T, 1)
                if two: gate_n(T); gate_z(T)

            def high_parts(b):
                n = min(G, NT - b * G)
                act.wait_ge(set_pe, 1 + b + 1)
                copy(wt_hi[:, b * G:b * G + n, :], setup_bank(b)[:, 0:n, :]).then_inc(set_act, 1)

            T = Turn(-2, 0, (1,))
            act.wait_ge(w1_in, 16)
            copy(w1_hi[:], w1f[:]).then_inc(set_act, 1)
            a_t(T); agg(T)
            act.wait_ge(set_pe, 1)
            copy(vector_cols[:], bank[7][:, G - 1, 0:VR]).then_inc(set_act, 1)
            act.wait_ge(set_act, VECTORS_ACT)
            hidden(T, 0); hidden(T, 1); hidden(T, 2); hidden(T, 3)
            act.wait_ge(weights_in, ALL_WEIGHTS)
            copy(w31_hi[:], w31f[:]).then_inc(set_act, 1)
            act.wait_ge(set_dve, HALF_RMS)
            for c in range(H0):
                high_parts(c)
                tanh0(T, c)
            for b in range(H0, WT_BANKS):
                high_parts(b)
            k = MSG % G
            copy(wt_full[:], setup_bank(MSG // G)[:, k:k + 2, :]).then_inc(set_act, 1)
            act.wait_ge(set_dve, LOWS)
            act.wait_ge(codes_in, ALL_CODES)
            run_turns(act, turn, GROUPS)

        @block.vector
        def _(dve):
            V = nc.vector

            def norm_stats(k, y, y_ready, bn_done, mv_done, ve_done, count, was):
                dve.wait_ge(y_ready, count)
                for g in range(G):
                    last = V.bn_stats(stats[k][:, g, :], y[:, g, :])
                last.then_inc(bn_done, 1)
                dve.wait_ge(set_dve, LAYER0_DVE)
                dve.wait_ge(bn_done, count)
                after(dve, (sem["x1_rows"], sem["x2_rows"], sem["x3_rows"], sem["out_rows"])[k], was)
                for g in range(G):
                    last = V.bn_aggr(mv[k][:, g, :], stats[k][:, g, :])
                last.then_inc(mv_done, 1)
                dve.wait_ge(mv_done, count)
                V.tensor_scalar(ve[k][:], mv[k][:, :, 1], LN_EPS, None, ALU.add).then_inc(ve_done, 1)

            def apply(k, y, to, r_done, done, count):
                dve.wait_ge(r_done, count)
                for g in range(G):
                    last = V.tensor_scalar(to[:, g, :], y[:, g, :], mv[k][:, g, 0:1],
                                           rstd[k][:, g:g + 1], ALU.subtract, ALU.mult)
                last.then_inc(done, 1)

            def a_t_eps(T):
                dve.wait_ge(sem["adj_t_ps"], T.now1)
                after(dve, sem["nb_ps"], T.was1)
                V.scalar_tensor_tensor(out=at_eps[:], in0=over_graphs(ident), scalar=eps0[:],
                                       in1=bank[0][:], op0=ALU.mult, op1=ALU.add).then_inc(sem["at_eps"], 1)

            def row_sums(T):
                dve.wait_ge(adj_in[T.slot1], T.loads)
                after(dve, sem["prop"], T.old1)
                V.tensor_reduce(row_sum[:], adj_rows[T.slot1][:], AX_X, ALU.add).then_inc(sem["row_sum"], 1)
                dve.wait_ge(sem["row_sum"], T.now1)
                V.tensor_scalar(row_sum_eps[:], row_sum[:], ROW_SUM_EPS, None, ALU.add
                                ).then_inc(sem["row_inv"], 1)
                dve.wait_ge(sem["row_inv"], T.twice1)
                V.reciprocal(row_inv[T.slot1][:], row_sum_eps[:]).then_inc(sem["row_inv"], 1)

            def agg(T):
                dve.wait_ge(sem["agg_hi"], T.now1)
                after(dve, sem["h_ps3"], T.was1)
                V.tensor_tensor(agg_lo[:], bank[1][:], agg_hi[:].bitcast(F32), ALU.subtract
                                ).then_inc(sem["agg_lo"], 1)

            def sum_squares(T):
                dve.wait_ge(sem["sq01"], T.now1)
                dve.wait_ge(sem["sq23"], T.now1)
                V.tensor_tensor(sq_sum[:], sq01[:], sq23[:], ALU.add).then_inc(sem["sq_sum"], 1)

            def mean_square(T):
                dve.wait_ge(sem["sq_ps"], T.now1)
                V.tensor_scalar(ms[:], bank[1][:, :, 0], 1.0 / (H0 * P), RMS_EPS, ALU.mult, ALU.add
                                ).then_inc(sem["ms"], 1)

            def normalise(T, c):
                dve.wait_ge(sem["r_ps"], T.now1)
                V.tensor_tensor(hn[c][:], bank[0][:], h[c][:], ALU.mult
                                ).then_inc((sem["hn0"], sem["hn1"], sem["hn2"], sem["hn3"])[c], 1)

            def silu(T, c):
                dve.wait_ge((sem["th0"], sem["th1"], sem["th2"], sem["th3"])[c], T.now1)
                V.scalar_tensor_tensor(out=s[c][:], in0=th[c][:], scalar=1.0, in1=hn[c][:],
                                       op0=ALU.add, op1=ALU.mult
                                       ).then_inc((sem["s0"], sem["s1"], sem["s2"], sem["s3"])[c], 1)

            def residual0(T):
                dve.wait_ge(sem["y0_ps"], T.now1)
                dve.wait_ge(sem["xb"], T.now1)
                after(dve, sem["x1_rows"], T.was1)
                V.tensor_tensor(y0[:], bank[1][:], xb[:], ALU.add).then_inc(sem["y0"], 1)
                norm_stats(0, y0, sem["y0"], sem["bn0"], sem["mv0"], sem["ve0"], T.now1, T.was1)

            def apply0(T):
                after(dve, sem["x1_ps"], T.was1)
                apply(0, y0, x1_rows, sem["r0"], sem["x1_rows"], T.now1)

            def x1_low(T):
                dve.wait_ge(sem["x1"], T.now2)
                after(dve, sem["z_gate_ps"], T.was2)
                V.tensor_tensor(x1_lo[:], bank[3][:], x1_hi[:].bitcast(F32), ALU.subtract
                                ).then_inc(sem["x1_lo"], 1)

            def message_bias(T):
                dve.wait_ge(sem["msg_ps"], T.now2)
                after(dve, sem["msg"], T.was2)
                V.tensor_tensor(msg_pre[:], bank[4][:], over_graphs(msg_row), ALU.add
                                ).then_inc(sem["msg_pre"], 1)

            def points(T):
                dve.wait_ge(sem["pts_r0"], T.now2)
                after(dve, sem["dist_ps"], T.was2)
                V.tensor_scalar(pts_l[0:CODES], bank[5][0:CODES], codes_b[0:CODES], -2.0, ALU.add,
                                ALU.mult).then_inc(sem["pts_l0"], 1)

            def conv1_full(T):
                dve.wait_ge(sem["hc_hi"], T.now2)
                after(dve, sem["hc_lo"], T.was2)
                V.tensor_scalar(hc[:], bank[3][:], bn_shift[:, 0:1], 0.0, ALU.add, ALU.max
                                ).then_inc(sem["hc"], 1)

            def nmp_low(T):
                dve.wait_ge(sem["xn_hi"], T.now2)
                after(dve, sem["z_gate_ps"], T.was2)
                V.tensor_tensor(xn_lo[:], bank[5][:], xn_hi[:].bitcast(F32), ALU.subtract
                                ).then_inc(sem["xn_lo"], 1)

            def conv_residual(T):
                dve.wait_ge(sem["c2_ps"], T.now2)
                dve.wait_ge(sem["x1"], T.now2)
                after(dve, sem["xc_hi"], T.was2)
                V.tensor_tensor(c2_res[:], bank[2][:], x1[:], ALU.add).then_inc(sem["c2_res"], 1)

            def conv_full(T):
                dve.wait_ge(sem["c2_res"], T.now2)
                after(dve, sem["xc_lo"], T.was2)
                V.tensor_scalar(xc[:], c2_res[:], bn_shift[:, 1:2], 0.0, ALU.add, ALU.max
                                ).then_inc(sem["xc"], 1)

            def conv_low(T):
                dve.wait_ge(sem["xc"], T.now2)
                dve.wait_ge(sem["xc_hi"], T.now2)
                after(dve, sem["z_gate_ps"], T.was2)
                V.tensor_tensor(xc_lo[:], xc[:], xc_hi[:].bitcast(F32), ALU.subtract
                                ).then_inc(sem["xc_lo"], 1)

            def gate_u(T):
                dve.wait_ge(sem["tr"], T.now2)
                dve.wait_ge(sem["ghn"], T.now2)
                after(dve, sem["nn"], T.was2)
                V.scalar_tensor_tensor(out=u[:], in0=tr[:], scalar=1.0, in1=ghn[:], op0=ALU.add,
                                       op1=ALU.mult).then_inc(sem["u"], 1)

            def gate_v(T):
                dve.wait_ge(sem["u"], T.now2)
                dve.wait_ge(sem["n_gate_ps"], T.now2)
                V.tensor_tensor(v[:], bank[5][:], u[:], ALU.add).then_inc(sem["v"], 1)

            def add_n(T):
                dve.wait_ge(sem["nn"], T.now2)
                V.tensor_tensor(x_plus_n[:], x1[:], nn[:], ALU.add).then_inc(sem["x_plus_n"], 1)

            def residual1(T):
                dve.wait_ge(sem["x_plus_n"], T.now2)
                dve.wait_ge(sem["x_minus_n"], T.now2)
                dve.wait_ge(sem["tz"], T.now2)
                after(dve, sem["y1_ps"], T.was2)
                V.scalar_tensor_tensor(out=zq[:], in0=tz[:], scalar=1.0, in1=x_minus_n[:],
                                       op0=ALU.add, op1=ALU.mult).then_inc(sem["zq"], 1)
                dve.wait_ge(sem["zq"], T.now2)
                V.scalar_tensor_tensor(out=y1[:], in0=zq[:], scalar=0.5, in1=x_plus_n[:],
                                       op0=ALU.mult, op1=ALU.add).then_inc(sem["y1"], 1)

            def norm1(T):
                norm_stats(1, bank[6], sem["y1_ps"], sem["bn1"], sem["mv1"], sem["ve1"], T.now3, T.was3)

            def apply1(T):
                after(dve, sem["x2_ps"], T.was3)
                after(dve, sem["y2"], T.was3)
                apply(1, bank[6], x2_rows, sem["r1"], sem["x2_rows"], T.now3)

            def hop(T, k):
                hop_ps = (sem["hop1_ps"], sem["hop2_ps"], sem["hop3_ps"])[k - 1]
                to = (t2, t1, prop)[k - 1]
                dve.wait_ge(hop_ps, T.now3)
                dve.wait_ge((sem["w2h"], sem["w1h"], sem["w0h"])[k - 1], T.now3)
                after(dve, (sem["hop2_ps"], sem["hop3_ps"], sem["y2"])[k - 1], T.was3)
                dve.wait_ge(sem["row_inv"], T.twice3)
                for g in range(G):
                    last = V.scalar_tensor_tensor(
                        out=to[:, g, :], in0=bank[(7, 6, 7)[k - 1]][:, g, :],
                        scalar=row_inv[T.slot3][:, g:g + 1], in1=wh[3 - k][:, g, :], op0=ALU.mult,
                        op1=ALU.add)
                last.then_inc((sem["t2"], sem["t1"], sem["prop"])[k - 1], 1)

            def leaky_relu(T):
                dve.wait_ge(sem["prop"], T.now3)
                V.scalar_tensor_tensor(out=leaky[:], in0=prop[:], scalar=LEAKY_SLOPE, in1=prop[:],
                                       op0=ALU.mult, op1=ALU.max).then_inc(sem["leaky"], 1)

            def norm2(T):
                norm_stats(2, y2, sem["y2"], sem["bn2"], sem["mv2"], sem["ve2"], T.now3, T.was3)

            def apply2(T):
                after(dve, sem["agg3_ps"], T.was3)
                after(dve, sem["x3b"], T.was3)
                apply(2, y2, x3_rows, sem["r2"], sem["x3_rows"], T.now3)

            def a_t3(T):
                dve.wait_ge(sem["at_now"], T.now3)
                after(dve, sem["agg3_ps"], T.was3)
                V.scalar_tensor_tensor(out=at3, in0=over_graphs(ident), scalar=one_eps3[:],
                                       in1=at_now, op0=ALU.mult, op1=ALU.add).then_inc(sem["at3"], 1)

            def agg3(T):
                dve.wait_ge(sem["agg3_hi"], T.now3)
                after(dve, sem["z_ps1"], T.was3)
                V.tensor_tensor(agg3_lo[:], bank[6][:], agg3_hi[:].bitcast(F32), ALU.subtract
                                ).then_inc(sem["agg3_lo"], 1)

            def residual3(T):
                dve.wait_ge(sem["y3_ps"], T.now3)
                dve.wait_ge(sem["x3b"], T.now3)
                after(dve, sem["out_rows"], T.was3)
                V.tensor_tensor(y3, bank[7][:], x3b, ALU.add).then_inc(sem["y3"], 1)
                norm_stats(3, y3, sem["y3"], sem["bn3"], sem["mv3"], sem["ve3"], T.now3, T.was3)

            def apply3(T):
                after(dve, stored[T.slot3], T.stores)
                apply(3, y3, out_rows[T.slot3], sem["r3"], sem["out_rows"], T.now3)

            def turn(T):
                one, two, three = (k in T.stages for k in (1, 2, 3))
                T.loads = loads_of(T, dve)
                if isinstance(T.t, int):
                    T.twice1, T.twice3 = 2 * (T.t + 2) + 1, 2 * T.t + 2
                    T.stores = 16 * (T.t // 2)
                else:
                    T.twice1, T.twice3 = dve.snap(2 * T.t + 5), dve.snap(2 * T.t + 2)
                    T.stores = dve.snap(8 * (T.t - T.slot3))
                if two: x1_low(T)
                if one: a_t_eps(T)
                if three: norm1(T)
                if two: message_bias(T); points(T)
                if one: agg(T)
                if three: apply1(T)
                if two: conv1_full(T)
                if three: a_t3(T); hop(T, 1); hop(T, 2)
                if one: sum_squares(T)
                if three: hop(T, 3)
                if one: mean_square(T)
                if three: leaky_relu(T)
                if one: row_sums(T)
                if two: nmp_low(T)
                if one: normalise(T, 2)
                if three: norm2(T)
                if one: normalise(T, 0); normalise(T, 3); normalise(T, 1)
                if three: apply2(T)
                if one: silu(T, 0); silu(T, 2); silu(T, 1)
                if two: conv_residual(T)
                if one: silu(T, 3)
                if two: conv_full(T)
                if three: agg3(T)
                if two: conv_low(T)
                if one: residual0(T)
                if two: gate_u(T); gate_v(T)
                if one: apply0(T)
                if two: add_n(T)
                if three: residual3(T)
                if two: residual1(T)
                if three: apply3(T)

            done = 0

            def step(instruction):
                nonlocal done
                instruction.then_inc(set_dve, 1)
                done += 1

            def low_parts(first, end):
                for b in range(first, end):
                    n = min(G, NT - b * G)
                    dve.wait_ge(set_act, SPLIT_ACT if b == WT_BANKS - 1 else HIGHS + b + 1)
                    step(V.tensor_tensor(wt_lo[:, b * G:b * G + n, :], setup_bank(b)[:, 0:n, :],
                                         wt_hi[:, b * G:b * G + n, :].bitcast(F32), ALU.subtract))

            T = Turn(-2, 0, (1,))
            T.loads, T.twice1 = loads_of(T, dve), 1
            dve.wait_ge(eps0_in, 16)
            a_t_eps(T)
            dve.wait_ge(w1_in, 16)
            dve.wait_ge(set_act, W1_HIGH)
            step(V.tensor_tensor(w1_lo[:], w1f[:], w1_hi[:].bitcast(F32), ALU.subtract))
            assert done == W1_LOW
            agg(T)
            dve.wait_ge(set_act, VECTORS_ACT)
            step(V.tensor_scalar(bn_ve[:], bn_v, BN_EPS, None, ALU.add))
            assert done == BN_VE
            step(V.tensor_scalar(half_rms[:], rms_col, 0.5, None, ALU.mult))
            assert done == HALF_RMS
            dve.wait_ge(layer0_in, ALL_LAYER0)
            dve.wait_ge(set_dve, done)
            for c in range(H0):
                step(V.tensor_scalar(w2[:, c, :], w2[:, c, :], half_rms[:, c:c + 1], None, ALU.mult))
            assert done == LAYER0_DVE
            row_sums(T)
            dve.wait_ge(set_pool, BN_POW)
            step(V.tensor_tensor(bn_scale[:], bn_g, bn_r[:], ALU.mult))
            dve.wait_ge(set_dve, done)
            step(V.tensor_tensor(bn_ms[:], bn_m, bn_scale[:], ALU.mult))
            dve.wait_ge(set_dve, done)
            step(V.tensor_tensor(bn_shift[:], bn_b, bn_ms[:], ALU.subtract))
            sum_squares(T)
            dve.wait_ge(weights_in, ALL_WEIGHTS)
            step(V.tensor_scalar(conv1_w[:], conv1_w[:], bn_scale[:, 0:1], None, ALU.mult))
            step(V.tensor_scalar(conv2_w, conv2_w, bn_scale[:, 1:2], None, ALU.mult))
            assert done == CONV_SCALED
            mean_square(T)
            step(V.tensor_tensor(gate_b[:], gate_bi[:, 0:2], gate_bh[:, 0:2], ALU.add))
            dve.wait_ge(set_dve, done)
            step(V.tensor_scalar(half_gate_b[:], gate_b[:], 0.5, None, ALU.mult))
            step(V.tensor_scalar(half_bhn[:], gate_bh[:, 2:3], 0.5, None, ALU.mult))
            step(V.tensor_scalar(one_eps3[:], eps3[:], 1.0, None, ALU.add))
            step(V.memset(pts_l[CODE_ROWS[2]:CODE_ROWS[2] + CODES], 1.0))
            step(V.memset(pts_r[CODE_ROWS[1]:CODE_ROWS[1] + CODES], 1.0))
            normalise(T, 0); normalise(T, 1); normalise(T, 2); normalise(T, 3)
            dve.wait_ge(set_act, HIGHS)
            step(V.tensor_tensor(w31_lo[:], w31f[:], w31_hi[:].bitcast(F32), ALU.subtract))
            assert done == LOWS
            for c in range(H0):
                low_parts(c, c + 1)
                silu(T, c)
            low_parts(H0, 6)
            residual0(T)
            low_parts(6, WT_BANKS)
            assert done == SPLIT_DVE
            apply0(T)
            dve.wait_ge(set_dve, done)
            dve.wait_ge(codes_in, ALL_CODES)
            run_turns(dve, turn, GROUPS)

        @block.gpsimd
        def _(pool):
            Q = nc.gpsimd

            def power(k, ready, done, count, was, base, to):
                pool.wait_ge(ready, count)
                Q.tensor_tensor(to[:], base[:], minus_half[:], ALU.pow).then_inc(done, 1)

            def x_bias(T):
                pool.wait_ge(x_in[T.slot1], T.loads)
                after(pool, sem["y0"], T.was1)
                Q.tensor_tensor(xb[:], x_rows[T.slot1][:], over_graphs(b2_row), ALU.add).then_inc(sem["xb"], 1)

            def add_squares01(T):
                pool.wait_ge(sem["sq0"], T.now1)
                pool.wait_ge(sem["sq1"], T.now1)
                Q.tensor_tensor(sq01[:], sq[0][:], sq[1][:], ALU.add).then_inc(sem["sq01"], 1)

            def add_squares23(T):
                pool.wait_ge(sem["sq2"], T.now1)
                pool.wait_ge(sem["sq3"], T.now1)
                Q.tensor_tensor(sq23[:], sq[2][:], sq[3][:], ALU.add).then_inc(sem["sq23"], 1)

            def rms(T):
                power(0, sem["ms"], sem["r_rms"], T.now1, T.was1, ms, r_rms)

            def norm0(T):
                power(0, sem["ve0"], sem["r0"], T.now1, T.was1, ve[0], rstd[0])

            def edge_weights(T):
                pool.wait_ge(sem["edge"], T.now2)
                pool.wait_ge(sem["at"], T.now2)
                after(pool, sem["nmp_ps"], T.was2)
                Q.tensor_tensor(edge_adj[:], edge[:], at[T.slot2][:], ALU.mult).then_inc(sem["edge_adj"], 1)

            def conv1_low(T):
                pool.wait_ge(sem["hc"], T.now2)
                pool.wait_ge(sem["hc_hi"], T.now2)
                after(pool, sem["c2_ps"], T.was2)
                Q.tensor_tensor(hc_lo[:, :, PAD:PAD + N], hc[:], hc_hi[:, :, PAD:PAD + N].bitcast(F32),
                                ALU.subtract).then_inc(sem["hc_lo"], 1)

            def minus(T):
                pool.wait_ge(sem["nn"], T.now2)
                after(pool, sem["zq"], T.was2)
                Q.tensor_tensor(x_minus_n[:], x1[:], nn[:], ALU.subtract).then_inc(sem["x_minus_n"], 1)

            def norm1(T):
                power(1, sem["ve1"], sem["r1"], T.now3, T.was3, ve[1], rstd[1])

            def residual2(T):
                pool.wait_ge(sem["leaky"], T.now3)
                after(pool, sem["x3_rows"], T.was3)
                Q.tensor_tensor(y2, leaky[:], x2_rows[:], ALU.add).then_inc(sem["y2"], 1)

            def norm2(T):
                power(2, sem["ve2"], sem["r2"], T.now3, T.was3, ve[2], rstd[2])

            def x3_bias(T):
                pool.wait_ge(sem["x3_rows"], T.now3)
                after(pool, sem["y3"], T.was3)
                Q.tensor_tensor(x3b, x3_rows, over_graphs(b32_row), ALU.add).then_inc(sem["x3b"], 1)

            def norm3(T):
                power(3, sem["ve3"], sem["r3"], T.now3, T.was3, ve[3], rstd[3])

            def turn(T):
                one, two, three = (k in T.stages for k in (1, 2, 3))
                T.loads = loads_of(T, pool)
                if three: norm1(T)
                if two: conv1_low(T)
                if one: add_squares01(T); x_bias(T); add_squares23(T)
                if two: edge_weights(T)
                if one: rms(T)
                if three: residual2(T); norm2(T); x3_bias(T)
                if one: norm0(T)
                if two: minus(T)
                if three: norm3(T)

            Q.memset(codes_w[:], 0.0).then_inc(cleared, 1)
            Q.memset(ident[:], 0.0).then_inc(set_pool, 1)
            pool.wait_ge(set_pool, 1)
            Q.affine_select(out=ident[:], in_=ident[:], compare_op=ALU.not_equal, fill=1.0, base=0,
                            pattern=[[-1, P]], channel_multiplier=1).then_inc(set_pool, 1)
            Q.memset(ones[:], 1.0)
            Q.memset(minus_half[:], -0.5)
            Q.memset(pts_l[:], 0.0)
            Q.memset(pts_r[:], 0.0)
            for tile in (hc_hi, hc_lo):
                Q.memset(tile[:, :, 0:PAD].bitcast(F32), 0.0)
                last = Q.memset(tile[:, :, PAD + N:NP].bitcast(F32), 0.0)
            last.then_inc(set_pool, 1)
            T = Turn(-2, 0, (1,))
            T.loads = loads_of(T, pool)
            pool.wait_ge(layer0_in, ALL_LAYER0)
            x_bias(T)
            pool.wait_ge(set_dve, BN_VE)
            pool.wait_ge(set_pool, TILES_SET)
            Q.tensor_tensor(bn_r[:], bn_ve[:], minus_half[:, 0:2], ALU.pow).then_inc(set_pool, 1)
            add_squares01(T); add_squares23(T); rms(T); norm0(T)
            pool.wait_ge(weights_in, ALL_WEIGHTS)
            run_turns(pool, turn, GROUPS)


_INS = ['x', 'adj', 'L0_gnn_epsilon', 'L0_gnn_W1', 'L0_gnn_b1', 'L0_gnn_rms_weight', 'L0_gnn_W2',
        'L0_gnn_b2', 'L1_gnn_w_se', 'L1_gnn_b_se', 'L1_gnn_conv1_w', 'L1_gnn_bn1_g', 'L1_gnn_bn1_b',
        'L1_gnn_bn1_m', 'L1_gnn_bn1_v', 'L1_gnn_conv2_w', 'L1_gnn_bn2_g', 'L1_gnn_bn2_b',
        'L1_gnn_bn2_m', 'L1_gnn_bn2_v', 'L1_gnn_w_msg', 'L1_gnn_b_msg', 'L1_gnn_w_ih',
        'L1_gnn_b_ih', 'L1_gnn_w_hh', 'L1_gnn_b_hh', 'L2_gnn_W', 'L2_gnn_conv_w', 'L2_gnn_conv_b',
        'L3_gnn_eps', 'L3_gnn_W1', 'L3_gnn_b1', 'L3_gnn_W2', 'L3_gnn_b2']


def kernel(**inputs):
    import numpy as np
    import concourse.bacc as bacc
    from concourse.bass_utils import run_bass_kernel_spmd

    nc = bacc.Bacc("TRN2", target_bir_lowering=False, num_devices=1)
    arrays, args = {}, {}
    for name in _INS:
        a = np.ascontiguousarray(inputs[name])
        if name == 'L0_gnn_epsilon':
            a = a.reshape(1, 1)
        arrays[f"in_{name}"] = a
        args[name] = nc.dram_tensor(f"in_{name}", a.shape, mybir.dt.from_np(a.dtype),
                                    kind="ExternalInput").ap()
    out = nc.dram_tensor("out", inputs['x'].shape, F32, kind="ExternalOutput").ap()
    graph_layers(nc, args.pop('x'), args.pop('adj'), out, args)
    result = run_bass_kernel_spmd(nc, [arrays], core_ids=[0])
    return result.results[0]["out"]
```

```python
from contextlib import ExitStack

import concourse.bass as bass
from concourse import mybir

F32 = mybir.dt.float32
F32R = mybir.dt.float32r
ALU = mybir.AluOpType
ACT = mybir.ActivationFunctionType
AX_X = mybir.AxisListType.X

P = 128
LN_EPS = 1e-5
RMS_EPS = 1e-6
BN_EPS = 1e-5
ROW_SUM_EPS = 1e-9
LEAKY_SLOPE = 0.2

STEPS = """
adj_t_ps at_eps at row_inv nb_ps agg_hi agg_lo h_ps0 h_ps1 h_ps2 h_ps3 h0 h1 h2 h3 sq0 sq1 sq2 sq3
sq01 sq23 sq_sum sq_ps ms r_rms r_ps hn0 hn1 hn2 hn3 th0 th1 th2 th3 s0 s1 s2 s3 row_sum
xb y0_ps y0 bn0 mv0 ve0 r0 x1_rows
x1_ps x1 x1_hi x1_lo msg_ps msg_pre msg pts_ps pts_r0 pts_l1 pts_r2 pts_l0 c1_ps hc_hi hc hc_lo
ghn_ps ghn dist_ps edge edge_adj nmp_ps xn_hi xn_lo c2_ps c2_res xc_hi xc xc_lo
r_gate_ps z_gate_ps n_gate_ps tr tz u v nn x_minus_n x_plus_n zq y1
at_now y1_ps bn1 mv1 ve1 r1 x2_rows ht_ps ht w3h w2h w1h w0h hop1_ps t2 hop2_ps t1 hop3_ps prop leaky
y2 bn2 mv2 ve2 r2 x3_rows
x3b at3 agg3_ps agg3_hi agg3_lo z_ps0 z_ps1 z0 z1 y3_ps y3 bn3 mv3 ve3 r3 out_rows
""".split()


def after(engine, semaphore, count):
    if isinstance(count, int) and count <= 0:
        return
    engine.wait_ge(semaphore, count)


class Turn:

    def __init__(self, t, parity, stages, engine=None):
        at = [t + k for k in range(-1, 4)]
        if engine is not None:
            at = [engine.snap(a) for a in at]
        self.t, self.stages = t, stages
        self.now1, self.was1, self.old1 = at[4], at[3], at[2]
        self.now2, self.was2 = at[3], at[2]
        self.now3, self.was3 = at[2], at[1]
        self.now4, self.was4 = at[1], at[0]
        self.slot1, self.slot2, self.slot3, self.slot4 = parity, 1 - parity, parity, 1 - parity


def run_turns(engine, turn, groups):
    turn(Turn(-1, 1, (1, 2)))
    turn(Turn(0, 0, (1, 2, 3)))
    for t in (1, 2, 3):
        turn(Turn(t, t % 2, (1, 2, 3, 4)))
    with engine.Fori(4, groups - 2, 2) as t:
        turn(Turn(t, 0, (1, 2, 3, 4), engine))
        turn(Turn(t + 1, 1, (1, 2, 3, 4), engine))
    turn(Turn(groups - 2, 0, (2, 3, 4)))
    turn(Turn(groups - 1, 1, (3, 4)))
    turn(Turn(groups, 0, (4,)))


def graph_layers(nc, x, adj, out, w):
    B, N, D = x.shape
    G = 4
    GROUPS = B // G
    W = G * N
    assert N == P and D == P and GROUPS % 2 == 0
    H0 = w["L0_gnn_W1"].shape[1] // P
    H3 = w["L3_gnn_W1"].shape[1] // P
    TAPS = w["L1_gnn_conv2_w"].shape[2]
    PAD = TAPS // 2
    TAP_ORDER = [PAD] + [k for k in range(TAPS) if k != PAD]
    CODES = w["L1_gnn_w_se"].shape[0]

    CONV2, CONV1, SE = 0, TAPS, TAPS + 1
    IH = TAPS + 2
    HH = IH + 6
    MSG = HH + 3
    R_GATE, Z_GATE, N_GATE = range(3)
    PROP = MSG + 1
    NT = PROP + 1
    assert NT < 8 * G

    with ExitStack() as ctx:
        def sb(name, shape, dt=F32):
            return ctx.enter_context(nc.sbuf_tensor(name, shape, dt))

        def rows(name, dt=F32):
            return sb(name, [P, G, P], dt)

        bank = [ctx.enter_context(nc.psum_tensor(f"bank{i}", [P, G, P], F32)) for i in range(8)]
        sem = {n: ctx.enter_context(nc.semaphore(n)) for n in STEPS}
        x_in = [ctx.enter_context(nc.semaphore(f"x_in{i}")) for i in range(2)]
        adj_in = [ctx.enter_context(nc.semaphore(f"adj_in{i}")) for i in range(2)]
        stored = [ctx.enter_context(nc.semaphore(f"stored{i}")) for i in range(2)]
        vectors_in = ctx.enter_context(nc.semaphore("vectors_in"))
        eps0_in = ctx.enter_context(nc.semaphore("eps0_in"))
        w1_in = ctx.enter_context(nc.semaphore("w1_in"))
        layer0_in = ctx.enter_context(nc.semaphore("layer0_in"))
        weights_in = ctx.enter_context(nc.semaphore("weights_in"))
        codes_in = ctx.enter_context(nc.semaphore("codes_in"))
        cleared = ctx.enter_context(nc.semaphore("cleared"))
        set_pool = ctx.enter_context(nc.semaphore("set_pool"))
        set_dve = ctx.enter_context(nc.semaphore("set_dve"))
        set_pe = ctx.enter_context(nc.semaphore("set_pe"))
        set_act = ctx.enter_context(nc.semaphore("set_act"))

        ident = sb("ident", [P, P])
        ones = sb("ones", [P, P])
        minus_half = sb("minus_half", [P, G])
        w1f = sb("w1f", [P, H0 * P])
        w1_hi = sb("w1_hi", [P, H0 * P], F32R)
        w1_lo = sb("w1_lo", [P, H0 * P], F32R)
        w2 = sb("w2", [P, H0, D])
        w31f = sb("w31f", [P, H3 * P])
        w31_hi = sb("w31_hi", [P, H3 * P], F32R)
        w31_lo = sb("w31_lo", [P, H3 * P], F32R)
        w32 = sb("w32", [P, H3, D])
        arena = sb("arena", [P, 5, G, P])
        assert P * TAPS <= 5 * G * P
        conv2_w = arena[:].rearrange("p a g n -> p (a g n)")[:, 0:P * TAPS].rearrange(
            "p (i k) -> p i k", k=TAPS)
        conv1_w = sb("conv1_w", [P, P])
        codes_w = sb("codes_w", [P, P])
        msg_w = sb("msg_w", [P, P])
        ih_w = sb("ih_w", [P, 3, 2, P])
        hh_w = sb("hh_w", [P, 3, P])
        prop_w = sb("prop_w", [P, P])
        prop_sum, prop_mean = sb("prop_sum", [P, 1]), sb("prop_mean", [P, 1])
        wt_hi = sb("wt_hi", [P, NT, P], F32R)
        wt_lo = sb("wt_lo", [P, NT, P], F32R)
        wt_full = sb("wt_full", [P, 2, P])
        vectors = [("b1", w["L0_gnn_b1"], H0), ("rms", w["L0_gnn_rms_weight"], H0),
                   ("g1", w["L1_gnn_bn1_g"], 1), ("g2", w["L1_gnn_bn2_g"], 1),
                   ("b1n", w["L1_gnn_bn1_b"], 1), ("b2n", w["L1_gnn_bn2_b"], 1),
                   ("m1", w["L1_gnn_bn1_m"], 1), ("m2", w["L1_gnn_bn2_m"], 1),
                   ("v1", w["L1_gnn_bn1_v"], 1), ("v2", w["L1_gnn_bn2_v"], 1),
                   ("bi", w["L1_gnn_b_ih"], 3), ("bh", w["L1_gnn_b_hh"], 3),
                   ("b31", w["L3_gnn_b1"], H3)]
        first_row, VR = {}, 0
        for name, _, count in vectors:
            first_row[name] = VR
            VR += count
        vector_rows = sb("vector_rows", [VR, P])
        vector_cols = sb("vector_cols", [P, VR])

        def columns(name, count):
            return vector_cols[:, first_row[name]:first_row[name] + count]

        b1_col = columns("b1", H0)
        rms_col = columns("rms", H0)
        half_rms = sb("half_rms", [P, H0])
        b31_col = columns("b31", H3)
        codes_b = sb("codes_b", [P, 1])
        bn_g, bn_b, bn_m, bn_v = (columns(n, 2) for n in ("g1", "b1n", "m1", "v1"))
        bn_ve = sb("bn_ve", [P, 2])
        bn_r = sb("bn_r", [P, 2])
        bn_scale = sb("bn_scale", [P, 2])
        bn_ms = sb("bn_ms", [P, 2])
        bn_shift = sb("bn_shift", [P, 2])
        gate_bi = columns("bi", 3)
        gate_bh = columns("bh", 3)
        gate_b = sb("gate_b", [P, 2])
        half_gate_b = sb("half_gate_b", [P, 2])
        half_bhn = sb("half_bhn", [P, 1])
        b2_row = sb("b2_row", [P, D])
        msg_row = sb("msg_row", [P, D])
        b32_row = sb("b32_row", [P, D])
        eps0 = sb("eps0", [P, 1])
        eps3 = sb("eps3", [P, 1])
        one_eps3 = sb("one_eps3", [P, 1])
        prop_k = sb("prop_k", [P, 4])
        prop_b = sb("prop_b", [P, 1])

        x_rows = [rows(f"x_rows{i}") for i in range(2)]
        adj_rows = [rows(f"adj_rows{i}") for i in range(2)]
        at = [rows(f"at{i}") for i in range(2)]
        row_inv = [sb(f"row_inv{i}", [P, G]) for i in range(2)]
        row_sum = sb("row_sum", [P, G])
        row_sum_eps = sb("row_sum_eps", [P, G])
        at_now = w1f[:].rearrange("p (g n) -> p g n", g=G)
        at_eps = rows("at_eps")
        agg_hi, agg_lo = rows("agg_hi", F32R), rows("agg_lo", F32R)
        h = [rows(f"h{c}") for c in range(H0)]
        sq = [rows(f"sq{c}") for c in range(H0)]
        hn = [rows(f"hn{c}") for c in range(H0)]
        th = [rows(f"th{c}") for c in range(H0)]
        s = h
        sq01, sq23, sq_sum = sq[0], sq[2], sq[1]
        ms = sb("ms", [P, G])
        r_rms = sb("r_rms", [P, G])
        xb = rows("xb")
        y0 = rows("y0")
        x1_rows = rows("x1_rows")
        x1 = rows("x1")
        x1_hi, x1_lo = rows("x1_hi", F32R), rows("x1_lo", F32R)
        msg_pre, msg = rows("msg_pre"), rows("msg")
        pts_l, pts_r = rows("pts_l"), rows("pts_r")
        hc = rows("hc")
        hc_hi, hc_lo = sb("hc_hi", [P, G, N + 2], F32R), sb("hc_lo", [P, G, N + 2], F32R)
        ghn = rows("ghn")
        edge, edge_adj = rows("edge"), rows("edge_adj")
        xn_hi, xn_lo = rows("xn_hi", F32R), rows("xn_lo", F32R)
        c2_res, xc = rows("c2_res"), rows("xc")
        xc_hi, xc_lo = rows("xc_hi", F32R), rows("xc_lo", F32R)
        tr, tz, u, nn = rows("tr"), rows("tz"), rows("u"), rows("nn")
        v = u
        x_minus_n, x_plus_n, zq = rows("x_minus_n"), rows("x_plus_n"), rows("zq")
        y1 = zq
        x2_rows, ht = rows("x2_rows"), rows("ht")
        wh = [rows(f"w{k}h") for k in range(4)]
        t2, t1, prop = rows("t2"), rows("t1"), rows("prop")
        leaky = prop
        y2, x3_rows, x3b, at3, y3 = (arena[:, i] for i in range(5))
        agg3_hi, agg3_lo = rows("agg3_hi", F32R), rows("agg3_lo", F32R)
        z3 = [rows(f"z3_{c}") for c in range(H3)]
        out_rows = [rows(f"out_rows{i}") for i in range(2)]
        stats = [sb(f"stats{i}", [P, G, 6]) for i in range(4)]
        mv = [sb(f"mv{i}", [P, G, 2]) for i in range(4)]
        ve = [sb(f"ve{i}", [P, G]) for i in range(4)]
        rstd = [sb(f"rstd{i}", [P, G]) for i in range(4)]

        def cols(tile):
            return tile[:].rearrange("p g n -> p (g n)")

        def over_graphs(tile):
            return tile[:].unsqueeze(1).to_broadcast([P, G, P])

        x_dram = x.rearrange("(k g) n d -> k n g d", g=G)
        adj_dram = adj.rearrange("(k g) n m -> k n g m", g=G)
        out_dram = out.rearrange("(k g) n d -> k n g d", g=G)

        def one_row(vector):
            n = vector.shape[0]
            return vector.rearrange("(a d) -> a d", a=1).to_broadcast([P, n])

        IDENT_SET = 2
        TILES_SET = 3
        BN_POW = 4
        WT_BANKS = -(-NT // G)
        W1_HIGH = 1
        VECTORS_ACT = 2
        HIGHS = 3
        SPLIT_ACT = HIGHS + WT_BANKS + 1
        W1_LOW = 1
        BN_VE = 2
        HALF_RMS = 3
        LAYER0_DVE = HALF_RMS + H0
        CONV_SCALED = LAYER0_DVE + 8
        LOWS = CONV_SCALED + 7
        SPLIT_DVE = LOWS + WT_BANKS

        def setup_bank(b):
            return bank[2 + b % (8 - 2)]

        def loads_of(T, engine):
            if isinstance(T.t, int):
                return 16 * ((T.t + 2) // 2 + 1)
            return engine.snap(8 * (T.t - T.slot1) + 32)

        block = ctx.enter_context(nc.Block())

        LAYER0_LOADS = [
            (b2_row[:], one_row(w["L0_gnn_b2"])),
            (w2[:], w["L0_gnn_W2"].rearrange("(c p) d -> p c d", p=P)),
        ]
        WEIGHT_LOADS = [
            (conv1_w[:], w["L1_gnn_conv1_w"].rearrange("o i k -> o (i k)")),
            (conv2_w, w["L1_gnn_conv2_w"]),
            (msg_w[:], w["L1_gnn_w_msg"]),
            (msg_row[:], one_row(w["L1_gnn_b_msg"])),
            (ih_w[:], w["L1_gnn_w_ih"].rearrange("(a o) (b i) -> o a b i", a=3, b=2)),
            (hh_w[:], w["L1_gnn_w_hh"].rearrange("(a o) i -> o a i", a=3)),
            (prop_w[:], w["L2_gnn_W"]),
            (prop_k[:], one_row(w["L2_gnn_conv_w"])),
            (prop_b[:], one_row(w["L2_gnn_conv_b"])),
            (eps3[:], one_row(w["L3_gnn_eps"])),
            (w31f[:], w["L3_gnn_W1"]),
            (w32[:], w["L3_gnn_W2"].rearrange("(c p) d -> p c d", p=P)),
            (b32_row[:], one_row(w["L3_gnn_b2"])),
        ]
        ALL_LAYER0 = 16 * len(LAYER0_LOADS)
        ALL_WEIGHTS = 16 * len(WEIGHT_LOADS)
        CODE_ROWS = (0, 32, 64)
        ALL_CODES = 16 * 2 * len(CODE_ROWS)

        @block.sync
        def _(sp):
            def load(group, slot, count):
                after(sp, sem["adj_t_ps"], count)
                after(sp, sem["row_sum"], count)
                sp.dma_start(adj_rows[slot][:], adj_dram[group]).then_inc(adj_in[slot], 16)
                after(sp, sem["nb_ps"], count)
                after(sp, sem["xb"], count)
                sp.dma_start(x_rows[slot][:], x_dram[group]).then_inc(x_in[slot], 16)

            def turn(T):
                if 1 in T.stages:
                    load(T.t + 3, 1 - T.slot1, T.was1)
                if 4 in T.stages:
                    sp.wait_ge(sem["out_rows"], T.now4)
                    sp.dma_start(out_dram[T.t - 1], out_rows[T.slot4][:]).then_inc(stored[T.slot4], 16)

            sp.dma_start(eps0[:], w["L0_gnn_epsilon"].to_broadcast([P, 1])).then_inc(eps0_in, 16)
            load(0, 0, 0)
            sp.dma_start(w1f[:], w["L0_gnn_W1"]).then_inc(w1_in, 16)
            for name, vector, count in vectors:
                r = first_row[name]
                sp.dma_start(vector_rows[r:r + count, :], vector.rearrange("(a p) -> a p", a=count)
                             ).then_inc(vectors_in, 16)
            for tile, source in LAYER0_LOADS:
                sp.dma_start(tile, source).then_inc(layer0_in, 16)
            for tile, source in WEIGHT_LOADS:
                sp.dma_start(tile, source).then_inc(weights_in, 16)
            sp.wait_ge(cleared, 1)
            for at_row in CODE_ROWS:
                sp.dma_start(codes_w[at_row:at_row + CODES, :], w["L1_gnn_w_se"]).then_inc(codes_in, 16)
                sp.dma_start(codes_b[at_row:at_row + CODES, :],
                             w["L1_gnn_b_se"].rearrange("(p a) -> p a", a=1)).then_inc(codes_in, 16)

            turn(Turn(-2, 0, (1,)))
            turn(Turn(-1, 1, (1, 2)))
            turn(Turn(0, 0, (1, 2, 3)))
            turn(Turn(1, 1, (1, 2, 3, 4)))
            with sp.Fori(2, GROUPS - 4, 2) as t:
                turn(Turn(t, 0, (1, 2, 3, 4), sp))
                turn(Turn(t + 1, 1, (1, 2, 3, 4), sp))
            turn(Turn(GROUPS - 4, 0, (1, 2, 3, 4)))
            for t in range(GROUPS - 3, GROUPS + 1):
                turn(Turn(t, t % 2, (4,)))
            for slot in range(2):
                sp.wait_ge(stored[slot], 16 * (GROUPS // 2))

        @block.tensor
        def _(pe):
            def split_product(psum, hi, lo, moving_hi, moving_lo, start, stop):
                pe.matmul(psum, hi, moving_hi, start=start, stop=False)
                pe.matmul(psum, hi, moving_lo, start=False, stop=False)
                return pe.matmul(psum, lo, moving_hi, start=False, stop=stop)

            def weight(k):
                return wt_hi[:, k, :], wt_lo[:, k, :]

            def transposes(psum, tile):
                for g in range(G):
                    last = pe.transpose(psum[:, g, :], tile[:, g, :], ident[:])
                return last

            def by_graph(psum, lhs, rhs):
                for g in range(G):
                    last = pe.matmul(psum[:, g, :], lhs(g), rhs(g), start=True, stop=True)
                return last

            def adj_t(T):
                pe.wait_ge(adj_in[T.slot1], T.loads)
                for c in range(H0):
                    after(pe, sem[f"hn{c}"], T.was1)
                transposes(bank[0], adj_rows[T.slot1]).then_inc(sem["adj_t_ps"], 1)

            def neighbours(T):
                pe.wait_ge(x_in[T.slot1], T.loads)
                pe.wait_ge(sem["at_eps"], T.now1)
                after(pe, sem["y0"], T.was1)
                by_graph(bank[1], lambda g: x_rows[T.slot1][:, g, :],
                         lambda g: at_eps[:, g, :]).then_inc(sem["nb_ps"], 1)

            def hidden(T, c):
                if c == 0:
                    pe.wait_ge(sem["agg_hi"], T.now1)
                    pe.wait_ge(sem["agg_lo"], T.now1)
                if c == 1:
                    pe.wait_ge(sem["at"], T.now1)
                if c >= 2:
                    pe.wait_ge((sem["h0"], sem["h1"])[c - 2], T.now1)
                    pe.wait_ge((sem["sq0"], sem["sq1"])[c - 2], T.now1)
                split_product(bank[1 - c % 2][:].rearrange("p g n -> p (g n)"),
                              w1_hi[:, c * P:(c + 1) * P], w1_lo[:, c * P:(c + 1) * P],
                              cols(agg_hi), cols(agg_lo), True, True
                              ).then_inc((sem["h_ps0"], sem["h_ps1"], sem["h_ps2"], sem["h_ps3"])[c], 1)

            def square_sums(T):
                pe.wait_ge(sem["sq_sum"], T.now1)
                pe.wait_ge(sem["h2"], T.now1)
                by_graph(bank[1], lambda g: sq_sum[:, g, :], lambda g: ones[:]
                         ).then_inc(sem["sq_ps"], 1)

            def spread_rms(T):
                pe.wait_ge(sem["r_rms"], T.now1)
                pe.wait_ge(sem["h3"], T.now1)
                pe.wait_ge(sem["sq3"], T.now1)
                for g in range(G):
                    last = pe.transpose(bank[0][:, g, :], r_rms[:, g:g + 1].to_broadcast([P, P]),
                                        ident[:])
                last.then_inc(sem["r_ps"], 1)

            def down(T, c):
                pe.wait_ge((sem["s0"], sem["s1"], sem["s2"], sem["s3"])[c], T.now1)
                if c == 0:
                    pe.wait_ge(sem["ms"], T.now1)
                for g in range(G):
                    last = pe.matmul(bank[1][:, g, :], s[c][:, g, :], w2[:, c, :],
                                     start=(c == 0 and g == 0), stop=(c == H0 - 1),
                                     skip_group_check=True)
                if c == H0 - 1:
                    last.then_inc(sem["y0_ps"], 1)

            def x1_t(T):
                pe.wait_ge(sem["x1_rows"], T.now2)
                after(pe, sem["tr"], T.was2)
                transposes(bank[3], x1_rows).then_inc(sem["x1_ps"], 1)

            def messages(T):
                pe.wait_ge(sem["x1"], T.now2)
                after(pe, sem["tz"], T.was2)
                by_graph(bank[4], lambda g: x1[:, g, :], lambda g: wt_full[:, 0, :]
                         ).then_inc(sem["msg_ps"], 1)

            def codes(T):
                pe.wait_ge(sem["x1_lo"], T.now2)
                pe.wait_ge(sem["x1_hi"], T.now2)
                after(pe, sem["v"], T.was2)
                split_product(cols(bank[5]), *weight(SE), cols(x1_hi), cols(x1_lo), True, True
                              ).then_inc(sem["pts_ps"], 1)

            def conv1(T):
                pe.wait_ge(sem["x1_lo"], T.now2)
                pe.wait_ge(sem["x1"], T.now2)
                split_product(cols(bank[3]), *weight(CONV1), cols(x1_hi), cols(x1_lo), True, True
                              ).then_inc(sem["c1_ps"], 1)

            def hidden_n(T):
                pe.wait_ge(sem["x1_hi"], T.now2)
                pe.wait_ge(sem["x1_lo"], T.now2)
                after(pe, sem["c2_res"], T.was2)
                split_product(cols(bank[2]), *weight(HH + 2), cols(x1_hi), cols(x1_lo), True, True
                              ).then_inc(sem["ghn_ps"], 1)

            def distances(T):
                pe.wait_ge(sem["pts_l0"], T.now2)
                pe.wait_ge(sem["pts_r0"], T.now2)
                pe.wait_ge(sem["pts_l1"], T.now2)
                pe.wait_ge(sem["pts_r2"], T.now2)
                pe.wait_ge(sem["msg_pre"], T.now2)
                K = CODE_ROWS[2] + CODES
                by_graph(bank[4], lambda g: pts_l[0:K, g, :], lambda g: pts_r[0:K, g, :]
                         ).then_inc(sem["dist_ps"], 1)

            def conv2(T, first, end):
                if first == 0:
                    pe.wait_ge(sem["hc_lo"], T.now2)
                    pe.wait_ge(sem["hc_hi"], T.now2)
                    pe.wait_ge(sem["ghn"], T.now2)
                for i in range(first, end):
                    k = TAP_ORDER[i]
                    shift = k - PAD
                    start, stop = max(0, -shift) // 2 * 2, N - max(0, shift) // 2 * 2
                    to, moved = slice(start, stop), slice(start + shift + 1, stop + shift + 1)
                    last = split_product(bank[2][:, :, to], *weight(CONV2 + k), hc_hi[:, :, moved],
                                         hc_lo[:, :, moved], i == 0, i == TAPS - 1)
                if end == TAPS:
                    last.then_inc(sem["c2_ps"], 1)

            def gather(T):
                pe.wait_ge(sem["msg"], T.now2)
                pe.wait_ge(sem["edge_adj"], T.now2)
                pe.wait_ge(sem["pts_l0"], T.now2)
                pe.wait_ge(sem["pts_r2"], T.now2)
                by_graph(bank[5], lambda g: msg[:, g, :], lambda g: edge_adj[:, g, :]
                         ).then_inc(sem["nmp_ps"], 1)

            def gate_x(T, gate):
                if gate == R_GATE:
                    pe.wait_ge(sem["hc_hi"], T.now2)
                    pe.wait_ge(sem["hc"], T.now2)
                if gate == Z_GATE:
                    pe.wait_ge(sem["edge"], T.now2)
                split_product(cols(bank[3 + gate]), *weight(HH + gate), cols(x1_hi), cols(x1_lo),
                              True, False)

            def gate_nmp(T, gate):
                pe.wait_ge(sem["xn_hi"], T.now2)
                pe.wait_ge(sem["xn_lo"], T.now2)
                split_product(cols(bank[3 + gate]), *weight(IH + 2 * gate + 1), cols(xn_hi),
                              cols(xn_lo), gate == N_GATE, False)

            def gate_conv(T, gate):
                pe.wait_ge(sem["xc_hi"], T.now2)
                pe.wait_ge(sem["xc_lo"], T.now2)
                split_product(cols(bank[3 + gate]), *weight(IH + 2 * gate), cols(xc_hi), cols(xc_lo),
                              False, True
                              ).then_inc(sem[("r_gate_ps", "z_gate_ps", "n_gate_ps")[gate]], 1)

            def y1_t(T):
                pe.wait_ge(sem["y1"], T.now3)
                after(pe, sem["z1"], T.was3)
                transposes(bank[6], y1).then_inc(sem["y1_ps"], 1)

            def prop_in(T):
                pe.wait_ge(sem["y1"], T.now3)
                after(pe, sem["y3"], T.was3)
                by_graph(bank[7], lambda g: y1[:, g, :], lambda g: wt_full[:, 1, :]
                         ).then_inc(sem["ht_ps"], 1)

            def hop(T, k):
                pe.wait_ge(sem[("w3h", "t2", "t1")[k - 1]], T.now3)
                if k == 1:
                    pe.wait_ge(sem["at_now"], T.now3)
                moving = (wh[3], t2, t1)[k - 1]
                by_graph(bank[7], lambda g: at_now[:, g, :], lambda g: moving[:, g, :]
                         ).then_inc((sem["hop1_ps"], sem["hop2_ps"], sem["hop3_ps"])[k - 1], 1)

            def gather3(T):
                pe.wait_ge(sem["x3_rows"], T.now3)
                pe.wait_ge(sem["at3"], T.now3)
                pe.wait_ge(sem["x2_rows"], T.now3)
                by_graph(bank[6], lambda g: x3_rows[:, g, :], lambda g: at3[:, g, :]
                         ).then_inc(sem["agg3_ps"], 1)

            def hidden3(T, c):
                if c == 0:
                    pe.wait_ge(sem["agg3_hi"], T.now4)
                    pe.wait_ge(sem["agg3_lo"], T.now4)
                    pe.wait_ge(sem["prop"], T.now4)
                split_product(cols(bank[7 - c]), w31_hi[:, c * P:(c + 1) * P],
                              w31_lo[:, c * P:(c + 1) * P],
                              cols(agg3_hi), cols(agg3_lo), True, True
                              ).then_inc((sem["z_ps0"], sem["z_ps1"])[c], 1)

            def down3(T):
                pe.wait_ge(sem["z0"], T.now4)
                for c in range(H3):
                    if c == 1:
                        pe.wait_ge(sem["z1"], T.now4)
                    for g in range(G):
                        last = pe.matmul(bank[7][:, g, :], z3[c][:, g, :], w32[:, c, :],
                                         start=(c == 0 and g == 0), stop=(c == H3 - 1),
                                         skip_group_check=True)
                last.then_inc(sem["y3_ps"], 1)

            def turn(T):
                one, two, three, four = (k in T.stages for k in (1, 2, 3, 4))
                T.loads = loads_of(T, pe)
                if four: hidden3(T, 0); hidden3(T, 1)
                if one: adj_t(T)
                if two: x1_t(T)
                if four: down3(T)
                if three: y1_t(T)
                if one: neighbours(T)
                if two: conv1(T); hidden_n(T); messages(T)
                if one: hidden(T, 0)
                if two: codes(T)
                if one: hidden(T, 1)
                if three: prop_in(T)
                if one: hidden(T, 2)
                if two: conv2(T, 0, 1)
                if one: hidden(T, 3)
                if two: conv2(T, 1, 5)
                if three: hop(T, 1)
                if two: conv2(T, 5, 6)
                if one: square_sums(T)
                if two: conv2(T, 6, 7)
                if three: hop(T, 2)
                if two: conv2(T, 7, 8)
                if one: spread_rms(T)
                if two: conv2(T, 8, 10)
                if three: hop(T, 3)
                if two: conv2(T, 10, 11); distances(T); conv2(T, 11, TAPS); gather(T); gate_x(T, R_GATE)
                if one: down(T, 0); down(T, 1); down(T, 2); down(T, 3)
                if two: gate_nmp(T, R_GATE); gate_conv(T, R_GATE)
                if three: gather3(T)
                if two: gate_nmp(T, N_GATE); gate_conv(T, N_GATE); gate_x(T, Z_GATE)
                if two: gate_nmp(T, Z_GATE); gate_conv(T, Z_GATE)

            def transposed_weights(first, end):
                for b in range(first, end):
                    if b == 0:
                        pe.wait_ge(set_act, VECTORS_ACT)
                        pe.wait_ge(weights_in, ALL_WEIGHTS)
                        pe.wait_ge(codes_in, ALL_CODES)
                        pe.wait_ge(set_dve, CONV_SCALED)
                    if b >= 6:
                        pe.wait_ge(set_act, HIGHS + b - 6 + 1)
                        pe.wait_ge(set_dve, LOWS + b - 6 + 1)
                    for k in range(b * G, min(NT, (b + 1) * G)):
                        last = pe.transpose(setup_bank(b)[:, k % G, :], sources[k], ident[:])
                    last.then_inc(set_pe, 1)

            sources = [conv2_w[:, :, k] for k in range(TAPS)] + [conv1_w[:], codes_w[:]]
            sources += [ih_w[:, a, b, :] for a in range(3) for b in range(2)]
            sources += [hh_w[:, a, :] for a in range(3)] + [msg_w[:], prop_w[:]]
            T = Turn(-2, 0, (1,))
            T.loads = loads_of(T, pe)
            pe.wait_ge(set_pool, IDENT_SET)
            adj_t(T)
            neighbours(T)
            pe.wait_ge(vectors_in, 16 * len(vectors))
            pe.transpose(bank[7][:, G - 1, 0:VR], vector_rows[:], ident[0:VR, 0:VR]).then_inc(set_pe, 1)
            pe.wait_ge(set_act, W1_HIGH)
            pe.wait_ge(set_dve, W1_LOW)
            hidden(T, 0); hidden(T, 1); hidden(T, 2); hidden(T, 3)
            pe.wait_ge(set_pool, TILES_SET)
            square_sums(T); spread_rms(T)
            transposed_weights(0, 6)
            pe.wait_ge(set_dve, LAYER0_DVE)
            down(T, 0); down(T, 1); down(T, 2); down(T, 3)
            transposed_weights(6, WT_BANKS)
            pe.wait_ge(set_act, SPLIT_ACT)
            pe.wait_ge(set_dve, SPLIT_DVE)
            run_turns(pe, turn, GROUPS)

        @block.scalar
        def _(act):
            def copy(out, in_):
                return nc.scalar.activation(out, in_, ACT.Copy)

            def a_t(T):
                pe_at = at[T.slot1]
                act.wait_ge(sem["adj_t_ps"], T.now1)
                after(act, sem["at_now"], T.old1)
                after(act, sem["edge_adj"], T.old1)
                act.wait_ge(sem["at_eps"], T.now1)
                copy(pe_at[:], bank[0][:]).then_inc(sem["at"], 1)

            def agg(T):
                act.wait_ge(sem["nb_ps"], T.now1)
                after(act, sem["h_ps3"], T.was1)
                copy(agg_hi[:], bank[1][:]).then_inc(sem["agg_hi"], 1)

            def hidden(T, c):
                act.wait_ge((sem["h_ps0"], sem["h_ps1"], sem["h_ps2"], sem["h_ps3"])[c], T.now1)
                after(act, (sem["sq01"], sem["sq_sum"], sem["sq23"], sem["sq_sum"])[c], T.was1)
                after(act, sem["sq_ps"], T.was1)
                nc.scalar.activation(sq[c][:], bank[1 - c % 2][:], ACT.Square, bias=b1_col[:, c:c + 1]
                                     ).then_inc((sem["sq0"], sem["sq1"], sem["sq2"], sem["sq3"])[c], 1)
                after(act, sem["y0_ps"], T.was1)
                nc.scalar.activation(h[c][:], bank[1 - c % 2][:], ACT.Identity, bias=b1_col[:, c:c + 1]
                                     ).then_inc((sem["h0"], sem["h1"], sem["h2"], sem["h3"])[c], 1)

            def tanh0(T, c):
                act.wait_ge((sem["hn0"], sem["hn1"], sem["hn2"], sem["hn3"])[c], T.now1)
                after(act, (sem["s0"], sem["s1"], sem["s2"], sem["s3"])[c], T.was1)
                nc.scalar.activation(th[c][:], hn[c][:], ACT.Tanh, scale=half_rms[:, c:c + 1]
                                     ).then_inc((sem["th0"], sem["th1"], sem["th2"], sem["th3"])[c], 1)

            def x1_parts(T):
                act.wait_ge(sem["x1_ps"], T.now2)
                after(act, sem["z_gate_ps"], T.was2)
                copy(x1_hi[:], bank[3][:]).then_inc(sem["x1_hi"], 1)
                after(act, sem["x_plus_n"], T.was2)
                after(act, sem["x_minus_n"], T.was2)
                copy(x1[:], bank[3][:]).then_inc(sem["x1"], 1)

            def points(T):
                act.wait_ge(sem["pts_ps"], T.now2)
                after(act, sem["dist_ps"], T.was2)
                r0, r1, r2 = (slice(a, a + CODES) for a in CODE_ROWS)
                nc.scalar.activation(pts_r[r0], bank[5][r0], ACT.Identity, bias=codes_b[r0]
                                     ).then_inc(sem["pts_r0"], 1)
                nc.scalar.activation(pts_l[r1], bank[5][r1], ACT.Square, bias=codes_b[r1]
                                     ).then_inc(sem["pts_l1"], 1)
                nc.scalar.activation(pts_r[r2], bank[5][r2], ACT.Square, bias=codes_b[r2]
                                     ).then_inc(sem["pts_r2"], 1)

            def conv1_hi(T):
                act.wait_ge(sem["c1_ps"], T.now2)
                after(act, sem["c2_ps"], T.was2)
                nc.scalar.activation(hc_hi[:, :, 1:1 + N], bank[3][:], ACT.Relu, bias=bn_shift[:, 0:1]
                                     ).then_inc(sem["hc_hi"], 1)

            def message(T):
                act.wait_ge(sem["msg_pre"], T.now2)
                after(act, sem["nmp_ps"], T.was2)
                nc.scalar.activation(msg[:], msg_pre[:], ACT.Relu).then_inc(sem["msg"], 1)

            def hidden_n(T):
                act.wait_ge(sem["ghn_ps"], T.now2)
                after(act, sem["u"], T.was2)
                nc.scalar.activation(ghn[:], bank[2][:], ACT.Identity, bias=half_bhn[:], scale=0.5
                                     ).then_inc(sem["ghn"], 1)

            def edges(T):
                act.wait_ge(sem["dist_ps"], T.now2)
                after(act, sem["edge_adj"], T.was2)
                nc.scalar.activation(edge[:], bank[4][:], ACT.Exp, scale=-1.0).then_inc(sem["edge"], 1)

            def nmp_hi(T):
                act.wait_ge(sem["nmp_ps"], T.now2)
                after(act, sem["z_gate_ps"], T.was2)
                copy(xn_hi[:], bank[5][:]).then_inc(sem["xn_hi"], 1)

            def conv_hi(T):
                act.wait_ge(sem["c2_res"], T.now2)
                after(act, sem["z_gate_ps"], T.was2)
                nc.scalar.activation(xc_hi[:], c2_res[:], ACT.Relu, bias=bn_shift[:, 1:2]
                                     ).then_inc(sem["xc_hi"], 1)

            def gate_r(T):
                act.wait_ge(sem["r_gate_ps"], T.now2)
                after(act, sem["u"], T.was2)
                nc.scalar.activation(tr[:], bank[3][:], ACT.Tanh, bias=half_gate_b[:, 0:1], scale=0.5
                                     ).then_inc(sem["tr"], 1)

            def gate_z(T):
                act.wait_ge(sem["z_gate_ps"], T.now2)
                after(act, sem["zq"], T.was2)
                nc.scalar.activation(tz[:], bank[4][:], ACT.Tanh, bias=half_gate_b[:, 1:2], scale=0.5
                                     ).then_inc(sem["tz"], 1)

            def gate_n(T):
                act.wait_ge(sem["v"], T.now2)
                after(act, sem["x_minus_n"], T.was2)
                after(act, sem["x_plus_n"], T.was2)
                nc.scalar.activation(nn[:], v[:], ACT.Tanh, bias=gate_bi[:, 2:3]).then_inc(sem["nn"], 1)

            def a_now(T):
                act.wait_ge(sem["at"], T.now3)
                after(act, sem["hop3_ps"], T.was3)
                after(act, sem["at3"], T.was3)
                copy(at_now, at[T.slot3][:]).then_inc(sem["at_now"], 1)

            def multiple(T, k):
                act.wait_ge(sem["ht"], T.now3)
                after(act, sem[("prop", "t1", "t2", "hop1_ps")[k]], T.was3)
                if k > 0:
                    nc.scalar.activation(wh[k][:], ht[:], ACT.Copy, scale=prop_k[:, k:k + 1]
                                         ).then_inc(sem[("w0h", "w1h", "w2h", "w3h")[k]], 1)
                else:
                    nc.scalar.activation(wh[0][:], ht[:], ACT.Identity, bias=prop_b[:],
                                         scale=prop_k[:, 0:1]).then_inc(sem["w0h"], 1)

            def agg3(T):
                act.wait_ge(sem["agg3_ps"], T.now3)
                after(act, sem["z_ps1"], T.was3)
                copy(agg3_hi[:], bank[6][:]).then_inc(sem["agg3_hi"], 1)

            def hidden3(T, c):
                act.wait_ge((sem["z_ps0"], sem["z_ps1"])[c], T.now4)
                after(act, sem["y3_ps"], T.was4)
                nc.scalar.activation(z3[c][:], bank[7 - c][:], ACT.Relu, bias=b31_col[:, c:c + 1]
                                     ).then_inc((sem["z0"], sem["z1"])[c], 1)

            def turn(T):
                one, two, three, four = (k in T.stages for k in (1, 2, 3, 4))
                if four: hidden3(T, 0); hidden3(T, 1)
                if two: x1_parts(T)
                if three: a_now(T)
                if one: agg(T)
                if two: conv1_hi(T); hidden_n(T)
                if one: a_t(T); hidden(T, 0); hidden(T, 1); hidden(T, 2); hidden(T, 3)
                if three: multiple(T, 3); multiple(T, 2)
                if two: points(T)
                if three: multiple(T, 1); multiple(T, 0)
                if one: tanh0(T, 3); tanh0(T, 2); tanh0(T, 1); tanh0(T, 0)
                if two: edges(T); message(T); nmp_hi(T); conv_hi(T); gate_r(T)
                if three: agg3(T)
                if two: gate_n(T); gate_z(T)

            def high_parts(b):
                n = min(G, NT - b * G)
                act.wait_ge(set_pe, 1 + b + 1)
                copy(wt_hi[:, b * G:b * G + n, :], setup_bank(b)[:, 0:n, :]).then_inc(set_act, 1)

            T = Turn(-2, 0, (1,))
            act.wait_ge(w1_in, 16)
            copy(w1_hi[:], w1f[:]).then_inc(set_act, 1)
            a_t(T); agg(T)
            act.wait_ge(set_pe, 1)
            copy(vector_cols[:], bank[7][:, G - 1, 0:VR]).then_inc(set_act, 1)
            act.wait_ge(set_act, VECTORS_ACT)
            hidden(T, 0); hidden(T, 1); hidden(T, 2); hidden(T, 3)
            act.wait_ge(weights_in, ALL_WEIGHTS)
            copy(w31_hi[:], w31f[:]).then_inc(set_act, 1)
            act.wait_ge(set_dve, HALF_RMS)
            for c in range(H0):
                high_parts(c)
                tanh0(T, c)
            for b in range(H0, WT_BANKS):
                high_parts(b)
            k = MSG % G
            copy(wt_full[:], setup_bank(MSG // G)[:, k:k + 2, :]).then_inc(set_act, 1)
            act.wait_ge(set_dve, LOWS)
            act.wait_ge(codes_in, ALL_CODES)
            run_turns(act, turn, GROUPS)

        @block.vector
        def _(dve):
            V = nc.vector

            def norm_stats(k, y, y_ready, bn_done, mv_done, ve_done, count, was):
                dve.wait_ge(y_ready, count)
                for g in range(G):
                    last = V.bn_stats(stats[k][:, g, :], y[:, g, :])
                last.then_inc(bn_done, 1)
                dve.wait_ge(set_dve, LAYER0_DVE)
                dve.wait_ge(bn_done, count)
                after(dve, (sem["x1_rows"], sem["x2_rows"], sem["x3_rows"], sem["out_rows"])[k], was)
                for g in range(G):
                    last = V.bn_aggr(mv[k][:, g, :], stats[k][:, g, :])
                last.then_inc(mv_done, 1)
                dve.wait_ge(mv_done, count)
                V.tensor_scalar(ve[k][:], mv[k][:, :, 1], LN_EPS, None, ALU.add).then_inc(ve_done, 1)

            def apply(k, y, to, r_done, done, count):
                dve.wait_ge(r_done, count)
                for g in range(G):
                    last = V.tensor_scalar(to[:, g, :], y[:, g, :], mv[k][:, g, 0:1],
                                           rstd[k][:, g:g + 1], ALU.subtract, ALU.mult)
                last.then_inc(done, 1)

            def a_t_eps(T):
                dve.wait_ge(sem["adj_t_ps"], T.now1)
                after(dve, sem["nb_ps"], T.was1)
                V.scalar_tensor_tensor(out=at_eps[:], in0=over_graphs(ident), scalar=eps0[:],
                                       in1=bank[0][:], op0=ALU.mult, op1=ALU.add
                                                ).then_inc(sem["at_eps"], 1)

            def row_sums(T):
                dve.wait_ge(adj_in[T.slot1], T.loads)
                after(dve, sem["prop"], T.old1)
                V.tensor_reduce(row_sum[:], adj_rows[T.slot1][:], AX_X, ALU.add
                         ).then_inc(sem["row_sum"], 1)
                dve.wait_ge(sem["row_sum"], T.now1)
                V.tensor_scalar(row_sum_eps[:], row_sum[:], ROW_SUM_EPS, None, ALU.add
                                ).then_inc(sem["row_inv"], 1)
                dve.wait_ge(sem["row_inv"], T.twice1)
                V.reciprocal(row_inv[T.slot1][:], row_sum_eps[:]).then_inc(sem["row_inv"], 1)

            def agg(T):
                dve.wait_ge(sem["agg_hi"], T.now1)
                after(dve, sem["h_ps3"], T.was1)
                V.tensor_tensor(agg_lo[:], bank[1][:], agg_hi[:].bitcast(F32), ALU.subtract
                                ).then_inc(sem["agg_lo"], 1)

            def sum_squares(T):
                dve.wait_ge(sem["sq01"], T.now1)
                dve.wait_ge(sem["sq23"], T.now1)
                V.tensor_tensor(sq_sum[:], sq01[:], sq23[:], ALU.add).then_inc(sem["sq_sum"], 1)

            def mean_square(T):
                dve.wait_ge(sem["sq_ps"], T.now1)
                V.tensor_scalar(ms[:], bank[1][:, :, 0], 1.0 / (H0 * P), RMS_EPS, ALU.mult, ALU.add
                                ).then_inc(sem["ms"], 1)

            def normalise(T, c):
                dve.wait_ge(sem["r_ps"], T.now1)
                V.tensor_tensor(hn[c][:], bank[0][:], h[c][:], ALU.mult
                                ).then_inc((sem["hn0"], sem["hn1"], sem["hn2"], sem["hn3"])[c], 1)

            def silu(T, c):
                dve.wait_ge((sem["th0"], sem["th1"], sem["th2"], sem["th3"])[c], T.now1)
                V.scalar_tensor_tensor(out=s[c][:], in0=th[c][:], scalar=1.0, in1=hn[c][:],
                                       op0=ALU.add, op1=ALU.mult
                                       ).then_inc((sem["s0"], sem["s1"], sem["s2"], sem["s3"])[c], 1)

            def residual0(T):
                dve.wait_ge(sem["y0_ps"], T.now1)
                dve.wait_ge(sem["xb"], T.now1)
                after(dve, sem["x1_rows"], T.was1)
                V.tensor_tensor(y0[:], bank[1][:], xb[:], ALU.add).then_inc(sem["y0"], 1)
                norm_stats(0, y0, sem["y0"], sem["bn0"], sem["mv0"], sem["ve0"], T.now1, T.was1)

            def apply0(T):
                after(dve, sem["x1_ps"], T.was1)
                apply(0, y0, x1_rows, sem["r0"], sem["x1_rows"], T.now1)

            def x1_low(T):
                dve.wait_ge(sem["x1"], T.now2)
                after(dve, sem["z_gate_ps"], T.was2)
                V.tensor_tensor(x1_lo[:], bank[3][:], x1_hi[:].bitcast(F32), ALU.subtract
                                ).then_inc(sem["x1_lo"], 1)

            def message_bias(T):
                dve.wait_ge(sem["msg_ps"], T.now2)
                after(dve, sem["msg"], T.was2)
                V.tensor_tensor(msg_pre[:], bank[4][:], over_graphs(msg_row), ALU.add
                                ).then_inc(sem["msg_pre"], 1)

            def points(T):
                dve.wait_ge(sem["pts_r0"], T.now2)
                after(dve, sem["dist_ps"], T.was2)
                V.tensor_scalar(pts_l[0:CODES], bank[5][0:CODES], codes_b[0:CODES], -2.0, ALU.add,
                                ALU.mult).then_inc(sem["pts_l0"], 1)

            def conv1_full(T):
                dve.wait_ge(sem["hc_hi"], T.now2)
                after(dve, sem["hc_lo"], T.was2)
                V.tensor_scalar(hc[:], bank[3][:], bn_shift[:, 0:1], 0.0, ALU.add, ALU.max
                                ).then_inc(sem["hc"], 1)

            def nmp_low(T):
                dve.wait_ge(sem["xn_hi"], T.now2)
                after(dve, sem["z_gate_ps"], T.was2)
                V.tensor_tensor(xn_lo[:], bank[5][:], xn_hi[:].bitcast(F32), ALU.subtract
                                ).then_inc(sem["xn_lo"], 1)

            def conv_residual(T):
                dve.wait_ge(sem["c2_ps"], T.now2)
                dve.wait_ge(sem["x1"], T.now2)
                after(dve, sem["xc_hi"], T.was2)
                V.tensor_tensor(c2_res[:], bank[2][:], x1[:], ALU.add).then_inc(sem["c2_res"], 1)

            def conv_full(T):
                dve.wait_ge(sem["c2_res"], T.now2)
                after(dve, sem["xc_lo"], T.was2)
                V.tensor_scalar(xc[:], c2_res[:], bn_shift[:, 1:2], 0.0, ALU.add, ALU.max
                                ).then_inc(sem["xc"], 1)

            def conv_low(T):
                dve.wait_ge(sem["xc"], T.now2)
                dve.wait_ge(sem["xc_hi"], T.now2)
                after(dve, sem["z_gate_ps"], T.was2)
                V.tensor_tensor(xc_lo[:], xc[:], xc_hi[:].bitcast(F32), ALU.subtract
                                ).then_inc(sem["xc_lo"], 1)

            def gate_u(T):
                dve.wait_ge(sem["tr"], T.now2)
                dve.wait_ge(sem["ghn"], T.now2)
                after(dve, sem["nn"], T.was2)
                V.scalar_tensor_tensor(out=u[:], in0=tr[:], scalar=1.0, in1=ghn[:], op0=ALU.add,
                                       op1=ALU.mult).then_inc(sem["u"], 1)

            def gate_v(T):
                dve.wait_ge(sem["u"], T.now2)
                dve.wait_ge(sem["n_gate_ps"], T.now2)
                V.tensor_tensor(v[:], bank[5][:], u[:], ALU.add).then_inc(sem["v"], 1)

            def add_n(T):
                dve.wait_ge(sem["nn"], T.now2)
                V.tensor_tensor(x_plus_n[:], x1[:], nn[:], ALU.add).then_inc(sem["x_plus_n"], 1)

            def residual1(T):
                dve.wait_ge(sem["x_plus_n"], T.now2)
                dve.wait_ge(sem["x_minus_n"], T.now2)
                dve.wait_ge(sem["tz"], T.now2)
                after(dve, sem["y1_ps"], T.was2)
                after(dve, sem["ht_ps"], T.was2)
                V.scalar_tensor_tensor(out=zq[:], in0=tz[:], scalar=1.0, in1=x_minus_n[:],
                                       op0=ALU.add, op1=ALU.mult).then_inc(sem["zq"], 1)
                dve.wait_ge(sem["zq"], T.now2)
                V.scalar_tensor_tensor(out=y1[:], in0=zq[:], scalar=0.5, in1=x_plus_n[:],
                                       op0=ALU.mult, op1=ALU.add).then_inc(sem["y1"], 1)

            def norm1(T):
                norm_stats(1, bank[6], sem["y1_ps"], sem["bn1"], sem["mv1"], sem["ve1"], T.now3, T.was3)

            def apply1(T):
                after(dve, sem["y2"], T.was3)
                apply(1, bank[6], x2_rows, sem["r1"], sem["x2_rows"], T.now3)

            def scaled_h(T):
                dve.wait_ge(sem["ht_ps"], T.now3)
                dve.wait_ge(sem["r1"], T.now3)
                for k in range(4):
                    after(dve, sem[("w0h", "w1h", "w2h", "w3h")[k]], T.was3)
                V.tensor_tensor(ht[:], bank[7][:], rstd[1][:].unsqueeze(2).to_broadcast([P, G, P]),
                                ALU.mult).then_inc(sem["ht"], 1)

            def hop(T, k):
                hop_ps = (sem["hop1_ps"], sem["hop2_ps"], sem["hop3_ps"])[k - 1]
                to = (t2, t1, prop)[k - 1]
                dve.wait_ge(hop_ps, T.now3)
                dve.wait_ge((sem["w2h"], sem["w1h"], sem["w0h"])[k - 1], T.now3)
                after(dve, (sem["hop2_ps"], sem["hop3_ps"], sem["y2"])[k - 1], T.was3)
                dve.wait_ge(sem["row_inv"], T.twice3)
                for g in range(G):
                    last = V.scalar_tensor_tensor(
                        out=to[:, g, :], in0=bank[7][:, g, :],
                        scalar=row_inv[T.slot3][:, g:g + 1], in1=wh[3 - k][:, g, :], op0=ALU.mult,
                        op1=ALU.add)
                last.then_inc((sem["t2"], sem["t1"], sem["prop"])[k - 1], 1)

            def leaky_relu(T):
                dve.wait_ge(sem["prop"], T.now3)
                V.scalar_tensor_tensor(out=leaky[:], in0=prop[:], scalar=LEAKY_SLOPE, in1=prop[:],
                                       op0=ALU.mult, op1=ALU.max).then_inc(sem["leaky"], 1)

            def norm2(T):
                norm_stats(2, y2, sem["y2"], sem["bn2"], sem["mv2"], sem["ve2"], T.now3, T.was3)

            def apply2(T):
                after(dve, sem["agg3_ps"], T.was3)
                after(dve, sem["x3b"], T.was3)
                apply(2, y2, x3_rows, sem["r2"], sem["x3_rows"], T.now3)

            def a_t3(T):
                dve.wait_ge(sem["at_now"], T.now3)
                after(dve, sem["agg3_ps"], T.was3)
                V.scalar_tensor_tensor(out=at3, in0=over_graphs(ident), scalar=one_eps3[:],
                                       in1=at_now, op0=ALU.mult, op1=ALU.add).then_inc(sem["at3"], 1)

            def agg3(T):
                dve.wait_ge(sem["agg3_hi"], T.now3)
                after(dve, sem["z_ps1"], T.was3)
                V.tensor_tensor(agg3_lo[:], bank[6][:], agg3_hi[:].bitcast(F32), ALU.subtract
                                ).then_inc(sem["agg3_lo"], 1)

            def residual3(T):
                dve.wait_ge(sem["y3_ps"], T.now4)
                dve.wait_ge(sem["x3b"], T.now4)
                after(dve, sem["out_rows"], T.was4)
                V.tensor_tensor(y3, bank[7][:], x3b, ALU.add).then_inc(sem["y3"], 1)
                norm_stats(3, y3, sem["y3"], sem["bn3"], sem["mv3"], sem["ve3"], T.now4, T.was4)

            def apply3(T):
                after(dve, stored[T.slot4], T.stores)
                apply(3, y3, out_rows[T.slot4], sem["r3"], sem["out_rows"], T.now4)

            def turn(T):
                one, two, three, four = (k in T.stages for k in (1, 2, 3, 4))
                T.loads = loads_of(T, dve)
                if isinstance(T.t, int):
                    T.twice1, T.twice3 = 2 * (T.t + 2) + 1, 2 * T.t + 2
                    T.stores = 16 * ((T.t - 1) // 2)
                else:
                    T.twice1, T.twice3 = dve.snap(2 * T.t + 5), dve.snap(2 * T.t + 2)
                    T.stores = dve.snap(8 * (T.t - 1 - T.slot4))
                if one: a_t_eps(T)
                if two: x1_low(T)
                if three: norm1(T)
                if one: agg(T)
                if two: conv1_full(T)
                if four: residual3(T)
                if three: apply1(T)
                if two: message_bias(T)
                if three: scaled_h(T); a_t3(T)
                if four: apply3(T)
                if one: sum_squares(T)
                if three: hop(T, 1)
                if one: mean_square(T)
                if two: points(T)
                if three: hop(T, 2)
                if one: normalise(T, 3); normalise(T, 2); normalise(T, 1); normalise(T, 0)
                if three: hop(T, 3)
                if one: silu(T, 2)
                if three: leaky_relu(T)
                if one: silu(T, 1); silu(T, 3); silu(T, 0)
                if two: conv_residual(T)
                if three: norm2(T)
                if two: conv_full(T); nmp_low(T); conv_low(T)
                if three: apply2(T)
                if one: residual0(T)
                if two: gate_u(T)
                if three: agg3(T)
                if two: gate_v(T)
                if one: apply0(T)
                if two: add_n(T)
                if one: row_sums(T)
                if two: residual1(T)

            done = 0

            def step(instruction):
                nonlocal done
                instruction.then_inc(set_dve, 1)
                done += 1

            def low_parts(first, end):
                for b in range(first, end):
                    n = min(G, NT - b * G)
                    dve.wait_ge(set_act, SPLIT_ACT if b == WT_BANKS - 1 else HIGHS + b + 1)
                    step(V.tensor_tensor(wt_lo[:, b * G:b * G + n, :], setup_bank(b)[:, 0:n, :],
                                         wt_hi[:, b * G:b * G + n, :].bitcast(F32), ALU.subtract))

            T = Turn(-2, 0, (1,))
            T.loads, T.twice1 = loads_of(T, dve), 1
            dve.wait_ge(eps0_in, 16)
            a_t_eps(T)
            dve.wait_ge(w1_in, 16)
            dve.wait_ge(set_act, W1_HIGH)
            step(V.tensor_tensor(w1_lo[:], w1f[:], w1_hi[:].bitcast(F32), ALU.subtract))
            assert done == W1_LOW
            agg(T)
            dve.wait_ge(set_act, VECTORS_ACT)
            step(V.tensor_scalar(bn_ve[:], bn_v, BN_EPS, None, ALU.add))
            assert done == BN_VE
            step(V.tensor_scalar(half_rms[:], rms_col, 0.5, None, ALU.mult))
            assert done == HALF_RMS
            dve.wait_ge(layer0_in, ALL_LAYER0)
            dve.wait_ge(set_dve, done)
            for c in range(H0):
                step(V.tensor_scalar(w2[:, c, :], w2[:, c, :], half_rms[:, c:c + 1], None, ALU.mult))
            assert done == LAYER0_DVE
            row_sums(T)
            dve.wait_ge(set_pool, BN_POW)
            step(V.tensor_tensor(bn_scale[:], bn_g, bn_r[:], ALU.mult))
            dve.wait_ge(set_dve, done)
            step(V.tensor_tensor(bn_ms[:], bn_m, bn_scale[:], ALU.mult))
            dve.wait_ge(set_dve, done)
            step(V.tensor_tensor(bn_shift[:], bn_b, bn_ms[:], ALU.subtract))
            sum_squares(T)
            dve.wait_ge(weights_in, ALL_WEIGHTS)
            step(V.tensor_reduce(prop_sum[:], prop_w[:], AX_X, ALU.add))
            dve.wait_ge(set_dve, done)
            step(V.tensor_scalar(prop_mean[:], prop_sum[:], 1.0 / D, None, ALU.mult))
            dve.wait_ge(set_dve, done)
            step(V.tensor_scalar(prop_w[:], prop_w[:], prop_mean[:, 0:1], None, ALU.subtract))
            step(V.tensor_scalar(conv1_w[:], conv1_w[:], bn_scale[:, 0:1], None, ALU.mult))
            step(V.tensor_scalar(conv2_w, conv2_w, bn_scale[:, 1:2], None, ALU.mult))
            assert done == CONV_SCALED
            mean_square(T)
            step(V.tensor_tensor(gate_b[:], gate_bi[:, 0:2], gate_bh[:, 0:2], ALU.add))
            dve.wait_ge(set_dve, done)
            step(V.tensor_scalar(half_gate_b[:], gate_b[:], 0.5, None, ALU.mult))
            step(V.tensor_scalar(half_bhn[:], gate_bh[:, 2:3], 0.5, None, ALU.mult))
            step(V.tensor_scalar(one_eps3[:], eps3[:], 1.0, None, ALU.add))
            step(V.memset(pts_l[CODE_ROWS[2]:CODE_ROWS[2] + CODES], 1.0))
            step(V.memset(pts_r[CODE_ROWS[1]:CODE_ROWS[1] + CODES], 1.0))
            normalise(T, 0); normalise(T, 1); normalise(T, 2); normalise(T, 3)
            dve.wait_ge(set_act, HIGHS)
            step(V.tensor_tensor(w31_lo[:], w31f[:], w31_hi[:].bitcast(F32), ALU.subtract))
            assert done == LOWS
            low_parts(0, 1)
            silu(T, 0)
            low_parts(1, 2)
            silu(T, 1); silu(T, 2); silu(T, 3)
            low_parts(2, 3)
            residual0(T)
            low_parts(3, WT_BANKS)
            assert done == SPLIT_DVE
            apply0(T)
            dve.wait_ge(set_dve, done)
            dve.wait_ge(codes_in, ALL_CODES)
            run_turns(dve, turn, GROUPS)

        @block.gpsimd
        def _(pool):
            Q = nc.gpsimd

            def power(k, ready, done, count, was, base, to):
                pool.wait_ge(ready, count)
                Q.tensor_tensor(to[:], base[:], minus_half[:], ALU.pow).then_inc(done, 1)

            def x_bias(T):
                pool.wait_ge(x_in[T.slot1], T.loads)
                after(pool, sem["y0"], T.was1)
                Q.tensor_tensor(xb[:], x_rows[T.slot1][:], over_graphs(b2_row), ALU.add
                         ).then_inc(sem["xb"], 1)

            def add_squares01(T):
                pool.wait_ge(sem["sq0"], T.now1)
                pool.wait_ge(sem["sq1"], T.now1)
                Q.tensor_tensor(sq01[:], sq[0][:], sq[1][:], ALU.add).then_inc(sem["sq01"], 1)

            def add_squares23(T):
                pool.wait_ge(sem["sq2"], T.now1)
                pool.wait_ge(sem["sq3"], T.now1)
                Q.tensor_tensor(sq23[:], sq[2][:], sq[3][:], ALU.add).then_inc(sem["sq23"], 1)

            def rms(T):
                power(0, sem["ms"], sem["r_rms"], T.now1, T.was1, ms, r_rms)

            def norm0(T):
                power(0, sem["ve0"], sem["r0"], T.now1, T.was1, ve[0], rstd[0])

            def edge_weights(T):
                pool.wait_ge(sem["edge"], T.now2)
                pool.wait_ge(sem["at"], T.now2)
                after(pool, sem["nmp_ps"], T.was2)
                Q.tensor_tensor(edge_adj[:], edge[:], at[T.slot2][:], ALU.mult
                         ).then_inc(sem["edge_adj"], 1)

            def conv1_low(T):
                pool.wait_ge(sem["hc"], T.now2)
                pool.wait_ge(sem["hc_hi"], T.now2)
                after(pool, sem["c2_ps"], T.was2)
                Q.tensor_tensor(hc_lo[:, :, 1:1 + N], hc[:], hc_hi[:, :, 1:1 + N].bitcast(F32),
                                ALU.subtract).then_inc(sem["hc_lo"], 1)

            def minus(T):
                pool.wait_ge(sem["nn"], T.now2)
                after(pool, sem["zq"], T.was2)
                Q.tensor_tensor(x_minus_n[:], x1[:], nn[:], ALU.subtract).then_inc(sem["x_minus_n"], 1)

            def norm1(T):
                after(pool, sem["ht"], T.was3)
                power(1, sem["ve1"], sem["r1"], T.now3, T.was3, ve[1], rstd[1])

            def residual2(T):
                pool.wait_ge(sem["leaky"], T.now3)
                after(pool, sem["x3_rows"], T.was3)
                Q.tensor_tensor(y2, leaky[:], x2_rows[:], ALU.add).then_inc(sem["y2"], 1)

            def norm2(T):
                power(2, sem["ve2"], sem["r2"], T.now3, T.was3, ve[2], rstd[2])

            def x3_bias(T):
                pool.wait_ge(sem["x3_rows"], T.now3)
                after(pool, sem["y3"], T.was3)
                Q.tensor_tensor(x3b, x3_rows, over_graphs(b32_row), ALU.add).then_inc(sem["x3b"], 1)

            def norm3(T):
                power(3, sem["ve3"], sem["r3"], T.now4, T.was4, ve[3], rstd[3])

            def turn(T):
                one, two, three, four = (k in T.stages for k in (1, 2, 3, 4))
                T.loads = loads_of(T, pool)
                if three: norm1(T)
                if one: x_bias(T)
                if two: conv1_low(T)
                if four: norm3(T)
                if one: add_squares01(T); add_squares23(T); rms(T)
                if two: edge_weights(T)
                if three: residual2(T); norm2(T)
                if one: norm0(T)
                if two: minus(T)
                if three: x3_bias(T)

            Q.memset(codes_w[:], 0.0).then_inc(cleared, 1)
            Q.memset(ident[:], 0.0).then_inc(set_pool, 1)
            pool.wait_ge(set_pool, 1)
            Q.affine_select(out=ident[:], in_=ident[:], compare_op=ALU.not_equal, fill=1.0, base=0,
                            pattern=[[-1, P]], channel_multiplier=1).then_inc(set_pool, 1)
            Q.memset(ones[:], 1.0)
            Q.memset(minus_half[:], -0.5)
            Q.memset(pts_l[:], 0.0)
            Q.memset(pts_r[:], 0.0)
            for tile in (hc_hi, hc_lo):
                Q.memset(tile[:, :, 0:1].bitcast(F32), 0.0)
                last = Q.memset(tile[:, :, 1 + N:2 + N].bitcast(F32), 0.0)
            last.then_inc(set_pool, 1)
            T = Turn(-2, 0, (1,))
            T.loads = loads_of(T, pool)
            pool.wait_ge(layer0_in, ALL_LAYER0)
            x_bias(T)
            pool.wait_ge(set_dve, BN_VE)
            pool.wait_ge(set_pool, TILES_SET)
            Q.tensor_tensor(bn_r[:], bn_ve[:], minus_half[:, 0:2], ALU.pow).then_inc(set_pool, 1)
            add_squares01(T); add_squares23(T); rms(T); norm0(T)
            pool.wait_ge(weights_in, ALL_WEIGHTS)
            run_turns(pool, turn, GROUPS)


_INS = ['x', 'adj', 'L0_gnn_epsilon', 'L0_gnn_W1', 'L0_gnn_b1', 'L0_gnn_rms_weight', 'L0_gnn_W2',
        'L0_gnn_b2', 'L1_gnn_w_se', 'L1_gnn_b_se', 'L1_gnn_conv1_w', 'L1_gnn_bn1_g', 'L1_gnn_bn1_b',
        'L1_gnn_bn1_m', 'L1_gnn_bn1_v', 'L1_gnn_conv2_w', 'L1_gnn_bn2_g', 'L1_gnn_bn2_b',
        'L1_gnn_bn2_m', 'L1_gnn_bn2_v', 'L1_gnn_w_msg', 'L1_gnn_b_msg', 'L1_gnn_w_ih',
        'L1_gnn_b_ih', 'L1_gnn_w_hh', 'L1_gnn_b_hh', 'L2_gnn_W', 'L2_gnn_conv_w', 'L2_gnn_conv_b',
        'L3_gnn_eps', 'L3_gnn_W1', 'L3_gnn_b1', 'L3_gnn_W2', 'L3_gnn_b2']


def kernel(**inputs):
    import numpy as np
    import concourse.bacc as bacc
    from concourse.bass_utils import run_bass_kernel_spmd

    nc = bacc.Bacc("TRN2", target_bir_lowering=False, num_devices=1)
    arrays, args = {}, {}
    for name in _INS:
        a = np.ascontiguousarray(inputs[name])
        if name == 'L0_gnn_epsilon':
            a = a.reshape(1, 1)
        arrays[f"in_{name}"] = a
        args[name] = nc.dram_tensor(f"in_{name}", a.shape, mybir.dt.from_np(a.dtype),
                                    kind="ExternalInput").ap()
    out = nc.dram_tensor("out", inputs['x'].shape, F32, kind="ExternalOutput").ap()
    graph_layers(nc, args.pop('x'), args.pop('adj'), out, args)
    result = run_bass_kernel_spmd(nc, [arrays], core_ids=[0])
    return result.results[0]["out"]
```
